# Optimizing a Trainium2 kernel written in Bass

```python
import numpy as np
import jax
import jax.numpy as jnp

def _softmax(x, axis=-1):
    return jax.nn.softmax(x, axis=axis)

def _gelu(x):
    return jax.nn.gelu(x, approximate=True)

def _silu(x):
    return jax.nn.silu(x)

def _sigmoid(x):
    return jax.nn.sigmoid(x)

def _layernorm(x, axis=-1, eps=1e-05):
    m = jnp.mean(x, axis=axis, keepdims=True)
    v = jnp.var(x, axis=axis, keepdims=True)
    return (x - m) / jnp.sqrt(v + eps)

def _scatter_add(tgt, idx, src, axis=0):
    return tgt.at[idx].add(src)

def _segment_sum(src, seg, n):
    return jax.ops.segment_sum(src, seg, n)
kernel_name = 'mk_adaln_attn_ffn_d1_seqx_r4_a11f84'

def setup_inputs(seed: int=0):
    np.random.seed(seed)
    _w = jnp.asarray

    def _rec_inputs():
        import jax
        import jax.numpy as jnp
        _rk = jax.random.key(seed)
        x = -0.0002928 + 1 * jax.random.normal(jax.random.fold_in(_rk, 1), (64, 64, 256), jnp.float32)
        _lenS = 64 - jax.random.randint(jax.random.fold_in(_rk, 7), (64,), 0, max(1, 64 // 4) + 1, jnp.int32)
        _lenS2 = 64 - jax.random.randint(jax.random.fold_in(_rk, 8), (64,), 0, max(1, 64 // 4) + 1, jnp.int32)
        fside_16xSxS_0 = -5.72187e-05 + 0.999849 * jax.random.normal(jax.random.fold_in(_rk, 11), (16, 64, 64), jnp.float32)
        cond_64 = -0.0265395 + 0.99382 * jax.random.normal(jax.random.fold_in(_rk, 13), (64, 64), jnp.float32)
        _validS = jnp.arange(64)[None, :] < _lenS[:, None]
        _validS2 = jnp.arange(64)[None, :] < _lenS2[:, None]
        _causal = jnp.tril(jnp.ones((64, 64), dtype=bool))
        mask_BxS_bk0 = jnp.logical_not(jnp.broadcast_to(_validS[:, :], (64, 64)))
        mask_BxS_bf1 = jnp.ones((64, 64), dtype=bool)
        return (x, fside_16xSxS_0, cond_64, mask_BxS_bk0, mask_BxS_bf1)
    x, fside_16xSxS_0, cond_64, mask_BxS_bk0, mask_BxS_bf1 = _rec_inputs()

    def _L0_cond_setup():
        import jax, jax.numpy as jnp
        import numpy as np
        B, N, DIM, H, DH = (2, 512, 256, 16, 64)
        INNER = H * DH
        EPS = 1e-05

        def layernorm(x, g):
            mean = jnp.mean(x, axis=-1, keepdims=True)
            var = jnp.var(x, axis=-1, keepdims=True)
            return (x - mean) * jax.lax.rsqrt(var + EPS) * g
        key = jax.random.key(seed)
        ks = jax.random.split(key, 10)
        x = jax.random.normal(ks[0], (B, N, DIM), dtype=jnp.float32)
        attn_bias = jax.random.normal(ks[1], (H, N, N), dtype=jnp.float32)
        mask = jax.random.randint(ks[2], (B, N), 0, 2).astype(bool)
        g_in = jnp.ones((DIM,), dtype=jnp.float32)
        null_attn_bias = jax.random.normal(ks[3], (H,), dtype=jnp.float32)
        null_kv = jax.random.normal(ks[4], (2, DH), dtype=jnp.float32)
        Wq = jax.random.normal(ks[5], (DIM, INNER), dtype=jnp.float32) * 0.02
        Wkv = jax.random.normal(ks[6], (DIM, 2 * DH), dtype=jnp.float32) * 0.02
        Wo = jax.random.normal(ks[7], (INNER, DIM), dtype=jnp.float32) * 0.02
        g_out = jnp.ones((DIM,), dtype=jnp.float32)
        return {'x': x, 'attn_bias': attn_bias, 'mask': mask, 'g_in': g_in, 'null_attn_bias': null_attn_bias, 'null_kv': null_kv, 'Wq': Wq, 'Wkv': Wkv, 'Wo': Wo, 'g_out': g_out}
    _L0_cond_all = _L0_cond_setup()
    _L0_cond_in = {k: v for k, v in _L0_cond_all.items() if k in ('g_in', 'null_attn_bias', 'Wq', 'Wkv', 'Wo', 'g_out')}
    del _L0_cond_all

    def _L0_attn_setup():
        import jax, jax.numpy as jnp
        import numpy as np
        B, T, H = (2, 512, 256)
        EXPAND, N = (2, 16)
        DIN = H * EXPAND
        EPS = 1e-06

        def rmsnorm(x, w):
            var = jnp.mean(x * x, axis=-1, keepdims=True)
            return x * jax.lax.rsqrt(var + EPS) * w

        def liquid_scan(x_in, a_mod, a_base, B_in, C_in):

            def step(h, inp):
                a_t, b_t, c_t, x_t = inp
                h = a_t[:, :, None] * a_base * h + b_t[:, None, :] * x_t[:, :, None]
                y_t = jnp.einsum('bdn,bn->bd', h, c_t)
                return (h, y_t)
            h0 = jnp.zeros((x_in.shape[0], DIN, N), x_in.dtype)
            xs = (jnp.swapaxes(a_mod, 0, 1), jnp.swapaxes(B_in, 0, 1), jnp.swapaxes(C_in, 0, 1), jnp.swapaxes(x_in, 0, 1))
            _, ys = jax.lax.scan(step, h0, xs)
            return jnp.swapaxes(ys, 0, 1)
        key = jax.random.key(seed)
        ks = jax.random.split(key, 9)
        s_h = 1.0 / np.sqrt(H)
        s_d = 1.0 / np.sqrt(DIN)
        return {'x': jax.random.normal(ks[0], (B, T, H), jnp.float32), 'norm_w': jnp.ones((H,), jnp.float32), 'in_proj_w': jax.random.normal(ks[1], (H, 2 * DIN), jnp.float32) * s_h, 'A_proj_w': jax.random.normal(ks[2], (DIN, DIN), jnp.float32) * s_d, 'A_proj_b': jax.random.normal(ks[3], (DIN,), jnp.float32) * 0.02, 'A_base': jnp.log(jnp.arange(1, N + 1, dtype=jnp.float32)), 'B_proj_w': jax.random.normal(ks[4], (DIN, N), jnp.float32) * s_d, 'C_proj_w': jax.random.normal(ks[5], (DIN, N), jnp.float32) * s_d, 'D': jnp.ones((DIN,), jnp.float32), 'out_proj_w': jax.random.normal(ks[6], (DIN, H), jnp.float32) * s_d}
    _L0_attn_all = _L0_attn_setup()
    _L0_attn_in = {k: v for k, v in _L0_attn_all.items() if k in ('norm_w', 'in_proj_w', 'A_proj_w', 'A_proj_b', 'A_base', 'B_proj_w', 'C_proj_w', 'D', 'out_proj_w')}
    del _L0_attn_all

    def _L0_cond2_setup():
        import jax, jax.numpy as jnp
        import numpy as np
        DIM = 256
        HEADS = 16
        DIM_HEAD = 64
        SCALE = 8.0

        def ln(x, g, eps=1e-05):
            mean = x.mean(axis=-1, keepdims=True)
            var = ((x - mean) ** 2).mean(axis=-1, keepdims=True)
            return (x - mean) * jax.lax.rsqrt(var + eps) * g

        def l2norm(t):
            n = jnp.maximum(jnp.linalg.norm(t, axis=-1, keepdims=True), 1e-12)
            return t / n

        def rel_pos_bias(n, w0, b0, g0, w1, b1, g1, w2, b2, dtype):
            pos = jnp.arange(-n + 1, n, dtype=dtype)[:, None]
            h = jax.nn.silu(ln(pos @ w0 + b0, g0))
            h = jax.nn.silu(ln(h @ w1 + b1, g1))
            h = h @ w2 + b2
            i = jnp.arange(n)
            idx = i[:, None] - i[None, :] + n - 1
            bias = h[idx]
            return jnp.transpose(bias, (2, 0, 1))
        key = jax.random.key(seed)
        ks = jax.random.split(key, 16)
        b, n = (2, 512)
        inner = HEADS * DIM_HEAD
        s = 0.02
        return {'x': jax.random.normal(ks[0], (b, n, DIM), jnp.float32), 'mask': jnp.ones((b, n), dtype=bool), 'g_norm': jnp.ones((DIM,), jnp.float32), 'Wq': jax.random.normal(ks[1], (DIM, inner), jnp.float32) * s, 'Wkv': jax.random.normal(ks[2], (DIM, 2 * DIM_HEAD), jnp.float32) * s, 'q_scale': jnp.ones((DIM_HEAD,), jnp.float32), 'k_scale': jnp.ones((DIM_HEAD,), jnp.float32), 'null_kv': jax.random.normal(ks[3], (2, DIM_HEAD), jnp.float32), 'null_attn_bias': jax.random.normal(ks[4], (HEADS,), jnp.float32), 'w0': jax.random.normal(ks[5], (1, DIM), jnp.float32) * s, 'b0': jnp.zeros((DIM,), jnp.float32), 'g0': jnp.ones((DIM,), jnp.float32), 'w1': jax.random.normal(ks[6], (DIM, DIM), jnp.float32) * s, 'b1': jnp.zeros((DIM,), jnp.float32), 'g1': jnp.ones((DIM,), jnp.float32), 'w2': jax.random.normal(ks[7], (DIM, HEADS), jnp.float32) * s, 'b2': jnp.zeros((HEADS,), jnp.float32), 'Wout': jax.random.normal(ks[8], (inner, DIM), jnp.float32) * s, 'g_out': jnp.ones((DIM,), jnp.float32)}
    _L0_cond2_all = _L0_cond2_setup()
    _L0_cond2_in = {k: v for k, v in _L0_cond2_all.items() if k in ('g_norm', 'Wq', 'Wkv', 'q_scale', 'k_scale', 'null_attn_bias', 'w0', 'b0', 'g0', 'w1', 'b1', 'g1', 'w2', 'b2', 'Wout', 'g_out')}
    del _L0_cond2_all

    def _L0_ffn_setup():
        import jax, jax.numpy as jnp
        import numpy as np
        NUM_EXPERTS = 8
        D_MODEL = 256
        D_OUT = 256
        key = jax.random.key(seed)
        ks = jax.random.split(key, 5)
        B, S = (2, 512)
        x = jax.random.normal(ks[0], (B, S, D_MODEL), dtype=jnp.float32)
        gate_w = jax.random.normal(ks[1], (D_MODEL, NUM_EXPERTS), dtype=jnp.float32) * 0.02
        gate_b = jnp.zeros((NUM_EXPERTS,), dtype=jnp.float32)
        expert_w = jax.random.normal(ks[2], (NUM_EXPERTS, D_MODEL, D_OUT), dtype=jnp.float32) * 0.02
        expert_b = jnp.zeros((NUM_EXPERTS, D_OUT), dtype=jnp.float32)
        return {'x': x, 'gate_w': gate_w, 'gate_b': gate_b, 'expert_w': expert_w, 'expert_b': expert_b}
    _L0_ffn_all = _L0_ffn_setup()
    _L0_ffn_in = {k: v for k, v in _L0_ffn_all.items() if k in ('gate_w', 'gate_b', 'expert_w', 'expert_b')}
    del _L0_ffn_all
    return {'x': x, 'fside_16xSxS_0': fside_16xSxS_0, 'cond_64': cond_64, 'mask_BxS_bk0': mask_BxS_bk0, 'mask_BxS_bf1': mask_BxS_bf1, 'L0_cond_g_in': _L0_cond_in['g_in'], 'L0_cond_null_attn_bias': _L0_cond_in['null_attn_bias'], 'L0_cond_Wq': _L0_cond_in['Wq'], 'L0_cond_Wkv': _L0_cond_in['Wkv'], 'L0_cond_Wo': _L0_cond_in['Wo'], 'L0_cond_g_out': _L0_cond_in['g_out'], 'L0_attn_norm_w': _L0_attn_in['norm_w'], 'L0_attn_in_proj_w': _L0_attn_in['in_proj_w'], 'L0_attn_A_proj_w': _L0_attn_in['A_proj_w'], 'L0_attn_A_proj_b': _L0_attn_in['A_proj_b'], 'L0_attn_A_base': _L0_attn_in['A_base'], 'L0_attn_B_proj_w': _L0_attn_in['B_proj_w'], 'L0_attn_C_proj_w': _L0_attn_in['C_proj_w'], 'L0_attn_D': _L0_attn_in['D'], 'L0_attn_out_proj_w': _L0_attn_in['out_proj_w'], 'L0_cond2_g_norm': _L0_cond2_in['g_norm'], 'L0_cond2_Wq': _L0_cond2_in['Wq'], 'L0_cond2_Wkv': _L0_cond2_in['Wkv'], 'L0_cond2_q_scale': _L0_cond2_in['q_scale'], 'L0_cond2_k_scale': _L0_cond2_in['k_scale'], 'L0_cond2_null_attn_bias': _L0_cond2_in['null_attn_bias'], 'L0_cond2_w0': _L0_cond2_in['w0'], 'L0_cond2_b0': _L0_cond2_in['b0'], 'L0_cond2_g0': _L0_cond2_in['g0'], 'L0_cond2_w1': _L0_cond2_in['w1'], 'L0_cond2_b1': _L0_cond2_in['b1'], 'L0_cond2_g1': _L0_cond2_in['g1'], 'L0_cond2_w2': _L0_cond2_in['w2'], 'L0_cond2_b2': _L0_cond2_in['b2'], 'L0_cond2_Wout': _L0_cond2_in['Wout'], 'L0_cond2_g_out': _L0_cond2_in['g_out'], 'L0_ffn_gate_w': _L0_ffn_in['gate_w'], 'L0_ffn_gate_b': _L0_ffn_in['gate_b'], 'L0_ffn_expert_w': _L0_ffn_in['expert_w'], 'L0_ffn_expert_b': _L0_ffn_in['expert_b']}

def reference(x, fside_16xSxS_0, cond_64, mask_BxS_bk0, mask_BxS_bf1, L0_cond_g_in, L0_cond_null_attn_bias, L0_cond_Wq, L0_cond_Wkv, L0_cond_Wo, L0_cond_g_out, L0_attn_norm_w, L0_attn_in_proj_w, L0_attn_A_proj_w, L0_attn_A_proj_b, L0_attn_A_base, L0_attn_B_proj_w, L0_attn_C_proj_w, L0_attn_D, L0_attn_out_proj_w, L0_cond2_g_norm, L0_cond2_Wq, L0_cond2_Wkv, L0_cond2_q_scale, L0_cond2_k_scale, L0_cond2_null_attn_bias, L0_cond2_w0, L0_cond2_b0, L0_cond2_g0, L0_cond2_w1, L0_cond2_b1, L0_cond2_g1, L0_cond2_w2, L0_cond2_b2, L0_cond2_Wout, L0_cond2_g_out, L0_ffn_gate_w, L0_ffn_gate_b, L0_ffn_expert_w, L0_ffn_expert_b):
    import jax
    import jax.numpy as jnp

    def _L0_cond_ref(x, attn_bias, mask, g_in, null_attn_bias, null_kv, Wq, Wkv, Wo, g_out):
        import jax, jax.numpy as jnp
        import numpy as np
        B, N, DIM, H, DH = (2, 512, 256, 16, 64)
        INNER = H * DH
        EPS = 1e-05

        def layernorm(x, g):
            mean = jnp.mean(x, axis=-1, keepdims=True)
            var = jnp.var(x, axis=-1, keepdims=True)
            return (x - mean) * jax.lax.rsqrt(var + EPS) * g
        b, n, _ = x.shape
        scale = DH ** (-0.5)
        xn = layernorm(x, g_in)
        q = (xn @ Wq).reshape(b, n, H, DH).transpose(0, 2, 1, 3) * scale
        kv = xn @ Wkv
        k, v = (kv[..., :DH], kv[..., DH:])
        nk = jnp.broadcast_to(null_kv[0], (b, 1, DH))
        nv = jnp.broadcast_to(null_kv[1], (b, 1, DH))
        k = jnp.concatenate([nk, k], axis=1)
        v = jnp.concatenate([nv, v], axis=1)
        sim = jnp.einsum('bhid,bjd->bhij', q, k)
        null_col = jnp.broadcast_to(null_attn_bias[:, None, None], (H, n, 1))
        bias = jnp.concatenate([null_col, attn_bias], axis=-1)
        sim = sim + bias
        neg = -jnp.finfo(sim.dtype).max
        j = n + 1
        causal_mask = jnp.triu(jnp.ones((n, j), dtype=bool), k=j - n + 1)
        sim = jnp.where(causal_mask, neg, sim)
        mask_p = jnp.pad(mask, ((0, 0), (1, 0)), constant_values=True)
        sim = jnp.where(mask_p[:, None, None, :], sim, neg)
        attn = jax.nn.softmax(sim, axis=-1)
        out = jnp.einsum('bhij,bjd->bhid', attn, v)
        out = out.transpose(0, 2, 1, 3).reshape(b, n, INNER)
        out = out @ Wo
        return layernorm(out, g_out)

    def _L0_attn_ref(x, norm_w, in_proj_w, A_proj_w, A_proj_b, A_base, B_proj_w, C_proj_w, D, out_proj_w):
        import jax, jax.numpy as jnp
        import numpy as np
        B, T, H = (2, 512, 256)
        EXPAND, N = (2, 16)
        DIN = H * EXPAND
        EPS = 1e-06

        def rmsnorm(x, w):
            var = jnp.mean(x * x, axis=-1, keepdims=True)
            return x * jax.lax.rsqrt(var + EPS) * w

        def liquid_scan(x_in, a_mod, a_base, B_in, C_in):

            def step(h, inp):
                a_t, b_t, c_t, x_t = inp
                h = a_t[:, :, None] * a_base * h + b_t[:, None, :] * x_t[:, :, None]
                y_t = jnp.einsum('bdn,bn->bd', h, c_t)
                return (h, y_t)
            h0 = jnp.zeros((x_in.shape[0], DIN, N), x_in.dtype)
            xs = (jnp.swapaxes(a_mod, 0, 1), jnp.swapaxes(B_in, 0, 1), jnp.swapaxes(C_in, 0, 1), jnp.swapaxes(x_in, 0, 1))
            _, ys = jax.lax.scan(step, h0, xs)
            return jnp.swapaxes(ys, 0, 1)
        residual = x
        xn = rmsnorm(x, norm_w)
        xz = xn @ in_proj_w
        x_in, z = jnp.split(xz, 2, axis=-1)
        x_in = jax.nn.silu(x_in)
        a_mod = jax.nn.sigmoid(x_in @ A_proj_w + A_proj_b)
        a_base = jax.nn.sigmoid(A_base)
        B_in = x_in @ B_proj_w
        C_in = x_in @ C_proj_w
        y = liquid_scan(x_in, a_mod, a_base, B_in, C_in)
        y = (y + D * x_in) * jax.nn.silu(z)
        return residual + y @ out_proj_w

    def _L0_cond2_ref(x, mask, g_norm, Wq, Wkv, q_scale, k_scale, null_kv, null_attn_bias, w0, b0, g0, w1, b1, g1, w2, b2, Wout, g_out):
        import jax, jax.numpy as jnp
        import numpy as np
        DIM = 256
        HEADS = 16
        DIM_HEAD = 64
        SCALE = 8.0

        def ln(x, g, eps=1e-05):
            mean = x.mean(axis=-1, keepdims=True)
            var = ((x - mean) ** 2).mean(axis=-1, keepdims=True)
            return (x - mean) * jax.lax.rsqrt(var + eps) * g

        def l2norm(t):
            n = jnp.maximum(jnp.linalg.norm(t, axis=-1, keepdims=True), 1e-12)
            return t / n

        def rel_pos_bias(n, w0, b0, g0, w1, b1, g1, w2, b2, dtype):
            pos = jnp.arange(-n + 1, n, dtype=dtype)[:, None]
            h = jax.nn.silu(ln(pos @ w0 + b0, g0))
            h = jax.nn.silu(ln(h @ w1 + b1, g1))
            h = h @ w2 + b2
            i = jnp.arange(n)
            idx = i[:, None] - i[None, :] + n - 1
            bias = h[idx]
            return jnp.transpose(bias, (2, 0, 1))
        b, n, _ = x.shape
        xn = ln(x, g_norm)
        q = (xn @ Wq).reshape(b, n, HEADS, DIM_HEAD).transpose(0, 2, 1, 3)
        kv = xn @ Wkv
        k, v = (kv[..., :DIM_HEAD], kv[..., DIM_HEAD:])
        nk = jnp.broadcast_to(null_kv[0], (b, 1, DIM_HEAD))
        nv = jnp.broadcast_to(null_kv[1], (b, 1, DIM_HEAD))
        k = jnp.concatenate([nk, k], axis=1)
        v = jnp.concatenate([nv, v], axis=1)
        q = l2norm(q) * q_scale
        k = l2norm(k) * k_scale
        sim = jnp.einsum('bhid,bjd->bhij', q, k) * SCALE
        bias = rel_pos_bias(n, w0, b0, g0, w1, b1, g1, w2, b2, q.dtype)
        null_bias = jnp.broadcast_to(null_attn_bias[:, None, None], (HEADS, n, 1))
        attn_bias = jnp.concatenate([null_bias, bias], axis=-1)
        sim = sim + attn_bias
        neg = -jnp.finfo(sim.dtype).max
        causal = jnp.triu(jnp.ones((n, n + 1), dtype=bool), k=2)
        sim = jnp.where(causal, neg, sim)
        m = jnp.pad(mask, ((0, 0), (1, 0)), constant_values=True)[:, None, None, :]
        sim = jnp.where(m, sim, neg)
        attn = jax.nn.softmax(sim, axis=-1)
        out = jnp.einsum('bhij,bjd->bhid', attn, v)
        out = out.transpose(0, 2, 1, 3).reshape(b, n, HEADS * DIM_HEAD)
        return ln(out @ Wout, g_out)

    def _L0_ffn_ref(x, gate_w, gate_b, expert_w, expert_b):
        import jax, jax.numpy as jnp
        import numpy as np
        NUM_EXPERTS = 8
        D_MODEL = 256
        D_OUT = 256
        orig_shape = x.shape
        xt = x.reshape(-1, D_MODEL)
        logits = xt @ gate_w + gate_b
        gates = jax.nn.softmax(logits, axis=-1)
        sel = jnp.argmax(gates, axis=-1)
        onehot = jax.nn.one_hot(sel, NUM_EXPERTS, dtype=xt.dtype)
        y_all = jnp.einsum('td,edh->eth', xt, expert_w) + expert_b[:, None, :]
        out = jnp.einsum('te,eth->th', onehot, y_all)
        return out.reshape(*orig_shape[:-1], D_OUT)
    x = x + _L0_attn_ref(_L0_cond_ref(x, fside_16xSxS_0, mask_BxS_bk0, L0_cond_g_in, L0_cond_null_attn_bias, cond_64, L0_cond_Wq, L0_cond_Wkv, L0_cond_Wo, L0_cond_g_out), L0_attn_norm_w, L0_attn_in_proj_w, L0_attn_A_proj_w, L0_attn_A_proj_b, L0_attn_A_base, L0_attn_B_proj_w, L0_attn_C_proj_w, L0_attn_D, L0_attn_out_proj_w)
    x = x + _L0_ffn_ref(_L0_cond2_ref(x, mask_BxS_bf1, L0_cond2_g_norm, L0_cond2_Wq, L0_cond2_Wkv, L0_cond2_q_scale, L0_cond2_k_scale, cond_64, L0_cond2_null_attn_bias, L0_cond2_w0, L0_cond2_b0, L0_cond2_g0, L0_cond2_w1, L0_cond2_b1, L0_cond2_g1, L0_cond2_w2, L0_cond2_b2, L0_cond2_Wout, L0_cond2_g_out), L0_ffn_gate_w, L0_ffn_gate_b, L0_ffn_expert_w, L0_ffn_expert_b)
    return x

_drawn_inputs = setup_inputs


def setup_inputs(seed=0):
    import zlib

    import numpy as np

    out = dict(_drawn_inputs(seed))
    spreads = {'L0_cond_g_in': (1.0, 0.2),
     'L0_cond_g_out': (1.0, 0.2),
     'L0_attn_norm_w': (1.0, 0.2),
     'L0_attn_D': (1.0, 0.555),
     'L0_cond2_g_norm': (1.0, 0.2),
     'L0_cond2_q_scale': (1.0, 0.2),
     'L0_cond2_k_scale': (1.0, 0.6),
     'L0_cond2_b0': (0.0, 1.383),
     'L0_cond2_g0': (1.0, 0.6),
     'L0_cond2_b1': (0.0, 2.0),
     'L0_cond2_g1': (1.0, 0.6),
     'L0_cond2_b2': (0.0, 1.692),
     'L0_cond2_g_out': (1.0, 0.2),
     'L0_ffn_gate_b': (0.0, 0.273),
     'L0_ffn_expert_b': (0.0, 0.1)}
    factors = {'L0_attn_A_proj_b': 8.0, 'L0_cond2_w0': 6.443, 'L0_cond2_w1': 3.986, 'L0_cond2_w2': 3.372}
    for name, (base, spread) in spreads.items():
        noise = np.random.default_rng([zlib.crc32(name.encode()), seed]).standard_normal(out[name].shape)
        drawn = base * np.exp(spread * noise) if base else spread * noise
        out[name] = jnp.asarray(drawn.astype(out[name].dtype))
    for name, factor in factors.items():
        out[name] = (out[name] * factor).astype(out[name].dtype)
    return out
```

```python
from contextlib import ExitStack

import numpy as np

import concourse.bass as bass
from concourse import mybir

P = 128
S = 64
BT = P // S
D = 256
KD = D // P
H = 16
DH = 64
HP = H // 2
HI = H * S
E2 = 512
KE = E2 // P
NST = 16
NLV = 4
LVW = 32
NE = 8
NPOS = 2 * S - 1
NEG = -1.0e30
DECAY_FLOOR = 20.0
LAMBDA_FLOOR = 12.0
GUARD = float(2.0 ** 57)
L2_SCALE = float(2.0 ** 20)

ALU = mybir.AluOpType
ACT = mybir.ActivationFunctionType
F32 = mybir.dt.float32
F32R = mybir.dt.float32r
BF16 = mybir.dt.bfloat16
U8 = mybir.dt.uint8
AX_X = mybir.AxisListType.X


def constants():
    tok = np.arange(P)
    seq, pos = tok // S, tok % S
    same = seq[:, None] == seq[None, :]
    parts = {"ident": np.eye(P)}
    parts["causal"] = np.where(np.arange(S)[None, :] > pos[:, None], NEG, 0.0)
    half = (tok[:, None] // DH) == (tok[None, :] // DH)
    parts["halves"] = half * 1.0
    parts["pair"] = half[:, [0, DH]] * 1.0
    sums, count_b, count_c, masks = [], [], [], []
    r, t = pos[:, None], pos[None, :]
    ref = (t // 8) * 8 + 3
    sums.append(same * (1.0 * ((r > ref) & (r <= t)) - 1.0 * ((r > t) & (r <= ref))))
    count_c.append(pos - ((pos // 8) * 8 + 3))
    count_b.append(-count_c[0])
    masks.append(same & (r // 8 == t // 8) & (r <= t))
    for m in (8, 16, 32):
        left = (t // m) % 2 == 0
        start = (t // (2 * m)) * 2 * m + m
        sums.append(same * np.where(left, (r > t) & (r < start), (r >= start) & (r <= t)))
        start = (pos // (2 * m)) * 2 * m + m
        is_left = (pos // m) % 2 == 0
        count_b.append(np.where(is_left, start - 1 - pos, 0))
        count_c.append(np.where(is_left, 0, pos - start + 1))
        masks.append(same & (r // (2 * m) == t // (2 * m)) & ((r // m) % 2 == 0) & ((t // m) % 2 == 1))
    parts["sums"] = np.concatenate(sums, 1)
    parts["neg_count_b"] = -np.stack(count_b, 1)
    parts["neg_count_c"] = -np.stack(count_c, 1)
    parts["scan_mask"] = np.concatenate(masks, 1)
    parts["level_rows"] = (tok[:, None] // LVW == np.arange(NLV)[None, :]) * 1.0
    parts["rank"] = np.broadcast_to(NE - np.arange(NE), (P, NE))
    parts["distance"] = (S - 1 - tok)[:, None]
    at, n = {}, 0
    for name, a in parts.items():
        at[name] = (n, a.shape[1])
        n += a.shape[1]
    return at, np.concatenate([np.asarray(a, np.float32) for a in parts.values()], 1)


class Progress:

    def __init__(self, sem, names):
        self.sem, self.names, self.turn = sem, names, 0

    def at(self, name, t):
        value = t * len(self.names) + (self.names.index(name) + 1)
        return self.sem, max(value, 0) if isinstance(value, int) else value

    def done(self, name):
        assert self.names[self.turn] == name, (name, self.names[self.turn])
        self.turn = (self.turn + 1) % len(self.names)
        return self.sem


ATT_PE = ["xt", "kv", "q0", "q1", "S0", "S1", "PT0", "PT1", "O0", "O1", "W"]
ATT_ACT = ["rstd_l", "rstd", "xnT", "q0", "q1", "expm", "prob", "PT0", "PT1", "O0", "O1", "rstd2_l", "rstd2"]
ATT_DVE = ["st", "mv", "xn", "K0", "K1", "V0", "V1", "S0", "S1", "mx", "mx0", "sub", "sum", "den", "rden",
           "st2", "mv2", "cn", "c"]
ATT_POOL = ["biasm", "norm"]
COS_PE = ["xt", "kv", "ks", "q0", "q1", "qs", "S0", "S1", "PT0", "PT1", "O0", "O1", "W",
          "ct", "lg", "oT", "ex0", "ex1", "ex2", "ex3", "eb"]
COS_ACT = ["rstd_l", "rstd", "xnT", "ksq", "kr_l", "kr", "q0", "q1", "qr_l", "qr", "expm", "prob",
           "PT0", "PT1", "O0", "O1", "rstd2_l", "rstd2", "cT", "le", "oT"]
COS_DVE = ["x1c", "st", "mv", "xn", "ks", "kn", "K0", "K1", "V0", "V1", "qs", "S0", "S1", "mx", "mx0", "sub",
           "sum", "den", "rden", "st2", "mv2", "cn", "c",
           "lb", "lm", "ld", "eq", "em", "oh"] + [f"ac{e}" for e in range(NE)] + ["out"]
COS_POOL = ["biasm", "qsq", "addb", "norm"]
SCAN_PE = ["xt", "x", "z", "xiT", "a", "bc", "gt", "E0", "E1", "E2", "E3", "G", "m0", "m1", "m2", "m3", "yT", "out"]
SCAN_ACT = ["ss", "r_l", "r", "xnT", "xe", "ze", "xl", "xs", "zl", "zs", "xiT", "ae", "nl", "BT",
            "E0", "E0u", "E1", "E2", "E3", "yT"]
SCAN_DVE = ["xn", "xg", "zg", "xi", "zi", "ag", "Bt", "Ct", "CD", "Gm", "t0", "t1", "t2", "t3", "x1"]
SCAN_POOL = ["resid", "dx", "u0", "u1", "u2", "u3", "y0", "y1", "y2", "y3", "y"]

ATT_BANK = {"xt": 0, "kv": 1, "q0": 2, "q1": 0, "S0": 1, "S1": 2, "PT0": 0, "PT1": 1, "O0": 2, "O1": 0, "W": 1}
COS_BANK = {"xt": 0, "kv": 1, "ks": 2, "q0": 0, "q1": 1, "qs": 2, "S0": 0, "S1": 1, "PT0": 2, "PT1": 0,
            "O0": 1, "O1": 2, "W": 0, "ct": 1, "lg": 2, "oT": 0, "ex0": 1, "ex1": 2, "ex2": 0, "ex3": 1, "eb": 2}
SCAN_BANK = {"xt": 0, "x": 1, "z": 0, "xiT": 1, "a": 0, "bc": 1, "gt": 0, "E0": 1, "E1": 0, "E2": 1, "E3": 0,
             "G": 1, "m0": 0, "m1": 1, "m2": 0, "m3": 1, "yT": 0, "out": 1}
ATT_LAST = {"xt": ("act", "xnT"), "kv": ("dve", "V1"), "q0": ("act", "q0"), "q1": ("act", "q1"),
            "S0": ("dve", "S0"), "S1": ("dve", "S1"), "PT0": ("act", "PT0"), "PT1": ("act", "PT1"),
            "O0": ("act", "O0"), "O1": ("act", "O1"), "W": ("dve", "cn")}
COS_LAST = dict(ATT_LAST, ks=("dve", "ks"), qs=("dve", "qs"), ct=("act", "cT"), lg=("dve", "lb"), oT=("act", "oT"),
                ex0=("dve", "ac1"), ex1=("dve", "ac3"), ex2=("dve", "ac5"), ex3=("dve", "ac7"), eb=("dve", "out"))
SCAN_LAST = {"xt": ("act", "xnT"), "x": ("dve", "xi"), "z": ("dve", "zi"), "xiT": ("act", "xiT"), "a": ("act", "ae"),
             "bc": ("dve", "Ct"), "gt": ("dve", "CD"), "G": ("dve", "Gm"), "E0": ("act", "E0u"), "E1": ("act", "E1"),
             "E2": ("act", "E2"), "E3": ("act", "E3"), "m0": ("dve", "t0"), "m1": ("dve", "t1"), "m2": ("dve", "t2"),
             "m3": ("dve", "t3"), "yT": ("act", "yT"), "out": ("dve", "x1")}

MLP_DVE = ["h0", "st0", "mv0", "n0", "v0", "e0", "s0", "T0", "h1", "st1", "mv1", "n1", "v1", "e1", "s1", "T1",
           "pos", "posT"]
MLP_ACT = ["rl0", "r0", "e0", "l0", "s0", "rl1", "r1", "e1", "l1", "s1"]
MLP_PE = ["T0", "h1", "T1", "pos", "posT"]

ORDER = [
    "a.st", "b.rms", "c.st", "a.xn", "b.xn", "c.xn", "a.xt", "b.xt", "c.xt", "a.kv", "b.in", "c.kv",
    "a.q", "b.silu", "c.kn", "c.q", "b.xiT", "a.S", "c.qn", "b.ab", "c.S", "a.sm", "b.gt", "b.E", "c.sm", "a.norm",
    "b.G", "c.norm", "a.PT", "b.m01", "c.PT", "a.PV", "b.m23", "c.PV", "a.W", "c.W", "b.yT", "a.fin", "c.fin",
    "b.out", "c.ct", "c.lg", "c.ex", "c.eb",
]


class Stream:

    def __init__(self, s, sem, names, banks, bank, last):
        self.pe, self.act, self.dve, self.pool = (Progress(sem(f"{s}_{e}_done"), names[e])
                                                  for e in ("pe", "act", "dve", "pool"))
        self.bank = {unit: banks[n] for unit, n in bank.items()}
        self.number, self.last = bank, last

    def free(self, unit, t):
        mates = [u for u in self.number if self.number[u] == self.number[unit]]
        k = mates.index(unit)
        engine, mark = self.last[mates[k - 1]]
        readers = {"act": self.act, "dve": self.dve}
        return readers[engine].at(mark, t if k else t - 1)


def build(nc, x, out, ins, consts_dram, consts_at):
    NT = x.shape[0] * x.shape[1] // P
    ctx = ExitStack()
    with ctx:
        def sb(name, shape, dt=F32):
            return ctx.enter_context(nc.sbuf_tensor(name, shape, dt))

        def sem(name):
            return ctx.enter_context(nc.semaphore(name))

        banks = {s: [ctx.enter_context(nc.psum_tensor(f"{s}_bank{n}", [P, 512], F32)) for n in range(k)]
                 for s, k in (("a", 3), ("b", 2), ("c", 3))}

        def stream(s, names, bank, last):
            return Stream(s, sem, names, banks[s], bank, last)

        A = stream("a", {"pe": ATT_PE, "act": ATT_ACT, "dve": ATT_DVE, "pool": ATT_POOL}, ATT_BANK, ATT_LAST)
        B = stream("b", {"pe": SCAN_PE, "act": SCAN_ACT, "dve": SCAN_DVE, "pool": SCAN_POOL}, SCAN_BANK, SCAN_LAST)
        C = stream("c", {"pe": COS_PE, "act": COS_ACT, "dve": COS_DVE, "pool": COS_POOL}, COS_BANK, COS_LAST)

        consts = sb("consts", [P, consts_dram.shape[1]])

        def const(name, rows=P):
            n, w = consts_at[name]
            return consts[0:rows, n:n + w]

        ident = const("ident")
        for X, s in ((A, "a"), (C, "c")):
            X.wq = sb(f"{s}_wq", [P, KD, H * DH])
            X.wkk = sb(f"{s}_wkk", [P, KD, 2, DH])
            X.wv = sb(f"{s}_wv", [P, KD, DH])
            X.wo = sb(f"{s}_wo", [P, HP, D])
            X.g = sb(f"{s}_g", [P, KD])
            X.g_out = sb(f"{s}_g_out", [P, D])
            X.null_bias = sb(f"{s}_null_bias", [P, H])
            X.bias = sb(f"{s}_bias", [P, H, S])
            X.mask = sb(f"{s}_mask", [P, NT, S], BF16)
            X.xin = sb(f"{s}_xin", [P, D])
            X.st = sb(f"{s}_st", [P, 6])
            X.mv = sb(f"{s}_mv", [P, 2])
            X.rstd_l = sb(f"{s}_rstd_l", [P, 1])
            X.rstd = sb(f"{s}_rstd", [P, 1])
            X.xn = sb(f"{s}_xn", [P, D])
            X.xnT = sb(f"{s}_xnT", [P, KD, P])
            X.K = sb(f"{s}_K", [P, BT, P])
            X.V = sb(f"{s}_V", [P, BT, P])
            X.qT = sb(f"{s}_qT", [P, HP, P])
            X.biasm = sb(f"{s}_biasm", [P, H, S])
            X.prob = sb(f"{s}_prob", [P, H, S])
            X.mx = sb(f"{s}_mx", [P, H])
            X.mx0 = sb(f"{s}_mx0", [P, H])
            X.expm = sb(f"{s}_expm", [P, H])
            X.sum = sb(f"{s}_sum", [P, H])
            X.den = sb(f"{s}_den", [P, H])
            X.rden = sb(f"{s}_rden", [P, H])
            X.PT = sb(f"{s}_PT", [P, HP, P])
            X.OT = sb(f"{s}_OT", [P, HP, P])
            X.st2 = sb(f"{s}_st2", [P, 6])
            X.mv2 = sb(f"{s}_mv2", [P, 2])
            X.rstd2_l = sb(f"{s}_rstd2_l", [P, 1])
            X.rstd2 = sb(f"{s}_rstd2", [P, 1])
            X.cn = X.xn
            X.c = sb(f"{s}_c", [P, D])
            X.wkv = X.PT[:, 0:KD, :]
            X.mask_u8 = X.prob[:, 0:NT * S // (4 * S), :].bitcast(U8).rearrange("p a (b s) -> p (a b) s", s=S)
        nk_col = sb("nk_col", [P, 1])
        nv_col = sb("nv_col", [P, 1])
        nv_row = sb("nv_row", [P, DH])
        eps5 = sb("eps5", [P, 1])
        wait_carrier = sb("wait_carrier", [P, 1])
        eps6 = sb("eps6", [P, 1])
        w_in = sb("w_in", [P, KD, 2 * E2])
        w_a = sb("w_a", [P, KE, E2])
        w_bc = sb("w_bc", [P, KE, 2 * NST])
        w_out = sb("w_out", [P, KE, D])
        norm_w = sb("norm_w", [P, KD])
        a_bias_hi = sb("decay_bias_hi", [1, E2], F32R)
        a_bias_lo = sb("decay_bias_lo", [1, E2], F32R)
        ones_r = sb("ones_r", [1, P], F32R)
        d_row = sb("d_row", [P, E2])
        a_base = sb("a_base", [P, NST])
        lam_e = sb("lam_e", [P, NST])
        lam_g = sb("lam_g", [P, NST])
        lam = sb("lam", [P, NST])
        lam_b = sb("lam_b", [P, NLV, NST])
        lam_c = sb("lam_c", [P, NLV, NST])
        xres = sb("xres", [P, D])
        resid = sb("resid", [P, D])
        ss = sb("ss", [P, 1])
        r_l = sb("r_l", [P, 1])
        r_ms = sb("r_ms", [P, 1])
        yn = sb("yn", [P, D])
        ynT = sb("ynT", [P, KD, P])
        xe = sb("xe", [P, E2])
        ze = sb("ze", [P, E2])
        xs, zs = xe, ze
        xi = sb("xi", [P, E2])
        zi = sb("zi", [P, E2])
        xiT = sb("xiT", [P, KE, P])
        nl = sb("nl", [P, E2])
        ae = nl
        Bt = sb("Bt", [P, NLV, LVW])
        Ct = sb("Ct", [P, NLV, LVW])
        BTt = sb("BTt", [P, P])
        CD = sb("CD", [P, NLV, P])
        Gm = sb("Gm", [P, NLV, P])
        Ef = [sb(f"Ef{l}", [P, E2]) for l in range(NLV)]
        E0u = sb("E0u", [P, E2])
        u = [sb(f"u{l}", [P, E2]) for l in range(NLV)]
        tm = u
        y = sb("y", [P, E2])
        a_bias = y[0:1, :]
        ones_f = E0u[0:1, 0:P]
        yT = sb("yT", [P, KE, P])
        x1 = sb("x1", [P, D])
        q_scale = sb("q_scale", [P, 1])
        k_scale = sb("k_scale", [P, 1])
        kq = sb("kq", [P, 1])
        nk_sq = sb("nk_sq", [P, 1])
        nk_ss = sb("nk_ss", [P, 1])
        nk_l = sb("nk_l", [P, 1])
        nk_r = sb("nk_r", [P, 1])
        nk_n = sb("nk_n", [P, 1])
        ksq = sb("ksq", [P, P])
        kss = sb("kss", [P, P])
        kr_l = kr = kn = kss
        qss = sb("qss", [P, H])
        qr_l = sb("qr_l", [P, H])
        qr = sb("qr", [P, H])
        gate_w = sb("gate_w", [P, KD, NE])
        gate_b = sb("gate_b", [P, NE])
        w_e = sb("w_e", [P, KD, NE, D])
        b_e = sb("b_e", [NE, D])
        cT = sb("cT", [P, KD, P])
        lb = sb("lb", [P, NE])
        lm = sb("lm", [P, 1])
        ld = sb("ld", [P, NE])
        le = sb("le", [P, NE])
        eq = sb("eq", [P, NE])
        em = sb("em", [P, 1])
        oh = sb("oh", [P, NE])
        ohT = sb("ohT", [NE, P])
        acc = sb("acc", [P, D])
        acc2 = C.cn
        yout = acc
        qsq = C.PT
        m_w0, m_b0, m_g0 = Ef[0][:, 0:D], Ef[0][:, D:], Ef[1][:, 0:D]
        m_b1, m_g1 = Ef[1][:, D:], Ef[2][:, 0:D]
        m_w1 = u[0][:, :].rearrange("p (k n) -> p k n", k=KD)
        m_w2 = Ef[3][:, 0:KD * H].rearrange("p (k n) -> p k n", k=KD)
        m_b2 = Ef[3][:, 64:64 + H]
        mh = [CD[:, 0:2, :], CD[:, 2:4, :], Gm[:, 0:2, :], Gm[:, 2:4, :], y[:, 0:D], y[:, D:]]
        mh = [m.rearrange("p l n -> p (l n)") for m in mh[0:4]] + mh[4:]
        mhT = nl[:, 0:D].rearrange("p (k n) -> p k n", k=KD)
        m_pos = C.biasm[:, 2, 0:H]
        m_posT = C.biasm[0:H, 0:2, :].rearrange("p a n -> p (a n)")
        m_scr = nc.dram_tensor("position_rows", (H, S, NPOS), F32, kind="Internal").ap()

        ld_const, ld_a, ld_b, ld_mlp, ld_c = sem("ld_const"), sem("ld_a"), sem("ld_b"), sem("ld_mlp"), sem("ld_c")
        n_ld = {}

        def load(eng, s, dst, src):
            eng.dma_start(dst, src, allow_slow_non_contiguous=True).then_inc(s, 16)
            n_ld[s.name] = n_ld.get(s.name, 0) + 16

        prep_a, prep_b, prep_c = sem("prep_a"), sem("prep_b"), sem("prep_c")
        prep_lam = sem("prep_lam")
        prep_lam_g = sem("prep_lam_g")
        prep_pool_a, prep_pool_c = sem("prep_pool_a"), sem("prep_pool_c")
        prep_nk, prep_nk_pe, prep_nk_act = sem("prep_nk"), sem("prep_nk_pe"), sem("prep_nk_act")
        mlp_dve = Progress(sem("mlp_dve"), MLP_DVE)
        mlp_act = Progress(sem("mlp_act"), MLP_ACT)
        mlp_pe = Progress(sem("mlp_pe"), MLP_PE)
        mlp_dma = sem("mlp_dma")
        x_loaded, xres_loaded, out_stored = sem("x_loaded"), sem("xres_loaded"), sem("out_stored")

        xt_dram = x.rearrange("(t b) s d -> t (b s) d", b=BT)
        ot_dram = out.rearrange("(t b) s d -> t (b s) d", b=BT)

        def col(ap):
            return ap.rearrange("(k p) -> p k", p=P)

        def rows(ap, n=P):
            return ap.unsqueeze(0).broadcast_to([n, ap.shape[0]])

        null_k, null_v = ins["cond_64"][0], ins["cond_64"][1]

        block = ctx.enter_context(nc.Block())

        def tiles(eng, run):
            run(0, "a")
            run(1, "ab")
            run(2, "abc")
            with eng.Fori(3, NT) as i:
                run(i, "abc")
            run(NT, "bc")
            run(NT + 1, "c")

        LAG = {"a": 0, "b": 1, "c": 2}

        def in_order(steps, i, streams):
            for name in ORDER:
                if name[0] in streams and name in steps:
                    steps[name](i - LAG[name[0]])

        @block.sync
        def _(sp):
            load(sp, ld_const, consts[:, :], consts_dram)
            sp.dma_start(A.xin[:, :], xt_dram[0]).then_inc(x_loaded, 16)
            load(sp, ld_a, A.g[:, :], col(ins["L0_cond_g_in"]))
            load(sp, ld_a, A.wkv[:, :, :], ins["L0_cond_Wkv"].rearrange("(k p) n -> p k n", p=P))
            load(sp, ld_a, A.wq[:, :, :], ins["L0_cond_Wq"].rearrange("(k p) n -> p k n", p=P))
            load(sp, ld_a, nk_col[0:DH, :], null_k.unsqueeze(1))
            load(sp, ld_a, nk_col[DH:P, :], null_k.unsqueeze(1))
            load(sp, ld_a, nv_col[0:DH, :], null_v.unsqueeze(1))
            load(sp, ld_a, nv_col[DH:P, :], null_v.unsqueeze(1))
            load(sp, ld_a, nv_row[:, :], rows(null_v))
            load(sp, ld_a, A.null_bias[:, :], rows(ins["L0_cond_null_attn_bias"]))
            for b in range(BT):
                part = slice(b * S, (b + 1) * S)
                load(sp, ld_a, A.bias[part, :, :], ins["fside_16xSxS_0"].rearrange("h i j -> i h j"))
                load(sp, ld_a, A.mask_u8[part, :, :],
                     ins["mask_BxS_bk0"].rearrange("(t b) j -> b t j", b=BT)[b].unsqueeze(0).broadcast_to([S, NT, S]))
            load(sp, ld_a, A.wo[:, :, :], ins["L0_cond_Wo"].rearrange("(k p) n -> p k n", p=P))
            load(sp, ld_a, A.g_out[:, :], rows(ins["L0_cond_g_out"]))
            load(sp, ld_b, norm_w[:, :], col(ins["L0_attn_norm_w"]))
            load(sp, ld_b, w_in[:, :, :], ins["L0_attn_in_proj_w"].rearrange("(k p) n -> p k n", p=P))
            load(sp, ld_b, w_a[:, :, :], ins["L0_attn_A_proj_w"].rearrange("(k p) n -> p k n", p=P))
            load(sp, ld_b, w_bc[:, :, 0:NST], ins["L0_attn_B_proj_w"].rearrange("(k p) n -> p k n", p=P))
            load(sp, ld_b, w_bc[:, :, NST:], ins["L0_attn_C_proj_w"].rearrange("(k p) n -> p k n", p=P))
            load(sp, ld_b, w_out[:, :, :], ins["L0_attn_out_proj_w"].rearrange("(k p) n -> p k n", p=P))
            load(sp, ld_b, a_bias[:, :], ins["L0_attn_A_proj_b"].unsqueeze(0))
            load(sp, ld_b, d_row[:, :], rows(ins["L0_attn_D"]))
            load(sp, ld_b, a_base[:, :], rows(ins["L0_attn_A_base"]))
            load(sp, ld_mlp, m_w0, rows(ins["L0_cond2_w0"][0]))
            for dst, name in ((m_b0, "b0"), (m_g0, "g0"), (m_b1, "b1"), (m_g1, "g1"), (m_b2, "b2")):
                load(sp, ld_mlp, dst, rows(ins["L0_cond2_" + name]))
            load(sp, ld_mlp, m_w1, ins["L0_cond2_w1"].rearrange("(k p) n -> p k n", p=P))
            load(sp, ld_mlp, m_w2, ins["L0_cond2_w2"].rearrange("(k p) n -> p k n", p=P))
            load(sp, ld_c, C.g[:, :], col(ins["L0_cond2_g_norm"]))
            load(sp, ld_c, C.wkv[:, :, :], ins["L0_cond2_Wkv"].rearrange("(k p) n -> p k n", p=P))
            load(sp, ld_c, C.wq[:, :, :], ins["L0_cond2_Wq"].rearrange("(k p) n -> p k n", p=P))
            for part in (slice(0, DH), slice(DH, P)):
                load(sp, ld_c, q_scale[part, :], ins["L0_cond2_q_scale"].unsqueeze(1))
                load(sp, ld_c, k_scale[part, :], ins["L0_cond2_k_scale"].unsqueeze(1))
            load(sp, ld_c, C.null_bias[:, :], rows(ins["L0_cond2_null_attn_bias"]))
            for b in range(BT):
                part = slice(b * S, (b + 1) * S)
                load(sp, ld_c, C.mask_u8[part, :, :],
                     ins["mask_BxS_bf1"].rearrange("(t b) j -> b t j", b=BT)[b].unsqueeze(0).broadcast_to([S, NT, S]))
            load(sp, ld_c, C.wo[:, :, :], ins["L0_cond2_Wout"].rearrange("(k p) n -> p k n", p=P))
            load(sp, ld_c, C.g_out[:, :], rows(ins["L0_cond2_g_out"]))
            load(sp, ld_c, gate_w[:, :, :], ins["L0_ffn_gate_w"].rearrange("(k p) n -> p k n", p=P))
            load(sp, ld_c, gate_b[:, :], rows(ins["L0_ffn_gate_b"]))
            for k in range(KD):
                load(sp, ld_c, w_e[:, k, :, :],
                     ins["L0_ffn_expert_w"][:, k * P:(k + 1) * P, :].rearrange("e p n -> p e n"))
            load(sp, ld_c, b_e[:, :], ins["L0_ffn_expert_b"])
            def position_bias():
                sp.wait_ge(*mlp_dve.at("posT", 0))
                sp.dma_start(m_scr, m_posT[:, 0:NPOS].unsqueeze(1).broadcast_to([H, S, NPOS])).then_inc(mlp_dma, 16)
                sp.wait_ge(mlp_dma, 16)
                flat = m_scr.rearrange("h i w -> h (i w)")[:, S - 1:S - 1 + S * (NPOS - 1)]
                skewed = flat.rearrange("h (i w) -> i h w", w=NPOS - 1)[:, :, 0:S]
                for b in range(BT):
                    sp.dma_start(C.bias[b * S:(b + 1) * S, :, :], skewed).then_inc(mlp_dma, 16)

            def load_x(t):
                sp.wait_ge(*A.dve.at("xn", t))
                sp.dma_start(A.xin[:, :], xt_dram[t + 1]).then_inc(x_loaded, 16)

            def load_xres(t):
                sp.wait_ge(*B.pool.at("resid", t - 1))
                sp.dma_start(xres[:, :], xt_dram[t]).then_inc(xres_loaded, 16)

            def store(t):
                sp.wait_ge(*C.dve.at("out", t))
                sp.dma_start(ot_dram[t], yout[:, :]).then_inc(out_stored, 16)

            load_xres(0)
            load_x(0)
            load_x(1)
            position_bias()
            load_xres(1)
            load_x(2)
            load_xres(2)
            store(0)
            with sp.Fori(3, NT - 1) as i:
                load_x(i)
                load_xres(i)
                store(i - 2)
            load_xres(NT - 1)
            store(NT - 3)
            store(NT - 2)
            store(NT - 1)
            sp.wait_ge(out_stored, 16 * NT)

        @block.tensor
        def _(pe):
            def attention(X, s):
                p, act, dve, pool = X.pe, X.act, X.dve, X.pool

                def xt(t):
                    pe.wait_ge(*dve.at("xn", t))
                    pe.wait_ge(*X.free("xt", t))
                    for k in range(KD):
                        mm = pe.transpose(X.bank["xt"][:, k * P:(k + 1) * P], X.xn[:, k * P:(k + 1) * P], ident)
                    mm.then_inc(p.done("xt"), 1)

                def kv(t):
                    pe.wait_ge(*act.at("xnT", t))
                    pe.wait_ge(*X.free("kv", t))
                    bank = X.bank["kv"]
                    for k in range(KD):
                        pe.matmul(bank[:, 0:P], X.wkk[:, k, :, :], X.xnT[:, k, :],
                                  start=k == 0, stop=k == KD - 1)
                    for b in range(BT):
                        for half in range(2):
                            for k in range(KD):
                                mm = pe.matmul(bank[half * S:(half + 1) * S, P + b * DH:P + (b + 1) * DH],
                                               X.xnT[:, k, b * S:(b + 1) * S], X.wv[:, k, :],
                                               start=k == 0, stop=k == KD - 1)
                    mm.then_inc(p.done("kv"), 1)

                def ks(t):
                    pe.wait_ge(*act.at("ksq", t))
                    pe.wait_ge(*X.free("ks", t))
                    pe.matmul(X.bank["ks"][:, 0:P], const("halves"), ksq[:, :], start=True, stop=True)\
                      .then_inc(p.done("ks"), 1)

                def q(t):
                    for half in range(2):
                        pe.wait_ge(*X.free(f"q{half}", t))
                        for m in range(4):
                            hp = 4 * half + m
                            for k in range(KD):
                                mm = pe.matmul(X.bank[f"q{half}"][:, m * P:(m + 1) * P],
                                               X.wq[:, k, hp * P:(hp + 1) * P], X.xnT[:, k, :],
                                               start=k == 0, stop=k == KD - 1)
                        mm.then_inc(p.done(f"q{half}"), 1)

                def qn(t):
                    pe.wait_ge(*pool.at("qsq", t))
                    pe.wait_ge(*X.free("qs", t))
                    for hp in range(HP):
                        mm = pe.matmul(X.bank["qs"][:, 2 * hp:2 * hp + 2], qsq[:, hp, :], const("pair"),
                                       start=True, stop=True)
                    mm.then_inc(p.done("qs"), 1)

                def scores(t):
                    pe.wait_ge(*dve.at("K1", t))
                    for half in range(2):
                        pe.wait_ge(*act.at(f"q{half}", t))
                        pe.wait_ge(*X.free(f"S{half}", t))
                        for m in range(4):
                            for b in range(BT):
                                mm = pe.matmul(X.bank[f"S{half}"][b * S:(b + 1) * S, m * P:(m + 1) * P],
                                               X.qT[:, 4 * half + m, b * S:(b + 1) * S], X.K[:, b, :],
                                               start=True, stop=True)
                        mm.then_inc(p.done(f"S{half}"), 1)

                def PT(t):
                    pe.wait_ge(*pool.at("norm", t))
                    for half in range(2):
                        pe.wait_ge(*X.free(f"PT{half}", t))
                        for m in range(4):
                            hp = 4 * half + m
                            mm = pe.transpose(X.bank[f"PT{half}"][:, m * P:(m + 1) * P],
                                              X.prob[:, 2 * hp:2 * hp + 2, :], ident)
                        mm.then_inc(p.done(f"PT{half}"), 1)

                def PV(t):
                    pe.wait_ge(*dve.at("V1", t))
                    pe.wait_ge(*act.at("PT1", t))
                    for b in range(BT):
                        pe.wait_ge(*X.free(f"O{b}", t))
                        pe.matmul(X.bank[f"O{b}"][:, :], X.V[:, b, :], X.PT[:, :, b * S:(b + 1) * S],
                                  start=True, stop=True).then_inc(p.done(f"O{b}"), 1)

                def W(t):
                    pe.wait_ge(*act.at("O1", t))
                    pe.wait_ge(*X.free("W", t))
                    for hp in range(HP):
                        mm = pe.matmul(X.bank["W"][:, 0:D], X.OT[:, hp, :], X.wo[:, hp, :],
                                       start=hp == 0, stop=hp == HP - 1)
                    mm.then_inc(p.done("W"), 1)

                steps = {f"{s}.xt": xt, f"{s}.kv": kv, f"{s}.q": q, f"{s}.S": scores, f"{s}.PT": PT,
                         f"{s}.PV": PV, f"{s}.W": W}
                if s == "c":
                    steps |= {"c.kn": ks, "c.qn": qn}
                return steps

            def scan():
                p, act, dve, pool = B.pe, B.act, B.dve, B.pool

                def xt(t):
                    pe.wait_ge(*dve.at("xn", t))
                    pe.wait_ge(*B.free("xt", t))
                    for k in range(KD):
                        mm = pe.transpose(B.bank["xt"][:, k * P:(k + 1) * P], yn[:, k * P:(k + 1) * P], ident)
                    mm.then_inc(p.done("xt"), 1)

                def proj(t):
                    pe.wait_ge(*act.at("xnT", t))
                    for n, unit in enumerate(("x", "z")):
                        pe.wait_ge(*B.free(unit, t))
                        for k in range(KD):
                            mm = pe.matmul(B.bank[unit][:, :], ynT[:, k, :], w_in[:, k, n * E2:(n + 1) * E2],
                                           start=k == 0, stop=k == KD - 1)
                        mm.then_inc(p.done(unit), 1)

                def xiT_(t):
                    pe.wait_ge(*dve.at("xi", t))
                    pe.wait_ge(*B.free("xiT", t))
                    for k in range(KE):
                        mm = pe.transpose(B.bank["xiT"][:, k * P:(k + 1) * P], xi[:, k * P:(k + 1) * P], ident)
                    mm.then_inc(p.done("xiT"), 1)

                def ab(t):
                    pe.wait_ge(*act.at("xiT", t))
                    pe.wait_ge(*B.free("a", t))
                    for k in range(KE):
                        pe.matmul(B.bank["a"][:, :], xiT[:, k, :], w_a[:, k, :], start=k == 0, stop=False)
                    pe.matmul(B.bank["a"][:, :], ones_r[:, :], a_bias_hi[:, :], start=False, stop=False)
                    pe.matmul(B.bank["a"][:, :], ones_r[:, :], a_bias_lo[:, :], start=False, stop=True)\
                      .then_inc(p.done("a"), 1)
                    pe.wait_ge(*B.free("bc", t))
                    for k in range(KE):
                        mm = pe.matmul(B.bank["bc"][:, 0:2 * NST], xiT[:, k, :], w_bc[:, k, :],
                                       start=k == 0, stop=k == KE - 1)
                    mm.then_inc(p.done("bc"), 1)

                def gt(t):
                    pe.wait_ge(*dve.at("Ct", t))
                    pe.wait_ge(*B.free("gt", t))
                    pe.transpose(B.bank["gt"][:, 0:P], Bt[:, :, :], ident)
                    pe.transpose(B.bank["gt"][:, P:2 * P], Ct[:, :, :], ident).then_inc(p.done("gt"), 1)

                def G(t):
                    pe.wait_ge(*act.at("BT", t))
                    pe.wait_ge(*dve.at("CD", t))
                    pe.wait_ge(*B.free("G", t))
                    pe.matmul(B.bank["G"][:, :], BTt[:, :], CD[:, :, :], start=True, stop=True)\
                      .then_inc(p.done("G"), 1)

                def E(t):
                    pe.wait_ge(*act.at("nl", t))
                    for l in range(NLV):
                        pe.wait_ge(*B.free(f"E{l}", t))
                        pe.matmul(B.bank[f"E{l}"][:, :], const("sums")[:, l * P:(l + 1) * P], nl[:, :],
                                  start=True, stop=True).then_inc(p.done(f"E{l}"), 1)

                def mix(levels):
                    def run(t):
                        for l in levels:
                            pe.wait_ge(*dve.at("Gm", t))
                            pe.wait_ge(*pool.at(f"u{l}", t))
                            pe.wait_ge(*B.free(f"m{l}", t))
                            pe.matmul(B.bank[f"m{l}"][:, :], Gm[:, l, :], u[l][:, :],
                                      start=True, stop=True).then_inc(p.done(f"m{l}"), 1)
                    return run

                def yT_(t):
                    pe.wait_ge(*pool.at("y", t))
                    pe.wait_ge(*B.free("yT", t))
                    for k in range(KE):
                        mm = pe.transpose(B.bank["yT"][:, k * P:(k + 1) * P], y[:, k * P:(k + 1) * P], ident)
                    mm.then_inc(p.done("yT"), 1)

                def out_(t):
                    pe.wait_ge(*act.at("yT", t))
                    pe.wait_ge(*B.free("out", t))
                    for k in range(KE):
                        mm = pe.matmul(B.bank["out"][:, 0:D], yT[:, k, :], w_out[:, k, :],
                                       start=k == 0, stop=k == KE - 1)
                    mm.then_inc(p.done("out"), 1)

                return {"b.xt": xt, "b.in": proj, "b.xiT": xiT_, "b.ab": ab, "b.gt": gt, "b.G": G, "b.E": E,
                        "b.m01": mix((0, 1)), "b.m23": mix((2, 3)), "b.yT": yT_, "b.out": out_}

            def experts():
                p, act, dve = C.pe, C.act, C.dve

                def ct(t):
                    pe.wait_ge(*dve.at("c", t))
                    pe.wait_ge(*C.free("ct", t))
                    for k in range(KD):
                        mm = pe.transpose(C.bank["ct"][:, k * P:(k + 1) * P], C.c[:, k * P:(k + 1) * P], ident)
                    mm.then_inc(p.done("ct"), 1)

                def lg(t):
                    pe.wait_ge(*act.at("cT", t))
                    pe.wait_ge(*C.free("lg", t))
                    for k in range(KD):
                        mm = pe.matmul(C.bank["lg"][:, 0:NE], cT[:, k, :], gate_w[:, k, :],
                                       start=k == 0, stop=k == KD - 1)
                    mm.then_inc(p.done("lg"), 1)

                def ex(t):
                    pe.wait_ge(*dve.at("oh", t))
                    pe.wait_ge(*C.free("oT", t))
                    pe.transpose(C.bank["oT"][0:NE, 0:P], oh[:, :], ident).then_inc(p.done("oT"), 1)
                    for n in range(NE // 2):
                        pe.wait_ge(*C.free(f"ex{n}", t))
                        for k in range(KD):
                            mm = pe.matmul(C.bank[f"ex{n}"][:, :], cT[:, k, :], w_e[:, k, 2 * n:2 * n + 2, :],
                                           start=k == 0, stop=k == KD - 1)
                        mm.then_inc(p.done(f"ex{n}"), 1)

                def eb(t):
                    pe.wait_ge(*act.at("oT", t))
                    pe.wait_ge(*C.free("eb", t))
                    pe.matmul(C.bank["eb"][:, 0:D], ohT[:, :], b_e[:, :], start=True, stop=True)\
                      .then_inc(p.done("eb"), 1)

                return {"c.ct": ct, "c.lg": lg, "c.ex": ex, "c.eb": eb}

            steps = attention(A, "a") | scan() | attention(C, "c") | experts()
            pe.wait_ge(ld_const, 16)
            pe.wait_ge(prep_a, 1)

            def setup_c():
                bank = banks["c"]
                pe.wait_ge(prep_nk, 1)
                pe.matmul(bank[0][:, 0:1], const("halves"), nk_sq[:, :], start=True, stop=True)\
                  .then_inc(prep_nk_pe, 1)
                for layer in range(2):
                    pe.wait_ge(*mlp_dve.at(f"s{layer}", 0))
                    src = mh[2] if layer == 0 else mh[5]
                    for k in range(KD):
                        mm = pe.transpose(bank[1][:, k * P:(k + 1) * P], src[:, k * P:(k + 1) * P], ident)
                    mm.then_inc(mlp_pe.done(f"T{layer}"), 1)
                    pe.wait_ge(*mlp_dve.at(f"T{layer}", 0))
                    w, n = (m_w1, D) if layer == 0 else (m_w2, H)
                    for k in range(KD):
                        mm = pe.matmul(bank[2][:, 0:n], mhT[:, k, :], w[:, k, :],
                                       start=k == 0, stop=k == KD - 1)
                    mm.then_inc(mlp_pe.done("h1" if layer == 0 else "pos"), 1)
                pe.wait_ge(*mlp_dve.at("pos", 0))
                pe.transpose(bank[1][0:H, 0:P], m_pos, ident).then_inc(mlp_pe.done("posT"), 1)

            def run(i, streams):
                if isinstance(i, int) and i == 1:
                    setup_c()
                    pe.wait_ge(prep_b, 1)
                if isinstance(i, int) and i == 2:
                    pe.wait_ge(prep_c, 1)
                in_order(steps, i, streams)

            tiles(pe, run)

        @block.scalar
        def _(act):
            def rstd(X, t, src, mark_in, mid, dst, mark_l, mark):
                act.wait_ge(*X.dve.at(mark_in, t))
                act.activation(mid[:, :], src[:, 1:2], ACT.Ln, bias=eps5[:, :]).then_inc(X.act.done(mark_l), 1)
                act.wait_ge(*X.act.at(mark_l, t))
                act.activation(dst[:, :], mid[:, :], ACT.Exp, scale=-0.5).then_inc(X.act.done(mark), 1)

            def attention(X, s):
                p, a, dve, pool = X.pe, X.act, X.dve, X.pool

                def st(t):
                    act.wait_ge(*dve.at("xn", t - 1))
                    rstd(X, t, X.mv, "mv", X.rstd_l, X.rstd, "rstd_l", "rstd")

                def xt(t):
                    act.wait_ge(*p.at("xt", t))
                    act.wait_ge(*p.at("q1", t - 1))
                    act.copy(X.xnT[:, :, :], X.bank["xt"][:, 0:D]).then_inc(a.done("xnT"), 1)

                def kv(t):
                    if s == "c":
                        act.wait_ge(*p.at("kv", t))
                        act.wait_ge(*p.at("ks", t - 1))
                        act.activation(ksq[:, :], X.bank["kv"][:, 0:P], ACT.Square).then_inc(a.done("ksq"), 1)

                def kn_(t):
                    act.wait_ge(*dve.at("ks", t))
                    act.activation(kr_l[:, :], kss[:, :], ACT.Ln, scale=L2_SCALE).then_inc(a.done("kr_l"), 1)
                    act.wait_ge(*a.at("kr_l", t))
                    act.wait_ge(*dve.at("kn", t - 1))
                    act.activation(kr[:, :], kr_l[:, :], ACT.Exp, scale=-0.5).then_inc(a.done("kr"), 1)

                def q(t):
                    for half in range(2):
                        act.wait_ge(*p.at(f"q{half}", t))
                        act.wait_ge(*p.at("S1", t - 1))
                        if s == "c":
                            act.wait_ge(*pool.at("qsq", t - 1))
                        act.copy(X.qT[:, 4 * half:4 * half + 4, :], X.bank[f"q{half}"][:, :])\
                           .then_inc(a.done(f"q{half}"), 1)

                def qn(t):
                    act.wait_ge(*dve.at("qs", t))
                    act.activation(qr_l[:, :], qss[:, :], ACT.Ln, scale=L2_SCALE).then_inc(a.done("qr_l"), 1)
                    act.wait_ge(*a.at("qr_l", t))
                    act.wait_ge(*dve.at("S1", t - 1))
                    act.activation(qr[:, :], qr_l[:, :], ACT.Exp, scale=-0.5).then_inc(a.done("qr"), 1)

                def sm(t):
                    act.wait_ge(*dve.at("mx0", t))
                    act.wait_ge(*dve.at("den", t - 1))
                    act.activation(X.expm[:, :], X.mx0[:, :], ACT.Exp, scale=-1.0).then_inc(a.done("expm"), 1)
                    act.wait_ge(*dve.at("sub", t))
                    act.activation(X.prob[:, :, :], X.prob[:, :, :], ACT.Exp).then_inc(a.done("prob"), 1)

                def PT(t):
                    for half in range(2):
                        act.wait_ge(*p.at(f"PT{half}", t))
                        act.wait_ge(*p.at("O1", t - 1))
                        act.copy(X.PT[:, 4 * half:4 * half + 4, :], X.bank[f"PT{half}"][:, :])\
                           .then_inc(a.done(f"PT{half}"), 1)

                def PV(t):
                    for b in range(BT):
                        act.wait_ge(*p.at(f"O{b}", t))
                        act.wait_ge(*p.at("W", t - 1))
                        act.activation(X.OT[:, :, b * S:(b + 1) * S],
                                       X.bank[f"O{b}"][:, :].rearrange("p (h i) -> p h i", h=HP),
                                       ACT.Identity, bias=nv_col[:, :]).then_inc(a.done(f"O{b}"), 1)

                def fin(t):
                    act.wait_ge(*dve.at("cn", t - 1))
                    rstd(X, t, X.mv2, "mv2", X.rstd2_l, X.rstd2, "rstd2_l", "rstd2")

                steps = {f"{s}.st": st, f"{s}.xt": xt, f"{s}.kv": kv, f"{s}.q": q, f"{s}.sm": sm, f"{s}.PT": PT,
                         f"{s}.PV": PV, f"{s}.fin": fin}
                if s == "c":
                    steps |= {"c.kn": kn_, "c.qn": qn}
                return steps

            def scan():
                p, a, dve, pool = B.pe, B.act, B.dve, B.pool

                def rms(t):
                    act.wait_ge(*A.dve.at("c", t))
                    act.wait_ge(*p.at("z", t - 1))
                    act.activation(ynT[:, :, :], A.c[:, :], ACT.Square, accum_out=ss[:, :])\
                       .then_inc(a.done("ss"), 1)
                    act.wait_ge(*a.at("ss", t))
                    act.activation(r_l[:, :], ss[:, :], ACT.Ln, scale=1.0 / D, bias=eps6[:, :])\
                       .then_inc(a.done("r_l"), 1)
                    act.wait_ge(*a.at("r_l", t))
                    act.wait_ge(*dve.at("xn", t - 1))
                    act.activation(r_ms[:, :], r_l[:, :], ACT.Exp, scale=-0.5).then_inc(a.done("r"), 1)

                def xt(t):
                    act.wait_ge(*p.at("xt", t))
                    act.wait_ge(*p.at("z", t - 1))
                    act.copy(ynT[:, :, :], B.bank["xt"][:, 0:D]).then_inc(a.done("xnT"), 1)

                def proj(t):
                    act.wait_ge(*p.at("x", t))
                    act.activation(xe[:, :], B.bank["x"][:, :], ACT.Exp, scale=-1.0).then_inc(a.done("xe"), 1)
                    act.wait_ge(*p.at("z", t))
                    act.activation(ze[:, :], B.bank["z"][:, :], ACT.Exp, scale=-1.0).then_inc(a.done("ze"), 1)

                def silu(t):
                    act.wait_ge(*dve.at("xg", t))
                    act.activation(xe[:, :], xe[:, :], ACT.Ln).then_inc(a.done("xl"), 1)
                    act.wait_ge(*a.at("xl", t))
                    act.activation(xs[:, :], xe[:, :], ACT.Exp, scale=-1.0).then_inc(a.done("xs"), 1)
                    act.wait_ge(*dve.at("zg", t))
                    act.activation(ze[:, :], ze[:, :], ACT.Ln).then_inc(a.done("zl"), 1)
                    act.wait_ge(*a.at("zl", t))
                    act.activation(zs[:, :], ze[:, :], ACT.Exp, scale=-1.0).then_inc(a.done("zs"), 1)

                def xiT_(t):
                    act.wait_ge(*p.at("xiT", t))
                    act.wait_ge(*p.at("bc", t - 1))
                    act.copy(xiT[:, :, :], B.bank["xiT"][:, :]).then_inc(a.done("xiT"), 1)

                def ab(t):
                    act.wait_ge(*p.at("a", t))
                    act.activation(ae[:, :], B.bank["a"][:, :], ACT.Exp, scale=-1.0).then_inc(a.done("ae"), 1)
                    act.wait_ge(*dve.at("ag", t))
                    act.wait_ge(*p.at("E3", t - 1))
                    act.activation(nl[:, :], ae[:, :], ACT.Ln).then_inc(a.done("nl"), 1)

                def gt(t):
                    act.wait_ge(*p.at("gt", t))
                    act.wait_ge(*p.at("G", t - 1))
                    act.copy(BTt[:, :], B.bank["gt"][:, 0:P]).then_inc(a.done("BT"), 1)

                def E(t):
                    act.wait_ge(*p.at("E0", t))
                    act.wait_ge(*dve.at("t0", t - 1))
                    act.activation(Ef[0][:, :], B.bank["E0"][:, :], ACT.Exp, scale=-1.0).then_inc(a.done("E0"), 1)
                    act.wait_ge(*pool.at("u0", t - 1))
                    act.activation(E0u[:, :], B.bank["E0"][:, :], ACT.Exp).then_inc(a.done("E0u"), 1)
                    for l in range(1, NLV):
                        act.wait_ge(*p.at(f"E{l}", t))
                        act.wait_ge(*dve.at(f"t{l}", t - 1))
                        act.wait_ge(*pool.at(f"u{l}", t - 1))
                        act.activation(Ef[l][:, :], B.bank[f"E{l}"][:, :], ACT.Exp, scale=-1.0)\
                           .then_inc(a.done(f"E{l}"), 1)

                def yT_(t):
                    act.wait_ge(*p.at("yT", t))
                    act.wait_ge(*p.at("out", t - 1))
                    act.copy(yT[:, :, :], B.bank["yT"][:, :]).then_inc(a.done("yT"), 1)

                return {"b.rms": rms, "b.xt": xt, "b.in": proj, "b.silu": silu, "b.xiT": xiT_, "b.ab": ab,
                        "b.gt": gt, "b.E": E, "b.yT": yT_}

            def experts():
                p, a, dve = C.pe, C.act, C.dve

                def ct(t):
                    act.wait_ge(*p.at("ct", t))
                    act.wait_ge(*p.at("ex3", t - 1))
                    act.copy(cT[:, :, :], C.bank["ct"][:, 0:D]).then_inc(a.done("cT"), 1)

                def lg(t):
                    act.wait_ge(*dve.at("ld", t))
                    act.wait_ge(*dve.at("eq", t - 1))
                    act.activation(le[:, :], ld[:, :], ACT.Exp).then_inc(a.done("le"), 1)

                def ex(t):
                    act.wait_ge(*p.at("oT", t))
                    act.wait_ge(*p.at("eb", t - 1))
                    act.copy(ohT[:, :], C.bank["oT"][0:NE, 0:P]).then_inc(a.done("oT"), 1)

                return {"c.ct": ct, "c.lg": lg, "c.ex": ex}

            steps = attention(A, "a") | scan() | attention(C, "c") | experts()
            act.preload_act_table_set("natural_log_exp_and_others")

            def setup_lam():
                act.wait_ge(ld_b, n_ld[ld_b.name])
                act.activation(lam_e[:, :], a_base[:, :], ACT.Exp, scale=-1.0).then_inc(prep_lam, 1)
                act.wait_ge(prep_lam_g, 1)
                act.activation(lam[:, :], lam_g[:, :], ACT.Ln).then_inc(prep_lam, 1)
                act.wait_ge(prep_lam, 2)
                for l in range(NLV):
                    act.activation(lam_b[:, l, :], lam[:, :], ACT.Exp, scale=const("neg_count_b")[:, l:l + 1])\
                       .then_inc(prep_lam, 1)
                    act.activation(lam_c[:, l, :], lam[:, :], ACT.Exp, scale=const("neg_count_c")[:, l:l + 1])\
                       .then_inc(prep_lam, 1)

            def setup_c():
                act.wait_ge(prep_nk, 2)
                act.activation(nk_l[:, :], nk_ss[:, :], ACT.Ln, scale=L2_SCALE).then_inc(prep_nk_act, 1)
                act.wait_ge(prep_nk_act, 1)
                act.activation(nk_r[:, :], nk_l[:, :], ACT.Exp, scale=-0.5).then_inc(prep_nk_act, 1)
                for layer in range(2):
                    act.wait_ge(*mlp_dve.at(f"mv{layer}", 0))
                    act.activation(C.rstd_l[:, :], C.mv[:, 1:2], ACT.Ln, bias=eps5[:, :])\
                       .then_inc(mlp_act.done(f"rl{layer}"), 1)
                    act.wait_ge(*mlp_act.at(f"rl{layer}", 0))
                    act.activation(C.rstd[:, :], C.rstd_l[:, :], ACT.Exp, scale=-0.5)\
                       .then_inc(mlp_act.done(f"r{layer}"), 1)
                    v = mh[1] if layer == 0 else mh[4]
                    act.wait_ge(*mlp_dve.at(f"v{layer}", 0))
                    act.activation(mh[3], v, ACT.Exp, scale=-1.0).then_inc(mlp_act.done(f"e{layer}"), 1)
                    act.wait_ge(*mlp_dve.at(f"e{layer}", 0))
                    act.activation(mh[3], mh[3], ACT.Ln).then_inc(mlp_act.done(f"l{layer}"), 1)
                    act.wait_ge(*mlp_act.at(f"l{layer}", 0))
                    act.activation(mh[3], mh[3], ACT.Exp, scale=-1.0).then_inc(mlp_act.done(f"s{layer}"), 1)

            def run(i, streams):
                if isinstance(i, int) and i == 0:
                    act.wait_ge(ld_a, n_ld[ld_a.name])
                    act.wait_ge(prep_a, 1)
                if isinstance(i, int) and i == 1:
                    setup_lam()
                    setup_c()
                in_order(steps, i, streams)

            tiles(act, run)

        @block.vector
        def _(dve):
            def stats(X, t, src, st, mv, mark_st, mark_mv):
                dve.bn_stats(st[:, :], src).then_inc(X.dve.done(mark_st), 1)
                dve.wait_ge(*X.dve.at(mark_st, t))
                dve.memset(wait_carrier[:, :], 0.0)
                dve.bn_aggr(mv[:, :], st[:, :]).then_inc(X.dve.done(mark_mv), 1)

            def attention(X, s):
                p, act, d, pool = X.pe, X.act, X.dve, X.pool

                def st(t):
                    if s == "a":
                        dve.wait_ge(x_loaded, 16 * (t + 1))
                    else:
                        dve.wait_ge(*B.dve.at("x1", t))
                        dve.tensor_copy(X.xin[:, :], x1[:, :]).then_inc(d.done("x1c"), 1)
                        dve.wait_ge(*d.at("x1c", t))
                    stats(X, t, X.xin[:, :], X.st, X.mv, "st", "mv")

                def xn(t):
                    dve.wait_ge(*act.at("rstd", t))
                    dve.wait_ge(*p.at("xt", t - 1))
                    dve.tensor_scalar(X.xn[:, :], X.xin[:, :], X.mv[:, 0:1], X.rstd[:, :],
                                      ALU.subtract, ALU.mult).then_inc(d.done("xn"), 1)

                def kv(t):
                    dve.wait_ge(*p.at("kv", t))
                    bank = X.bank["kv"]
                    if s == "a":
                        dve.wait_ge(*p.at("S1", t - 1))
                        for half in range(2):
                            part = slice(half * DH, (half + 1) * DH)
                            dve.tensor_scalar(X.K[part, :, half * S:(half + 1) * S],
                                              bank[part, 0:P].rearrange("p (b j) -> p b j", b=BT),
                                              nk_col[part, :], None, ALU.subtract)\
                               .then_inc(d.done(f"K{half}"), 1)
                        values(t)

                def values(t):
                    bank = X.bank["kv"]
                    dve.wait_ge(*p.at("O1", t - 1))
                    for half in range(2):
                        part = slice(half * S, (half + 1) * S)
                        dve.tensor_tensor(X.V[part, :, half * DH:(half + 1) * DH],
                                          bank[part, P:2 * P].rearrange("p (b n) -> p b n", b=BT),
                                          nv_row[part, :].unsqueeze(1).broadcast_to([S, BT, DH]),
                                          ALU.subtract).then_inc(d.done(f"V{half}"), 1)

                def kn_(t):
                    dve.wait_ge(*p.at("ks", t))
                    dve.tensor_scalar(kss[:, :], X.bank["ks"][:, 0:P], 1.0e-24, None, ALU.max)\
                       .then_inc(d.done("ks"), 1)
                    dve.wait_ge(*act.at("kr", t))
                    dve.tensor_tensor(kn[:, :], X.bank["kv"][:, 0:P], kr[:, :], ALU.mult).then_inc(d.done("kn"), 1)
                    dve.wait_ge(*d.at("kn", t))
                    dve.wait_ge(*p.at("S1", t - 1))
                    for half in range(2):
                        part = slice(half * DH, (half + 1) * DH)
                        dve.tensor_scalar(X.K[part, :, half * S:(half + 1) * S],
                                          kn[part, :].rearrange("p (b j) -> p b j", b=BT),
                                          kq[part, :], nk_n[part, :], ALU.mult, ALU.subtract)\
                           .then_inc(d.done(f"K{half}"), 1)
                    values(t)

                def qn(t):
                    dve.wait_ge(*p.at("qs", t))
                    dve.tensor_scalar(qss[:, :], X.bank["qs"][:, 0:H], 1.0e-24, None, ALU.max)\
                       .then_inc(d.done("qs"), 1)

                def scores(t):
                    for half in range(2):
                        heads = slice(8 * half, 8 * half + 8)
                        dve.wait_ge(*p.at(f"S{half}", t))
                        dve.wait_ge(*p.at("PT1", t - 1))
                        src = X.bank[f"S{half}"][:, :].rearrange("p (h j) -> p h j", h=8)
                        if s == "a":
                            dve.wait_ge(*pool.at("biasm", t))
                            dve.tensor_tensor(X.prob[:, heads, :], src, X.biasm[:, heads, :], ALU.add)\
                               .then_inc(d.done(f"S{half}"), 1)
                        else:
                            dve.wait_ge(*act.at("qr", t))
                            dve.tensor_tensor(X.prob[:, heads, :], src,
                                              qr[:, heads].unsqueeze(2).broadcast_to([P, 8, S]), ALU.mult)\
                               .then_inc(d.done(f"S{half}"), 1)

                def sm(t):
                    if s == "a":
                        dve.wait_ge(*d.at("S1", t))
                    else:
                        dve.wait_ge(*pool.at("addb", t))
                    dve.tensor_reduce(X.mx[:, :], X.prob[:, :, :], AX_X, ALU.max).then_inc(d.done("mx"), 1)
                    dve.wait_ge(*d.at("mx", t))
                    dve.tensor_scalar(X.mx0[:, :], X.mx[:, :], 0.0, None, ALU.max).then_inc(d.done("mx0"), 1)
                    dve.wait_ge(*d.at("mx0", t))
                    dve.tensor_tensor(X.prob[:, :, :], X.prob[:, :, :],
                                      X.mx0[:, :].unsqueeze(2).broadcast_to([P, H, S]), ALU.subtract)\
                       .then_inc(d.done("sub"), 1)

                def norm(t):
                    dve.wait_ge(*act.at("prob", t))
                    dve.tensor_reduce(X.sum[:, :], X.prob[:, :, :], AX_X, ALU.add).then_inc(d.done("sum"), 1)
                    dve.wait_ge(*d.at("sum", t))
                    dve.tensor_tensor(X.den[:, :], X.sum[:, :], X.expm[:, :], ALU.add).then_inc(d.done("den"), 1)
                    dve.wait_ge(*d.at("den", t))
                    dve.wait_ge(*pool.at("norm", t - 1))
                    dve.reciprocal(X.rden[:, :], X.den[:, :]).then_inc(d.done("rden"), 1)

                def fin(t):
                    dve.wait_ge(*p.at("W", t))
                    stats(X, t, X.bank["W"][:, 0:D], X.st2, X.mv2, "st2", "mv2")
                    dve.wait_ge(*act.at("rstd2", t))
                    dve.tensor_scalar(X.cn[:, :], X.bank["W"][:, 0:D], X.mv2[:, 0:1], X.rstd2[:, :],
                                      ALU.subtract, ALU.mult).then_inc(d.done("cn"), 1)
                    dve.wait_ge(*d.at("cn", t))
                    if s == "a":
                        dve.wait_ge(*B.act.at("ss", t - 1))
                        dve.wait_ge(*B.pool.at("resid", t - 1))
                        dve.wait_ge(*B.dve.at("xn", t - 1))
                    else:
                        dve.wait_ge(*p.at("ct", t - 1))
                    dve.tensor_tensor(X.c[:, :], X.cn[:, :], X.g_out[:, :], ALU.mult).then_inc(d.done("c"), 1)

                steps = {f"{s}.st": st, f"{s}.xn": xn, f"{s}.kv": kv, f"{s}.S": scores, f"{s}.sm": sm,
                         f"{s}.norm": norm, f"{s}.fin": fin}
                if s == "c":
                    steps |= {"c.kn": kn_, "c.qn": qn}
                return steps

            def scan():
                p, act, d, pool = B.pe, B.act, B.dve, B.pool

                def xn(t):
                    dve.wait_ge(*act.at("r", t))
                    dve.wait_ge(*p.at("xt", t - 1))
                    dve.tensor_scalar(yn[:, :], A.c[:, :], r_ms[:, :], None, ALU.mult).then_inc(d.done("xn"), 1)

                def silu(t):
                    dve.wait_ge(*act.at("xe", t))
                    dve.tensor_scalar(xe[:, :], xe[:, :], GUARD, 1.0, ALU.min, ALU.add).then_inc(d.done("xg"), 1)
                    dve.wait_ge(*act.at("ze", t))
                    dve.tensor_scalar(ze[:, :], ze[:, :], GUARD, 1.0, ALU.min, ALU.add).then_inc(d.done("zg"), 1)
                    dve.wait_ge(*act.at("xs", t))
                    dve.wait_ge(*p.at("xiT", t - 1))
                    dve.wait_ge(*pool.at("u3", t - 1))
                    dve.tensor_tensor(xi[:, :], B.bank["x"][:, :], xs[:, :], ALU.mult).then_inc(d.done("xi"), 1)
                    dve.wait_ge(*act.at("zs", t))
                    dve.wait_ge(*pool.at("y", t - 1))
                    dve.tensor_tensor(zi[:, :], B.bank["z"][:, :], zs[:, :], ALU.mult).then_inc(d.done("zi"), 1)

                def ab(t):
                    dve.wait_ge(*act.at("ae", t))
                    dve.tensor_scalar(ae[:, :], ae[:, :], float(np.exp(DECAY_FLOOR)), 1.0, ALU.min, ALU.add)\
                       .then_inc(d.done("ag"), 1)
                    dve.wait_ge(*p.at("bc", t))
                    dve.wait_ge(*p.at("gt", t - 1))
                    for n, (dst, table, mark) in enumerate(((Bt, lam_b, "Bt"), (Ct, lam_c, "Ct"))):
                        src = B.bank["bc"][:, n * NST:(n + 1) * NST].unsqueeze(1).broadcast_to([P, NLV, NST])
                        dve.tensor_tensor(dst[:, :, 0:NST], src, table[:, :, :], ALU.mult)\
                           .then_inc(d.done(mark), 1)

                def gt(t):
                    dve.wait_ge(*act.at("BT", t))
                    dve.wait_ge(*p.at("G", t - 1))
                    dve.tensor_tensor(CD[:, :, :],
                                      B.bank["gt"][:, P:2 * P].unsqueeze(1).broadcast_to([P, NLV, P]),
                                      const("level_rows").unsqueeze(2).broadcast_to([P, NLV, P]), ALU.mult)\
                       .then_inc(d.done("CD"), 1)

                def G(t):
                    dve.wait_ge(*p.at("G", t))
                    dve.wait_ge(*p.at("m3", t - 1))
                    dve.tensor_tensor(Gm[:, :, :], B.bank["G"][:, :].rearrange("p (l n) -> p l n", l=NLV),
                                      const("scan_mask").rearrange("p (l n) -> p l n", l=NLV), ALU.mult)\
                       .then_inc(d.done("Gm"), 1)

                def mix(levels):
                    def run(t):
                        for l in levels:
                            dve.wait_ge(*p.at(f"m{l}", t))
                            dve.wait_ge(*act.at(f"E{l}", t))
                            dve.wait_ge(*pool.at(f"y{l}", t - 1))
                            dve.tensor_tensor(tm[l][:, :], B.bank[f"m{l}"][:, :], Ef[l][:, :], ALU.mult)\
                               .then_inc(d.done(f"t{l}"), 1)
                    return run

                def out_(t):
                    dve.wait_ge(*p.at("out", t))
                    dve.wait_ge(*pool.at("resid", t))
                    dve.wait_ge(*C.dve.at("x1c", t - 1))
                    dve.tensor_tensor(x1[:, :], B.bank["out"][:, 0:D], resid[:, :], ALU.add)\
                       .then_inc(d.done("x1"), 1)

                return {"b.xn": xn, "b.silu": silu, "b.ab": ab, "b.gt": gt, "b.G": G, "b.m01": mix((0, 1)),
                        "b.m23": mix((2, 3)), "b.out": out_}

            def experts():
                p, act, d = C.pe, C.act, C.dve

                def lg(t):
                    dve.wait_ge(*p.at("lg", t))
                    dve.tensor_tensor(lb[:, :], C.bank["lg"][:, 0:NE], gate_b[:, :], ALU.add)\
                       .then_inc(d.done("lb"), 1)
                    dve.wait_ge(*d.at("lb", t))
                    dve.tensor_reduce(lm[:, :], lb[:, :], AX_X, ALU.max).then_inc(d.done("lm"), 1)
                    dve.wait_ge(*d.at("lm", t))
                    dve.tensor_scalar(ld[:, :], lb[:, :], lm[:, :], None, ALU.subtract).then_inc(d.done("ld"), 1)
                    dve.wait_ge(*act.at("le", t))
                    dve.scalar_tensor_tensor(eq[:, :], le[:, :], 1.0, const("rank"), ALU.is_ge, ALU.mult)\
                       .then_inc(d.done("eq"), 1)
                    dve.wait_ge(*d.at("eq", t))
                    dve.tensor_reduce(em[:, :], eq[:, :], AX_X, ALU.max).then_inc(d.done("em"), 1)
                    dve.wait_ge(*d.at("em", t))
                    dve.wait_ge(*p.at("oT", t - 1))
                    dve.tensor_scalar(oh[:, :], eq[:, :], em[:, :], None, ALU.is_equal).then_inc(d.done("oh"), 1)

                def ex(t):
                    dve.wait_ge(*d.at("oh", t))
                    for e in range(NE):
                        if e % 2 == 0:
                            dve.wait_ge(*p.at(f"ex{e // 2}", t))
                        if e:
                            dve.wait_ge(*d.at(f"ac{e - 1}", t))
                        if e == 0:
                            dve.wait_ge(out_stored, 16 * t)
                        src = C.xin if e == 0 else (acc2 if e % 2 == 0 else acc)
                        dst = acc if e % 2 == 0 else acc2
                        dve.scalar_tensor_tensor(dst[:, :], C.bank[f"ex{e // 2}"][:, (e % 2) * D:(e % 2 + 1) * D],
                                                 oh[:, e:e + 1], src[:, :], ALU.mult, ALU.add)\
                           .then_inc(d.done(f"ac{e}"), 1)

                def eb(t):
                    dve.wait_ge(*p.at("eb", t))
                    dve.wait_ge(*d.at(f"ac{NE - 1}", t))
                    dve.tensor_tensor(yout[:, :], C.bank["eb"][:, 0:D], acc2[:, :], ALU.add)\
                       .then_inc(d.done("out"), 1)

                return {"c.lg": lg, "c.ex": ex, "c.eb": eb}

            steps = attention(A, "a") | scan() | attention(C, "c") | experts()

            def setup_weights(X, prep, scale):
                for k in range(KD):
                    dve.tensor_scalar(X.wq[:, k, :], X.wq[:, k, :], X.g[:, k:k + 1], scale, ALU.mult, ALU.mult)
                    for half in range(2):
                        dve.tensor_scalar(X.wkk[:, k, half, :], X.wkv[:, k, 0:DH], X.g[:, k:k + 1], None, ALU.mult)
                    dve.tensor_scalar(X.wv[:, k, :], X.wkv[:, k, DH:], X.g[:, k:k + 1], None, ALU.mult)

            def setup_a():
                dve.memset(eps5[:, :], 1.0e-5)
                dve.memset(eps6[:, :], 1.0e-6)
                dve.memset(A.K[:, :, :], 0.0)
                dve.memset(A.V[:, :, :], 0.0)
                dve.memset(C.K[:, :, :], 0.0)
                dve.memset(C.V[:, :, :], 0.0)
                dve.memset(Bt[:, :, :], 0.0)
                dve.memset(Ct[:, :, :], 0.0)
                dve.memset(ones_f[:, :], 1.0)
                dve.wait_ge(ld_const, 16)
                dve.wait_ge(ld_a, n_ld[ld_a.name])
                setup_weights(A, prep_a, float(DH) ** -0.5)
                dve.tensor_scalar(A.mask[:, :, :], A.mask_u8[:, :, :], -NEG, NEG, ALU.mult, ALU.add)\
                   .then_inc(prep_a, 1)
                dve.wait_ge(prep_a, 1)

            def setup_b():
                dve.wait_ge(ld_b, n_ld[ld_b.name])
                for k in range(KD):
                    dve.tensor_scalar(w_in[:, k, :], w_in[:, k, :], norm_w[:, k:k + 1], None, ALU.mult)
                dve.wait_ge(prep_lam, 1)
                dve.tensor_scalar(lam_g[:, :], lam_e[:, :], float(np.exp(LAMBDA_FLOOR)), 1.0, ALU.min, ALU.add)\
                   .then_inc(prep_lam_g, 1)
                dve.tensor_copy(ones_r[:, :], ones_f[:, :])
                dve.tensor_copy(a_bias_hi[:, :], a_bias[:, :]).then_inc(prep_lam_g, 1)
                dve.wait_ge(prep_lam_g, 2)
                dve.tensor_tensor(a_bias_lo[:, :], a_bias[:, :], a_bias_hi[:, :].bitcast(F32), ALU.subtract)\
                   .then_inc(prep_b, 1)
                dve.wait_ge(prep_lam, 2 + 2 * NLV)

            def setup_c():
                dve.wait_ge(ld_c, n_ld[ld_c.name])
                dve.tensor_tensor(nk_sq[:, :], nk_col[:, :], nk_col[:, :], ALU.mult).then_inc(prep_nk, 1)
                setup_weights(C, prep_c, 1.0)
                dve.tensor_scalar(C.mask[:, :, :], C.mask_u8[:, :, :], -NEG, NEG, ALU.mult, ALU.add)
                dve.wait_ge(prep_nk_pe, 1)
                dve.tensor_scalar(nk_ss[:, :], banks["c"][0][:, 0:1], 1.0e-24, None, ALU.max).then_inc(prep_nk, 1)
                dve.tensor_scalar(kq[:, :], q_scale[:, :], k_scale[:, :], 8.0 * L2_SCALE, ALU.mult, ALU.mult)\
                   .then_inc(prep_nk, 1)
                dve.wait_ge(prep_nk, 3)
                dve.wait_ge(prep_nk_act, 2)
                dve.tensor_scalar(nk_n[:, :], nk_col[:, :], nk_r[:, :], kq[:, :], ALU.mult, ALU.mult)\
                   .then_inc(prep_c, 1)
                dve.wait_ge(prep_c, 1)

            def setup_mlp():
                d, bank = mlp_dve, banks["c"]
                dve.wait_ge(ld_mlp, n_ld[ld_mlp.name])
                dve.scalar_tensor_tensor(mh[0], m_w0, const("distance"), m_b0, ALU.mult, ALU.add)\
                   .then_inc(d.done("h0"), 1)
                for layer, (nrm, res, gain) in enumerate(((mh[1], mh[2], m_g0), (mh[4], mh[5], m_g1))):
                    dve.wait_ge(*d.at(f"h{layer}", 0))
                    dve.bn_stats(C.st[:, :], mh[0]).then_inc(d.done(f"st{layer}"), 1)
                    dve.wait_ge(*d.at(f"st{layer}", 0))
                    dve.bn_aggr(C.mv[:, :], C.st[:, :]).then_inc(d.done(f"mv{layer}"), 1)
                    dve.wait_ge(*mlp_act.at(f"r{layer}", 0))
                    dve.tensor_scalar(nrm, mh[0], C.mv[:, 0:1], C.rstd[:, :], ALU.subtract, ALU.mult)\
                       .then_inc(d.done(f"n{layer}"), 1)
                    dve.wait_ge(*d.at(f"n{layer}", 0))
                    dve.tensor_tensor(nrm, nrm, gain, ALU.mult).then_inc(d.done(f"v{layer}"), 1)
                    dve.wait_ge(*mlp_act.at(f"e{layer}", 0))
                    dve.tensor_scalar(mh[3], mh[3], GUARD, 1.0, ALU.min, ALU.add).then_inc(d.done(f"e{layer}"), 1)
                    dve.wait_ge(*mlp_act.at(f"s{layer}", 0))
                    dve.tensor_tensor(res, nrm, mh[3], ALU.mult).then_inc(d.done(f"s{layer}"), 1)
                    dve.wait_ge(*mlp_pe.at(f"T{layer}", 0))
                    dve.tensor_copy(mhT, bank[1][:, 0:D].rearrange("p (k n) -> p k n", k=KD))\
                       .then_inc(d.done(f"T{layer}"), 1)
                    if layer == 0:
                        dve.wait_ge(*mlp_pe.at("h1", 0))
                        dve.tensor_tensor(mh[0], bank[2][:, 0:D], m_b1, ALU.add).then_inc(d.done("h1"), 1)
                dve.wait_ge(*mlp_pe.at("pos", 0))
                dve.tensor_tensor(m_pos, bank[2][:, 0:H], m_b2, ALU.add).then_inc(d.done("pos"), 1)
                dve.wait_ge(*mlp_pe.at("posT", 0))
                dve.tensor_copy(m_posT, bank[1][0:H, 0:P]).then_inc(d.done("posT"), 1)

            def run(i, streams):
                if isinstance(i, int) and i == 0:
                    setup_a()
                if isinstance(i, int) and i == 1:
                    setup_b()
                    setup_c()
                    setup_mlp()
                in_order(steps, i, streams)

            tiles(dve, run)

        @block.gpsimd
        def _(pool):
            def attention(X, s):
                p, act, dve, g = X.pe, X.act, X.dve, X.pool

                def biasm(t):
                    if s == "a":
                        pool.wait_ge(*dve.at("S1", t - 1))
                    else:
                        pool.wait_ge(*g.at("addb", t - 1))
                    pool.tensor_tensor(X.biasm[:, :, :], X.bias[:, :, :],
                                       X.mask[:, t, :].unsqueeze(1).broadcast_to([P, H, S]), ALU.add)\
                        .then_inc(g.done("biasm"), 1)

                def q(t):
                    pool.wait_ge(*act.at("q1", t))
                    pool.wait_ge(*p.at("O1", t - 1))
                    pool.tensor_tensor(qsq[:, :, :], X.qT[:, :, :], X.qT[:, :, :], ALU.mult)\
                        .then_inc(g.done("qsq"), 1)

                def scores(t):
                    pool.wait_ge(*g.at("biasm", t))
                    pool.wait_ge(*dve.at("S1", t))
                    pool.tensor_tensor(X.prob[:, :, :], X.prob[:, :, :], X.biasm[:, :, :], ALU.add)\
                        .then_inc(g.done("addb"), 1)

                def norm(t):
                    pool.wait_ge(*dve.at("rden", t))
                    pool.tensor_tensor(X.prob[:, :, :], X.prob[:, :, :],
                                       X.rden[:, :].unsqueeze(2).broadcast_to([P, H, S]), ALU.mult)\
                        .then_inc(g.done("norm"), 1)

                steps = {f"{s}.st": biasm, f"{s}.norm": norm}
                if s == "c":
                    steps |= {"c.q": q, "c.S": scores}
                return steps

            def scan():
                p, act, dve, g = B.pe, B.act, B.dve, B.pool

                def rms(t):
                    pool.wait_ge(*A.dve.at("c", t))
                    pool.wait_ge(xres_loaded, 16 * (t + 1))
                    pool.wait_ge(*dve.at("x1", t - 1))
                    pool.tensor_tensor(resid[:, :], xres[:, :], A.c[:, :], ALU.add).then_inc(g.done("resid"), 1)

                def E(t):
                    pool.wait_ge(*dve.at("xi", t))
                    pool.tensor_tensor(y[:, :], xi[:, :], d_row[:, :], ALU.mult).then_inc(g.done("dx"), 1)
                    for l in range(NLV):
                        pool.wait_ge(*act.at("E0u" if l == 0 else f"E{l}", t))
                        pool.wait_ge(*p.at(f"m{l}", t - 1))
                        pool.tensor_tensor(u[l][:, :], xi[:, :], (E0u if l == 0 else Ef[l])[:, :], ALU.mult)\
                            .then_inc(g.done(f"u{l}"), 1)

                def mix(levels):
                    def run(t):
                        for l in levels:
                            pool.wait_ge(*g.at("dx" if l == 0 else f"y{l - 1}", t))
                            pool.wait_ge(*dve.at(f"t{l}", t))
                            pool.tensor_tensor(y[:, :], y[:, :], tm[l][:, :], ALU.add)\
                                .then_inc(g.done(f"y{l}"), 1)
                    return run

                def yT_(t):
                    pool.wait_ge(*g.at(f"y{NLV - 1}", t))
                    pool.wait_ge(*dve.at("zi", t))
                    pool.tensor_tensor(y[:, :], y[:, :], zi[:, :], ALU.mult).then_inc(g.done("y"), 1)

                def E_guarded(t):
                    pool.wait_ge(*p.at("yT", t - 1))
                    E(t)

                return {"b.rms": rms, "b.E": E_guarded, "b.m01": mix((0, 1)), "b.m23": mix((2, 3)), "b.yT": yT_}

            def fold_bias(X):
                done = sem("bias_folded_" + ("a" if X is A else "c"))
                pool.tensor_tensor(X.bias[:, :, :], X.bias[:, :, :],
                                   X.null_bias[:, :].unsqueeze(2).broadcast_to([P, H, S]), ALU.subtract)\
                    .then_inc(done, 1)
                pool.wait_ge(done, 1)
                pool.tensor_tensor(X.bias[:, :, :], X.bias[:, :, :],
                                   const("causal").unsqueeze(1).broadcast_to([P, H, S]), ALU.add)\
                    .then_inc(done, 1)
                pool.wait_ge(done, 2)

            steps = attention(A, "a") | scan() | attention(C, "c")

            def run(i, streams):
                if isinstance(i, int) and i == 0:
                    pool.wait_ge(ld_const, 16)
                    pool.wait_ge(ld_a, n_ld[ld_a.name])
                    fold_bias(A)
                    pool.wait_ge(prep_a, 1)
                if isinstance(i, int) and i == 1:
                    pool.wait_ge(ld_b, n_ld[ld_b.name])
                if isinstance(i, int) and i == 2:
                    pool.wait_ge(ld_c, n_ld[ld_c.name])
                    pool.wait_ge(mlp_dma, 16 + 16 * BT)
                    fold_bias(C)
                in_order(steps, i, streams)

            tiles(pool, run)


_INS = ["cond_64", "fside_16xSxS_0", "mask_BxS_bk0", "mask_BxS_bf1",
        "L0_cond_g_in", "L0_cond_null_attn_bias", "L0_cond_Wq", "L0_cond_Wkv", "L0_cond_Wo", "L0_cond_g_out",
        "L0_attn_norm_w", "L0_attn_in_proj_w", "L0_attn_A_proj_w", "L0_attn_A_proj_b", "L0_attn_A_base",
        "L0_attn_B_proj_w", "L0_attn_C_proj_w", "L0_attn_D", "L0_attn_out_proj_w",
        "L0_cond2_g_norm", "L0_cond2_Wq", "L0_cond2_Wkv", "L0_cond2_q_scale", "L0_cond2_k_scale",
        "L0_cond2_null_attn_bias", "L0_cond2_w0", "L0_cond2_b0", "L0_cond2_g0", "L0_cond2_w1", "L0_cond2_b1",
        "L0_cond2_g1", "L0_cond2_w2", "L0_cond2_b2", "L0_cond2_Wout", "L0_cond2_g_out",
        "L0_ffn_gate_w", "L0_ffn_gate_b", "L0_ffn_expert_w", "L0_ffn_expert_b"]


def kernel(**inputs):
    import numpy as _np
    import concourse.bacc as _bacc
    from concourse import mybir as _mybir
    from concourse.bass_utils import run_bass_kernel_spmd as _run

    nc = _bacc.Bacc("TRN2", target_bir_lowering=False, num_devices=1)
    arrays, aps = {}, {}
    for name in ["x"] + _INS:
        a = _np.ascontiguousarray(inputs[name])
        arrays[f"in_{name}"] = a
        aps[name] = nc.dram_tensor(f"in_{name}", a.shape, _mybir.dt.from_np(a.dtype), kind="ExternalInput").ap()
    at, table = constants()
    arrays["in_constants"] = table
    table_ap = nc.dram_tensor("in_constants", table.shape, _mybir.dt.float32, kind="ExternalInput").ap()
    shape = inputs["x"].shape
    out = nc.dram_tensor("out_0", shape, _mybir.dt.float32, kind="ExternalOutput").ap()
    build(nc, aps["x"], out, aps, table_ap, at)
    r = _run(nc, [arrays], core_ids=[0])
    return r.results[0]["out_0"]
```

```python
from contextlib import ExitStack

import numpy as np

import concourse.bass as bass
from concourse import mybir

P = 128
S = 64
BT = P // S
D = 256
KD = D // P
H = 16
DH = 64
HP = H // 2
HI = H * S
E2 = 512
KE = E2 // P
NST = 16
NLV = 4
LVW = 32
NE = 8
NPOS = 2 * S - 1
NEG = -1.0e30
DECAY_FLOOR = 20.0
LAMBDA_FLOOR = 12.0
GUARD = float(2.0 ** 57)
L2_SCALE = float(2.0 ** 20)

ALU = mybir.AluOpType
ACT = mybir.ActivationFunctionType
F32 = mybir.dt.float32
F32R = mybir.dt.float32r
BF16 = mybir.dt.bfloat16
U8 = mybir.dt.uint8
AX_X = mybir.AxisListType.X


def constants():
    tok = np.arange(P)
    seq, pos = tok // S, tok % S
    same = seq[:, None] == seq[None, :]
    parts = {"ident": np.eye(P)}
    parts["causal"] = np.where(np.arange(S)[None, :] > pos[:, None], NEG, 0.0)
    half = (tok[:, None] // DH) == (tok[None, :] // DH)
    parts["halves"] = half * 1.0
    parts["pair"] = half[:, [0, DH]] * 1.0
    sums, count_b, count_c, masks = [], [], [], []
    r, t = pos[:, None], pos[None, :]
    ref = (t // 8) * 8 + 3
    sums.append(same * (1.0 * ((r > ref) & (r <= t)) - 1.0 * ((r > t) & (r <= ref))))
    count_c.append(pos - ((pos // 8) * 8 + 3))
    count_b.append(-count_c[0])
    masks.append(same & (r // 8 == t // 8) & (r <= t))
    for m in (8, 16, 32):
        left = (t // m) % 2 == 0
        start = (t // (2 * m)) * 2 * m + m
        sums.append(same * np.where(left, (r > t) & (r < start), (r >= start) & (r <= t)))
        start = (pos // (2 * m)) * 2 * m + m
        is_left = (pos // m) % 2 == 0
        count_b.append(np.where(is_left, start - 1 - pos, 0))
        count_c.append(np.where(is_left, 0, pos - start + 1))
        masks.append(same & (r // (2 * m) == t // (2 * m)) & ((r // m) % 2 == 0) & ((t // m) % 2 == 1))
    parts["sums"] = np.concatenate(sums, 1)
    parts["neg_count_b"] = -np.stack(count_b, 1)
    parts["neg_count_c"] = -np.stack(count_c, 1)
    parts["scan_mask"] = np.concatenate(masks, 1)
    parts["level_rows"] = (tok[:, None] // LVW == np.arange(NLV)[None, :]) * 1.0
    parts["rank"] = np.broadcast_to(NE - np.arange(NE), (P, NE))
    parts["distance"] = (S - 1 - tok)[:, None]
    at, n = {}, 0
    for name, a in parts.items():
        at[name] = (n, a.shape[1])
        n += a.shape[1]
    return at, np.concatenate([np.asarray(a, np.float32) for a in parts.values()], 1)

ORDER = {
    "pe": """
        c.q1@4 b.z@3 a.kv@1 a.q0@1 a.PT0@2 c.qs@4 a.PT1@2 c.S0@4 b.xiT@3 c.S1@4 a.O0@2 a.O1@2
        b.a@3 b.bc@3 a.q1@1 a.S0@1 b.gt@3 b.E0@3 b.E1@3 b.E2@3 b.E3@3 c.PT0@4 c.PT1@4 b.G@3
        c.O0@4 c.O1@4 b.m0@3 b.m1@3 b.m2@3 a.S1@1 b.m3@3 c.W@4 a.W@2 c.ct@4 b.yT@3 a.xt@0 c.lg@4
        b.out@3 c.oT@4 c.ex0@4 c.ex1@4 c.ex2@4 c.xt@3 c.ex3@4 c.kv@3 b.xt@2 c.eb@4 c.ks@3 c.q0@3
        b.x@2""",
    "act": """
        a.rstd@0 c.kr@4 c.q0@4 c.q1@4 b.ze@3 b.xs@3 b.zs@3 a.PT0@2 a.PT1@2 b.xiT@3 c.qr@4 a.q0@1
        a.O0@2 a.O1@2 c.expm@4 b.ae@3 b.nl@3 c.prob@4 b.BT@3 b.E0@3 b.E0u@3 b.E1@3 a.q1@1 b.E2@3
        b.E3@3 c.PT0@4 c.PT1@4 c.O0@4 c.O1@4 c.rstd2@4 c.cT@4 b.yT@3 a.xnT@0 c.le@4 c.oT@4
        a.expm@1 a.rstd2@2 b.rms@2 c.rstd@3 c.xnT@3 c.ksq@3 a.prob@1 b.xnT@2 b.xe@2""",
    "dve": """
        a.den@2 c.V@4 c.ks@4 b.xg@3 a.st@0 a.xn@0 b.zg@3 b.xi@3 a.K@1 c.K@4 b.zi@3 c.qs@4 c.S0@4
        c.S1@4 c.mx@4 c.sub@4 b.ag@3 a.V@1 b.BC@3 c.den@4 b.CD@3 a.S0@1 b.Gm@3 b.t0@3 b.t1@3
        b.t2@3 a.S1@1 a.mx@1 b.t3@3 c.st2@4 c.c@4 a.sub@1 a.st2@2 c.lg@4 c.oh@4 b.x1@3 a.c@2
        c.ac0@4 c.st@3 c.xn@3 c.ac1@4 c.ac2@4 c.ac3@4 c.ac4@4 c.ac5@4 b.xn@2 c.ac6@4 c.ac7@4
        c.out@4 c.kc@3""",
    "pool": """
        a.biasm@1 a.norm@2 c.qsq@4 b.resid@3 c.addb@4 c.biasm@3 c.norm@4 b.dx@3 b.u0@3 b.u1@3
        b.u2@3 b.u3@3 b.y0@3 b.y1@3 b.y2@3 b.y3@3 b.y@3""",
    "sp": """
        a.x@0 b.xres@2 c.store@4""",
}
RESULTS = {
    "act": {"rstd": "rstd_l rstd", "rms": "ss r_l r", "xs": "xl xs", "zs": "zl zs", "kr": "kr_l kr",
            "qr": "qr_l qr", "rstd2": "rstd2_l rstd2"},
    "dve": {"a.st": "st mv", "c.st": "x1c st mv", "K": "K0 K1", "c.K": "kn K0 K1", "V": "V0 V1",
            "mx": "mx mx0", "den": "sum den rden", "st2": "st2 mv2", "c": "cn c", "BC": "Bt Ct",
            "lg": "lb lm ld", "oh": "eq em oh"},
}
TURNS = {
    0: """
        a.kv@1>dve.V1 b.E1@3>act.E1 b.m0@3>dve.t0 b.yT@3>act.yT c.oT@4>act.oT b.xt@2>act.xnT""",
    1: """
        b.z@3>dve.zi c.S0@4>dve.S0 a.O1@2>act.O1 a.S0@1>dve.S0 c.O1@4>act.O1 b.m3@3>dve.t3
        c.ct@4>act.cT c.eb@4>dve.out""",
    2: """
        a.PT1@2>act.PT1 a.O0@2>act.O0 b.a@3>act.ae a.S1@1>dve.S1 c.lg@4>dve.lb c.ex0@4>dve.ac1
        c.ks@3>dve.ks""",
    3: """
        a.q0@1>act.q0 a.q1@1>act.q1 c.PT1@4>act.PT1 c.W@4>dve.cn a.xt@0>act.xnT c.xt@3>act.xnT""",
    4: """
        c.q1@4>act.q1 a.PT0@2>act.PT0 b.gt@3>dve.CD c.PT0@4>act.PT0 a.W@2>dve.cn c.kv@3>dve.V1""",
    5: """
        b.E3@3>act.E3 c.O0@4>act.O0 b.m2@3>dve.t2 b.out@3>dve.x1 c.ex2@4>dve.ac5""",
    6: """
        c.qs@4>dve.qs b.xiT@3>act.xiT b.bc@3>dve.Ct b.E0@3>act.E0u b.E2@3>act.E2 b.G@3>dve.Gm
        b.m1@3>dve.t1 c.ex1@4>dve.ac3 b.x@2>dve.xi""",
    7: """
        c.S1@4>dve.S1 c.ex3@4>dve.ac7 c.q0@3>act.q0""",
}
MLP_BANKS = (5, 6, 7)

MLP_DVE = ["h0", "st0", "mv0", "n0", "v0", "e0", "s0", "T0", "h1", "st1", "mv1", "n1", "v1", "e1", "s1", "T1",
           "pos", "posT"]
MLP_ACT = ["rl0", "r0", "e0", "l0", "s0", "rl1", "r1", "e1", "l1", "s1"]
MLP_PE = ["T0", "h1", "T1", "pos", "posT"]


def steps_of(engine):
    entries = [entry.replace("@", ".").split(".") for entry in ORDER[engine].split()]
    return [(s, step, int(lag)) for s, step, lag in entries]


def results_of(engine, stream):
    table, out = RESULTS.get(engine, {}), []
    for s, step, lag in steps_of(engine):
        if s == stream:
            names = table.get(f"{s}.{step}", table.get(step, step))
            out += [(name, lag) for name in names.split()]
    return out


ENGINES = ("pe", "act", "dve", "pool")
MAX_LAG = max(lag for e in ORDER for _, _, lag in steps_of(e))
LOOP_FROM = MAX_LAG + 2


class Progress:

    def __init__(self, sem, results, tiles=1):
        self.sem, self.tiles = sem, tiles
        self.lag, self.place = dict(results), {name: n for n, (name, _) in enumerate(results)}

    def at(self, name, t):
        i = t + self.lag[name]
        done = [(self.lag[n], self.place[n] <= self.place[name]) for n in self.place]
        if not isinstance(t, int):
            return self.sem, i * len(done) + sum(upto - lag for lag, upto in done)
        if t < 0:
            return self.sem, 0
        return self.sem, sum(min(max(i - lag + upto, 0), self.tiles) for lag, upto in done)

    def done(self, name):
        assert name in self.place, name
        return self.sem


class Transfers:

    def __init__(self, sem, name):
        self.sem, self.name = sem, name

    def at(self, t):
        return self.sem, max(16 * (t + 1), 0) if isinstance(t, int) else 16 * (t + 1)


class Stream:

    def __init__(self, s, sem, tiles):
        self.name = s
        self.pe, self.act, self.dve, self.pool = (
            Progress(sem(f"{s}_{e}_done"), results_of(e, s), tiles) for e in ENGINES)


class Banks:

    def __init__(self, tensors, streams, tiles):
        self.streams, self.tiles, self.bank, self.turns = streams, tiles, {}, {}
        for n, text in TURNS.items():
            turns = []
            for turn in text.split():
                key, lag, end = turn.replace("@", ">").split(">")
                turns.append((key, int(lag), *end.split(".")))
            for key, *_ in turns:
                self.bank[key], self.turns[key] = tensors[n], turns

    def __getitem__(self, key):
        return self.bank[key]

    def free(self, key, t):
        turns = self.turns[key]
        n = [k for k, *_ in turns].index(key)
        for back in range(1, 1 + len(turns) * (2 + MAX_LAG)):
            before, lag, engine, step = turns[(n - back) % len(turns)]
            tile = t + turns[n][1] + (n - back) // len(turns) - lag
            if not isinstance(tile, int) or 0 <= tile < self.tiles:
                break
        stream = self.streams[before[0]]
        return {"act": stream.act, "dve": stream.dve}[engine].at(step, tile)


def build(nc, x, out, ins, consts_dram, consts_at):
    NT = x.shape[0] * x.shape[1] // P
    ctx = ExitStack()
    with ctx:
        def sb(name, shape, dt=F32):
            return ctx.enter_context(nc.sbuf_tensor(name, shape, dt))

        def sem(name):
            return ctx.enter_context(nc.semaphore(name))

        A, B, C = (Stream(s, sem, NT) for s in "abc")
        psum = [ctx.enter_context(nc.psum_tensor(f"bank{n}", [P, 512], F32)) for n in range(8)]
        banks = Banks(psum, {"a": A, "b": B, "c": C}, NT)
        mlp_bank = [psum[n] for n in MLP_BANKS]

        consts = sb("consts", [P, consts_dram.shape[1]])

        def const(name, rows=P):
            n, w = consts_at[name]
            return consts[0:rows, n:n + w]

        ident = const("ident")
        for X, s in ((A, "a"), (C, "c")):
            X.wq = sb(f"{s}_wq", [P, KD, H * DH])
            X.wkk = sb(f"{s}_wkk", [P, KD, 2, DH])
            X.wv = sb(f"{s}_wv", [P, KD, DH])
            X.wo = sb(f"{s}_wo", [P, HP, D])
            X.g = sb(f"{s}_g", [P, KD])
            X.g_out = sb(f"{s}_g_out", [P, D])
            X.null_bias = sb(f"{s}_null_bias", [P, H])
            X.bias = sb(f"{s}_bias", [P, H, S])
            X.mask = sb(f"{s}_mask", [P, NT, S], BF16)
            X.xin = sb(f"{s}_xin", [P, D])
            X.st = sb(f"{s}_st", [P, 6])
            X.mv = sb(f"{s}_mv", [P, 2])
            X.rstd_l = sb(f"{s}_rstd_l", [P, 1])
            X.rstd = sb(f"{s}_rstd", [P, 1])
            X.xn = sb(f"{s}_xn", [P, D])
            X.xnT = sb(f"{s}_xnT", [P, KD, P])
            X.K = sb(f"{s}_K", [P, BT, P])
            X.V = sb(f"{s}_V", [P, BT, P])
            X.qT = sb(f"{s}_qT", [P, HP, P])
            X.biasm = sb(f"{s}_biasm", [P, H, S])
            X.prob = sb(f"{s}_prob", [P, H, S])
            X.mx = sb(f"{s}_mx", [P, H])
            X.mx0 = sb(f"{s}_mx0", [P, H])
            X.expm = sb(f"{s}_expm", [P, H])
            X.sum = sb(f"{s}_sum", [P, H])
            X.den = sb(f"{s}_den", [P, H])
            X.rden = sb(f"{s}_rden", [P, H])
            X.PT = sb(f"{s}_PT", [P, HP, P])
            X.OT = sb(f"{s}_OT", [P, HP, P])
            X.st2 = sb(f"{s}_st2", [P, 6])
            X.mv2 = sb(f"{s}_mv2", [P, 2])
            X.rstd2_l = sb(f"{s}_rstd2_l", [P, 1])
            X.rstd2 = sb(f"{s}_rstd2", [P, 1])
            X.c = X.cn = sb(f"{s}_c", [P, D])
            X.wkv = X.PT[:, 0:KD, :]
            X.mask_u8 = X.prob[:, 0:NT * S // (4 * S), :].bitcast(U8).rearrange("p a (b s) -> p (a b) s", s=S)
        nk_col = sb("nk_col", [P, 1])
        nv_col = sb("nv_col", [P, 1])
        nv_row = sb("nv_row", [P, DH])
        eps5 = sb("eps5", [P, 1])
        wait_carrier = sb("wait_carrier", [P, 1])
        eps6 = sb("eps6", [P, 1])
        w_in = sb("w_in", [P, KD, 2 * E2])
        w_a = sb("w_a", [P, KE, E2])
        w_bc = sb("w_bc", [P, KE, 2 * NST])
        w_out = sb("w_out", [P, KE, D])
        norm_w = sb("norm_w", [P, KD])
        a_bias_hi = sb("decay_bias_hi", [1, E2], F32R)
        a_bias_lo = sb("decay_bias_lo", [1, E2], F32R)
        ones_r = sb("ones_r", [1, P], F32R)
        d_row = sb("d_row", [P, E2])
        a_base = sb("a_base", [P, NST])
        lam_e = sb("lam_e", [P, NST])
        lam_g = sb("lam_g", [P, NST])
        lam = sb("lam", [P, NST])
        lam_b = sb("lam_b", [P, NLV, NST])
        lam_c = sb("lam_c", [P, NLV, NST])
        xres = sb("xres", [P, D])
        resid = sb("resid", [P, D])
        ss = sb("ss", [P, 1])
        r_l = sb("r_l", [P, 1])
        r_ms = sb("r_ms", [P, 1])
        yn = sb("yn", [P, D])
        ynT = sb("ynT", [P, KD, P])
        xe = sb("xe", [P, E2])
        ze = sb("ze", [P, E2])
        xs, zs = xe, ze
        xi = sb("xi", [P, E2])
        zi = sb("zi", [P, E2])
        xiT = sb("xiT", [P, KE, P])
        nl = sb("nl", [P, E2])
        ae = nl
        Bt = sb("Bt", [P, NLV, LVW])
        Ct = sb("Ct", [P, NLV, LVW])
        BTt = sb("BTt", [P, P])
        CD = sb("CD", [P, NLV, P])
        Gm = sb("Gm", [P, NLV, P])
        Ef = [sb(f"Ef{l}", [P, E2]) for l in range(NLV)]
        E0u = sb("E0u", [P, E2])
        u = [sb(f"u{l}", [P, E2]) for l in range(NLV)]
        tm = u
        y = sb("y", [P, E2])
        a_bias = y[0:1, :]
        ones_f = E0u[0:1, 0:P]
        yT = sb("yT", [P, KE, P])
        x1 = sb("x1", [P, D])
        q_scale = sb("q_scale", [P, 1])
        k_scale = sb("k_scale", [P, 1])
        kq = sb("kq", [P, 1])
        nk_sq = sb("nk_sq", [P, 1])
        nk_ss = sb("nk_ss", [P, 1])
        nk_l = sb("nk_l", [P, 1])
        nk_r = sb("nk_r", [P, 1])
        nk_n = sb("nk_n", [P, 1])
        ksq = sb("ksq", [P, P])
        kss = sb("kss", [P, P])
        kraw = sb("kraw", [P, P])
        kr_l = kr = kn = kss
        qss = sb("qss", [P, H])
        qr_l = sb("qr_l", [P, H])
        qr = sb("qr", [P, H])
        gate_w = sb("gate_w", [P, KD, NE])
        gate_b = sb("gate_b", [P, NE])
        w_e = sb("w_e", [P, KD, NE, D])
        b_e = sb("b_e", [NE, D])
        cT = sb("cT", [P, KD, P])
        lb = sb("lb", [P, NE])
        lm = sb("lm", [P, 1])
        ld = sb("ld", [P, NE])
        le = sb("le", [P, NE])
        eq = sb("eq", [P, NE])
        em = sb("em", [P, 1])
        oh = sb("oh", [P, NE])
        ohT = sb("ohT", [NE, P])
        acc = sb("acc", [P, D])
        acc2 = C.cn
        yout = acc
        qsq = C.PT
        m_w0, m_b0, m_g0 = Ef[0][:, 0:D], Ef[0][:, D:], Ef[1][:, 0:D]
        m_b1, m_g1 = Ef[1][:, D:], Ef[2][:, 0:D]
        m_w1 = u[0][:, :].rearrange("p (k n) -> p k n", k=KD)
        m_w2 = Ef[3][:, 0:KD * H].rearrange("p (k n) -> p k n", k=KD)
        m_b2 = Ef[3][:, 64:64 + H]
        mh = [CD[:, 0:2, :], CD[:, 2:4, :], Gm[:, 0:2, :], Gm[:, 2:4, :], y[:, 0:D], y[:, D:]]
        mh = [m.rearrange("p l n -> p (l n)") for m in mh[0:4]] + mh[4:]
        mhT = nl[:, 0:D].rearrange("p (k n) -> p k n", k=KD)
        m_pos = C.biasm[:, 2, 0:H]
        m_posT = C.biasm[0:H, 0:2, :].rearrange("p a n -> p (a n)")
        m_scr = nc.dram_tensor("position_rows", (H, S, NPOS), F32, kind="Internal").ap()

        ld_const, ld_a, ld_b, ld_mlp, ld_c = sem("ld_const"), sem("ld_a"), sem("ld_b"), sem("ld_mlp"), sem("ld_c")
        n_ld = {}

        def load(eng, s, dst, src):
            eng.dma_start(dst, src, allow_slow_non_contiguous=True).then_inc(s, 16)
            n_ld[s.name] = n_ld.get(s.name, 0) + 16

        prep_a, prep_b, prep_c = sem("prep_a"), sem("prep_b"), sem("prep_c")
        prep_lam = sem("prep_lam")
        prep_lam_g = sem("prep_lam_g")
        prep_pool_a, prep_pool_c = sem("prep_pool_a"), sem("prep_pool_c")
        prep_nk, prep_nk_pe, prep_nk_act = sem("prep_nk"), sem("prep_nk_pe"), sem("prep_nk_act")
        mlp_dve = Progress(sem("mlp_dve"), [(name, 0) for name in MLP_DVE])
        mlp_act = Progress(sem("mlp_act"), [(name, 0) for name in MLP_ACT])
        mlp_pe = Progress(sem("mlp_pe"), [(name, 0) for name in MLP_PE])
        mlp_dma = sem("mlp_dma")
        x_loaded, xres_loaded, out_stored = (Transfers(sem(name), name)
                                             for name in ("x_loaded", "xres_loaded", "out_stored"))

        xt_dram = x.rearrange("(t b) s d -> t (b s) d", b=BT)
        ot_dram = out.rearrange("(t b) s d -> t (b s) d", b=BT)

        def col(ap):
            return ap.rearrange("(k p) -> p k", p=P)

        def rows(ap, n=P):
            return ap.unsqueeze(0).broadcast_to([n, ap.shape[0]])

        null_k, null_v = ins["cond_64"][0], ins["cond_64"][1]

        block = ctx.enter_context(nc.Block())

        def iterations(eng, engine, steps, before=None):
            def run(i):
                for s, step, lag in steps_of(engine):
                    if not isinstance(i, int) or 0 <= i - lag < NT:
                        steps[s][step](i - lag)

            for i in range(LOOP_FROM):
                if before and i in before:
                    before[i]()
                run(i)
            with eng.Fori(LOOP_FROM, NT) as i:
                run(i)
            for i in range(NT, NT + MAX_LAG):
                run(i)

        @block.sync
        def _(sp):
            def load_weights():
                load(sp, ld_const, consts[:, :], consts_dram)
                load(sp, ld_a, A.g[:, :], col(ins["L0_cond_g_in"]))
                load(sp, ld_a, A.wkv[:, :, :], ins["L0_cond_Wkv"].rearrange("(k p) n -> p k n", p=P))
                load(sp, ld_a, A.wq[:, :, :], ins["L0_cond_Wq"].rearrange("(k p) n -> p k n", p=P))
                load(sp, ld_a, nk_col[0:DH, :], null_k.unsqueeze(1))
                load(sp, ld_a, nk_col[DH:P, :], null_k.unsqueeze(1))
                load(sp, ld_a, nv_col[0:DH, :], null_v.unsqueeze(1))
                load(sp, ld_a, nv_col[DH:P, :], null_v.unsqueeze(1))
                load(sp, ld_a, nv_row[:, :], rows(null_v))
                load(sp, ld_a, A.null_bias[:, :], rows(ins["L0_cond_null_attn_bias"]))
                for b in range(BT):
                    part = slice(b * S, (b + 1) * S)
                    load(sp, ld_a, A.bias[part, :, :], ins["fside_16xSxS_0"].rearrange("h i j -> i h j"))
                    load(sp, ld_a, A.mask_u8[part, :, :],
                         ins["mask_BxS_bk0"].rearrange("(t b) j -> b t j", b=BT)[b].unsqueeze(0).broadcast_to([S, NT, S]))
                load(sp, ld_a, A.wo[:, :, :], ins["L0_cond_Wo"].rearrange("(k p) n -> p k n", p=P))
                load(sp, ld_a, A.g_out[:, :], rows(ins["L0_cond_g_out"]))
                load(sp, ld_b, norm_w[:, :], col(ins["L0_attn_norm_w"]))
                load(sp, ld_b, w_in[:, :, :], ins["L0_attn_in_proj_w"].rearrange("(k p) n -> p k n", p=P))
                load(sp, ld_b, w_a[:, :, :], ins["L0_attn_A_proj_w"].rearrange("(k p) n -> p k n", p=P))
                load(sp, ld_b, w_bc[:, :, 0:NST], ins["L0_attn_B_proj_w"].rearrange("(k p) n -> p k n", p=P))
                load(sp, ld_b, w_bc[:, :, NST:], ins["L0_attn_C_proj_w"].rearrange("(k p) n -> p k n", p=P))
                load(sp, ld_b, w_out[:, :, :], ins["L0_attn_out_proj_w"].rearrange("(k p) n -> p k n", p=P))
                load(sp, ld_b, a_bias[:, :], ins["L0_attn_A_proj_b"].unsqueeze(0))
                load(sp, ld_b, d_row[:, :], rows(ins["L0_attn_D"]))
                load(sp, ld_b, a_base[:, :], rows(ins["L0_attn_A_base"]))
                load(sp, ld_mlp, m_w0, rows(ins["L0_cond2_w0"][0]))
                for dst, name in ((m_b0, "b0"), (m_g0, "g0"), (m_b1, "b1"), (m_g1, "g1"), (m_b2, "b2")):
                    load(sp, ld_mlp, dst, rows(ins["L0_cond2_" + name]))
                load(sp, ld_mlp, m_w1, ins["L0_cond2_w1"].rearrange("(k p) n -> p k n", p=P))
                load(sp, ld_mlp, m_w2, ins["L0_cond2_w2"].rearrange("(k p) n -> p k n", p=P))
                load(sp, ld_c, C.g[:, :], col(ins["L0_cond2_g_norm"]))
                load(sp, ld_c, C.wkv[:, :, :], ins["L0_cond2_Wkv"].rearrange("(k p) n -> p k n", p=P))
                load(sp, ld_c, C.wq[:, :, :], ins["L0_cond2_Wq"].rearrange("(k p) n -> p k n", p=P))
                for part in (slice(0, DH), slice(DH, P)):
                    load(sp, ld_c, q_scale[part, :], ins["L0_cond2_q_scale"].unsqueeze(1))
                    load(sp, ld_c, k_scale[part, :], ins["L0_cond2_k_scale"].unsqueeze(1))
                load(sp, ld_c, C.null_bias[:, :], rows(ins["L0_cond2_null_attn_bias"]))
                for b in range(BT):
                    part = slice(b * S, (b + 1) * S)
                    load(sp, ld_c, C.mask_u8[part, :, :],
                         ins["mask_BxS_bf1"].rearrange("(t b) j -> b t j", b=BT)[b].unsqueeze(0).broadcast_to([S, NT, S]))
                load(sp, ld_c, C.wo[:, :, :], ins["L0_cond2_Wout"].rearrange("(k p) n -> p k n", p=P))
                load(sp, ld_c, C.g_out[:, :], rows(ins["L0_cond2_g_out"]))
                load(sp, ld_c, gate_w[:, :, :], ins["L0_ffn_gate_w"].rearrange("(k p) n -> p k n", p=P))
                load(sp, ld_c, gate_b[:, :], rows(ins["L0_ffn_gate_b"]))
                for k in range(KD):
                    load(sp, ld_c, w_e[:, k, :, :],
                         ins["L0_ffn_expert_w"][:, k * P:(k + 1) * P, :].rearrange("e p n -> p e n"))
                load(sp, ld_c, b_e[:, :], ins["L0_ffn_expert_b"])

            def position_bias():
                sp.wait_ge(*mlp_dve.at("posT", 0))
                sp.dma_start(m_scr, m_posT[:, 0:NPOS].unsqueeze(1).broadcast_to([H, S, NPOS])).then_inc(mlp_dma, 16)
                sp.wait_ge(mlp_dma, 16)
                flat = m_scr.rearrange("h i w -> h (i w)")[:, S - 1:S - 1 + S * (NPOS - 1)]
                skewed = flat.rearrange("h (i w) -> i h w", w=NPOS - 1)[:, :, 0:S]
                for b in range(BT):
                    sp.dma_start(C.bias[b * S:(b + 1) * S, :, :], skewed).then_inc(mlp_dma, 16)

            def load_x(t):
                sp.wait_ge(*A.dve.at("xn", t - 1))
                sp.dma_start(A.xin[:, :], xt_dram[t]).then_inc(x_loaded.sem, 16)

            def load_xres(t):
                sp.wait_ge(*B.pool.at("resid", t - 1))
                sp.dma_start(xres[:, :], xt_dram[t]).then_inc(xres_loaded.sem, 16)

            def store(t):
                sp.wait_ge(*C.dve.at("out", t))
                sp.dma_start(ot_dram[t], yout[:, :]).then_inc(out_stored.sem, 16)

            iterations(sp, "sp", {"a": {"x": load_x}, "b": {"xres": load_xres}, "c": {"store": store}},
                       before={0: load_weights, 2: position_bias})
            sp.wait_ge(*out_stored.at(NT - 1))

        @block.tensor
        def _(pe):
            def attention(X):
                s, p, act, dve, pool = X.name, X.pe, X.act, X.dve, X.pool

                def bank(unit):
                    return banks[f"{s}.{unit}"]

                def xt(t):
                    pe.wait_ge(*banks.free(f"{s}.xt", t))
                    pe.wait_ge(*dve.at("xn", t))
                    for k in range(KD):
                        mm = pe.transpose(bank("xt")[:, k * P:(k + 1) * P], X.xn[:, k * P:(k + 1) * P], ident)
                    mm.then_inc(p.done("xt"), 1)

                def kv(t):
                    pe.wait_ge(*banks.free(f"{s}.kv", t))
                    pe.wait_ge(*act.at("xnT", t))
                    for k in range(KD):
                        pe.matmul(bank("kv")[:, 0:P], X.wkk[:, k, :, :], X.xnT[:, k, :],
                                  start=k == 0, stop=k == KD - 1)
                    for b in range(BT):
                        for half in range(2):
                            for k in range(KD):
                                mm = pe.matmul(bank("kv")[half * S:(half + 1) * S, P + b * DH:P + (b + 1) * DH],
                                               X.xnT[:, k, b * S:(b + 1) * S], X.wv[:, k, :],
                                               start=k == 0, stop=k == KD - 1)
                    mm.then_inc(p.done("kv"), 1)

                def ks(t):
                    pe.wait_ge(*banks.free(f"{s}.ks", t))
                    pe.wait_ge(*act.at("ksq", t))
                    pe.matmul(bank("ks")[:, 0:P], const("halves"), ksq[:, :], start=True, stop=True)\
                      .then_inc(p.done("ks"), 1)

                def q(half):
                    def run(t):
                        pe.wait_ge(*banks.free(f"{s}.q{half}", t))
                        for m in range(4):
                            hp = 4 * half + m
                            for k in range(KD):
                                mm = pe.matmul(bank(f"q{half}")[:, m * P:(m + 1) * P],
                                               X.wq[:, k, hp * P:(hp + 1) * P], X.xnT[:, k, :],
                                               start=k == 0, stop=k == KD - 1)
                        mm.then_inc(p.done(f"q{half}"), 1)
                    return run

                def qs(t):
                    pe.wait_ge(*banks.free(f"{s}.qs", t))
                    pe.wait_ge(*pool.at("qsq", t))
                    for hp in range(HP):
                        mm = pe.matmul(bank("qs")[:, 2 * hp:2 * hp + 2], qsq[:, hp, :], const("pair"),
                                       start=True, stop=True)
                    mm.then_inc(p.done("qs"), 1)

                def scores(half):
                    def run(t):
                        pe.wait_ge(*banks.free(f"{s}.S{half}", t))
                        pe.wait_ge(*dve.at("K1", t))
                        pe.wait_ge(*act.at(f"q{half}", t))
                        for m in range(4):
                            for b in range(BT):
                                mm = pe.matmul(bank(f"S{half}")[b * S:(b + 1) * S, m * P:(m + 1) * P],
                                               X.qT[:, 4 * half + m, b * S:(b + 1) * S], X.K[:, b, :],
                                               start=True, stop=True)
                        mm.then_inc(p.done(f"S{half}"), 1)
                    return run

                def PT(half):
                    def run(t):
                        pe.wait_ge(*banks.free(f"{s}.PT{half}", t))
                        pe.wait_ge(*pool.at("norm", t))
                        for m in range(4):
                            hp = 4 * half + m
                            mm = pe.transpose(bank(f"PT{half}")[:, m * P:(m + 1) * P],
                                              X.prob[:, 2 * hp:2 * hp + 2, :], ident)
                        mm.then_inc(p.done(f"PT{half}"), 1)
                    return run

                def PV(b):
                    def run(t):
                        pe.wait_ge(*banks.free(f"{s}.O{b}", t))
                        pe.wait_ge(*dve.at("V1", t))
                        pe.wait_ge(*act.at("PT1", t))
                        pe.matmul(bank(f"O{b}")[:, :], X.V[:, b, :], X.PT[:, :, b * S:(b + 1) * S],
                                  start=True, stop=True).then_inc(p.done(f"O{b}"), 1)
                    return run

                def W(t):
                    pe.wait_ge(*banks.free(f"{s}.W", t))
                    pe.wait_ge(*act.at("O1", t))
                    for hp in range(HP):
                        mm = pe.matmul(bank("W")[:, 0:D], X.OT[:, hp, :], X.wo[:, hp, :],
                                       start=hp == 0, stop=hp == HP - 1)
                    mm.then_inc(p.done("W"), 1)

                return {"xt": xt, "kv": kv, "ks": ks, "q0": q(0), "q1": q(1), "qs": qs, "S0": scores(0),
                        "S1": scores(1), "PT0": PT(0), "PT1": PT(1), "O0": PV(0), "O1": PV(1), "W": W}

            def scan():
                p, act, dve, pool = B.pe, B.act, B.dve, B.pool

                def xt(t):
                    pe.wait_ge(*banks.free("b.xt", t))
                    pe.wait_ge(*dve.at("xn", t))
                    for k in range(KD):
                        mm = pe.transpose(banks["b.xt"][:, k * P:(k + 1) * P], yn[:, k * P:(k + 1) * P], ident)
                    mm.then_inc(p.done("xt"), 1)

                def proj(n, unit):
                    def run(t):
                        pe.wait_ge(*banks.free(f"b.{unit}", t))
                        pe.wait_ge(*act.at("xnT", t))
                        for k in range(KD):
                            mm = pe.matmul(banks[f"b.{unit}"][:, :], ynT[:, k, :], w_in[:, k, n * E2:(n + 1) * E2],
                                           start=k == 0, stop=k == KD - 1)
                        mm.then_inc(p.done(unit), 1)
                    return run

                def xiT_(t):
                    pe.wait_ge(*banks.free("b.xiT", t))
                    pe.wait_ge(*dve.at("xi", t))
                    for k in range(KE):
                        mm = pe.transpose(banks["b.xiT"][:, k * P:(k + 1) * P], xi[:, k * P:(k + 1) * P], ident)
                    mm.then_inc(p.done("xiT"), 1)

                def a(t):
                    pe.wait_ge(*banks.free("b.a", t))
                    pe.wait_ge(*act.at("xiT", t))
                    for k in range(KE):
                        pe.matmul(banks["b.a"][:, :], xiT[:, k, :], w_a[:, k, :], start=k == 0, stop=False)
                    pe.matmul(banks["b.a"][:, :], ones_r[:, :], a_bias_hi[:, :], start=False, stop=False)
                    pe.matmul(banks["b.a"][:, :], ones_r[:, :], a_bias_lo[:, :], start=False, stop=True)\
                      .then_inc(p.done("a"), 1)

                def bc(t):
                    pe.wait_ge(*banks.free("b.bc", t))
                    pe.wait_ge(*act.at("xiT", t))
                    for k in range(KE):
                        mm = pe.matmul(banks["b.bc"][:, 0:2 * NST], xiT[:, k, :], w_bc[:, k, :],
                                       start=k == 0, stop=k == KE - 1)
                    mm.then_inc(p.done("bc"), 1)

                def gt(t):
                    pe.wait_ge(*banks.free("b.gt", t))
                    pe.wait_ge(*dve.at("Ct", t))
                    pe.transpose(banks["b.gt"][:, 0:P], Bt[:, :, :], ident)
                    pe.transpose(banks["b.gt"][:, P:2 * P], Ct[:, :, :], ident).then_inc(p.done("gt"), 1)

                def G(t):
                    pe.wait_ge(*banks.free("b.G", t))
                    pe.wait_ge(*act.at("BT", t))
                    pe.wait_ge(*dve.at("CD", t))
                    pe.matmul(banks["b.G"][:, :], BTt[:, :], CD[:, :, :], start=True, stop=True)\
                      .then_inc(p.done("G"), 1)

                def E(l):
                    def run(t):
                        pe.wait_ge(*banks.free(f"b.E{l}", t))
                        pe.wait_ge(*act.at("nl", t))
                        pe.matmul(banks[f"b.E{l}"][:, :], const("sums")[:, l * P:(l + 1) * P], nl[:, :],
                                  start=True, stop=True).then_inc(p.done(f"E{l}"), 1)
                    return run

                def mix(l):
                    def run(t):
                        pe.wait_ge(*banks.free(f"b.m{l}", t))
                        pe.wait_ge(*dve.at("Gm", t))
                        pe.wait_ge(*pool.at(f"u{l}", t))
                        pe.matmul(banks[f"b.m{l}"][:, :], Gm[:, l, :], u[l][:, :],
                                  start=True, stop=True).then_inc(p.done(f"m{l}"), 1)
                    return run

                def yT_(t):
                    pe.wait_ge(*banks.free("b.yT", t))
                    pe.wait_ge(*pool.at("y", t))
                    for k in range(KE):
                        mm = pe.transpose(banks["b.yT"][:, k * P:(k + 1) * P], y[:, k * P:(k + 1) * P], ident)
                    mm.then_inc(p.done("yT"), 1)

                def out_(t):
                    pe.wait_ge(*banks.free("b.out", t))
                    pe.wait_ge(*act.at("yT", t))
                    for k in range(KE):
                        mm = pe.matmul(banks["b.out"][:, 0:D], yT[:, k, :], w_out[:, k, :],
                                       start=k == 0, stop=k == KE - 1)
                    mm.then_inc(p.done("out"), 1)

                return {"xt": xt, "x": proj(0, "x"), "z": proj(1, "z"), "xiT": xiT_, "a": a, "bc": bc, "gt": gt,
                        "G": G, "yT": yT_, "out": out_} | {f"E{l}": E(l) for l in range(NLV)}\
                    | {f"m{l}": mix(l) for l in range(NLV)}

            def experts():
                p, act, dve = C.pe, C.act, C.dve

                def ct(t):
                    pe.wait_ge(*banks.free("c.ct", t))
                    pe.wait_ge(*dve.at("c", t))
                    for k in range(KD):
                        mm = pe.transpose(banks["c.ct"][:, k * P:(k + 1) * P], C.c[:, k * P:(k + 1) * P], ident)
                    mm.then_inc(p.done("ct"), 1)

                def lg(t):
                    pe.wait_ge(*banks.free("c.lg", t))
                    pe.wait_ge(*act.at("cT", t))
                    for k in range(KD):
                        mm = pe.matmul(banks["c.lg"][:, 0:NE], cT[:, k, :], gate_w[:, k, :],
                                       start=k == 0, stop=k == KD - 1)
                    mm.then_inc(p.done("lg"), 1)

                def oT(t):
                    pe.wait_ge(*banks.free("c.oT", t))
                    pe.wait_ge(*dve.at("oh", t))
                    pe.transpose(banks["c.oT"][0:NE, 0:P], oh[:, :], ident).then_inc(p.done("oT"), 1)

                def ex(n):
                    def run(t):
                        pe.wait_ge(*banks.free(f"c.ex{n}", t))
                        pe.wait_ge(*act.at("cT", t))
                        for k in range(KD):
                            mm = pe.matmul(banks[f"c.ex{n}"][:, :], cT[:, k, :], w_e[:, k, 2 * n:2 * n + 2, :],
                                           start=k == 0, stop=k == KD - 1)
                        mm.then_inc(p.done(f"ex{n}"), 1)
                    return run

                def eb(t):
                    pe.wait_ge(*banks.free("c.eb", t))
                    pe.wait_ge(*act.at("oT", t))
                    pe.matmul(banks["c.eb"][:, 0:D], ohT[:, :], b_e[:, :], start=True, stop=True)\
                      .then_inc(p.done("eb"), 1)

                return {"ct": ct, "lg": lg, "oT": oT, "eb": eb} | {f"ex{n}": ex(n) for n in range(NE // 2)}

            pe.wait_ge(ld_const, 16)
            pe.wait_ge(prep_a, 1)

            def setup_bc():
                bank = mlp_bank
                pe.wait_ge(prep_nk, 1)
                pe.matmul(bank[0][:, 0:1], const("halves"), nk_sq[:, :], start=True, stop=True)\
                  .then_inc(prep_nk_pe, 1)
                for layer in range(2):
                    pe.wait_ge(*mlp_dve.at(f"s{layer}", 0))
                    src = mh[2] if layer == 0 else mh[5]
                    for k in range(KD):
                        mm = pe.transpose(bank[1][:, k * P:(k + 1) * P], src[:, k * P:(k + 1) * P], ident)
                    mm.then_inc(mlp_pe.done(f"T{layer}"), 1)
                    pe.wait_ge(*mlp_dve.at(f"T{layer}", 0))
                    w, n = (m_w1, D) if layer == 0 else (m_w2, H)
                    for k in range(KD):
                        mm = pe.matmul(bank[2][:, 0:n], mhT[:, k, :], w[:, k, :],
                                       start=k == 0, stop=k == KD - 1)
                    mm.then_inc(mlp_pe.done("h1" if layer == 0 else "pos"), 1)
                pe.wait_ge(*mlp_dve.at("pos", 0))
                pe.transpose(bank[1][0:H, 0:P], m_pos, ident).then_inc(mlp_pe.done("posT"), 1)
                pe.wait_ge(*mlp_dve.at("posT", 0))
                pe.wait_ge(prep_b, 1)
                pe.wait_ge(prep_c, 1)

            iterations(pe, "pe", {"a": attention(A), "b": scan(), "c": attention(C) | experts()},
                       before={1: setup_bc})

        @block.scalar
        def _(act):
            def rstd_of(X, t, src, mid, dst, mark_l, mark):
                act.activation(mid[:, :], src[:, 1:2], ACT.Ln, bias=eps5[:, :]).then_inc(X.act.done(mark_l), 1)
                act.wait_ge(*X.act.at(mark_l, t))
                act.activation(dst[:, :], mid[:, :], ACT.Exp, scale=-0.5).then_inc(X.act.done(mark), 1)

            def attention(X):
                s, p, a, dve, pool = X.name, X.pe, X.act, X.dve, X.pool

                def rstd(t):
                    act.wait_ge(*dve.at("mv", t))
                    act.wait_ge(*dve.at("xn", t - 1))
                    rstd_of(X, t, X.mv, X.rstd_l, X.rstd, "rstd_l", "rstd")

                def xnT(t):
                    act.wait_ge(*p.at("xt", t))
                    act.wait_ge(*p.at("q1", t - 1))
                    act.copy(X.xnT[:, :, :], banks[f"{s}.xt"][:, 0:D]).then_inc(a.done("xnT"), 1)

                def ksq_(t):
                    act.wait_ge(*p.at("kv", t))
                    act.wait_ge(*p.at("ks", t - 1))
                    act.activation(ksq[:, :], banks["c.kv"][:, 0:P], ACT.Square).then_inc(a.done("ksq"), 1)

                def kr_(t):
                    act.wait_ge(*dve.at("ks", t))
                    act.activation(kr_l[:, :], kss[:, :], ACT.Ln, scale=L2_SCALE).then_inc(a.done("kr_l"), 1)
                    act.wait_ge(*a.at("kr_l", t))
                    act.activation(kr[:, :], kr_l[:, :], ACT.Exp, scale=-0.5).then_inc(a.done("kr"), 1)

                def q(half):
                    def run(t):
                        act.wait_ge(*p.at(f"q{half}", t))
                        act.wait_ge(*p.at("S1", t - 1))
                        if s == "c":
                            act.wait_ge(*pool.at("qsq", t - 1))
                        act.copy(X.qT[:, 4 * half:4 * half + 4, :], banks[f"{s}.q{half}"][:, :])\
                           .then_inc(a.done(f"q{half}"), 1)
                    return run

                def qr_(t):
                    act.wait_ge(*dve.at("qs", t))
                    act.activation(qr_l[:, :], qss[:, :], ACT.Ln, scale=L2_SCALE).then_inc(a.done("qr_l"), 1)
                    act.wait_ge(*a.at("qr_l", t))
                    act.wait_ge(*dve.at("S1", t - 1))
                    act.activation(qr[:, :], qr_l[:, :], ACT.Exp, scale=-0.5).then_inc(a.done("qr"), 1)

                def expm(t):
                    act.wait_ge(*dve.at("mx0", t))
                    act.wait_ge(*dve.at("den", t - 1))
                    act.activation(X.expm[:, :], X.mx0[:, :], ACT.Exp, scale=-1.0).then_inc(a.done("expm"), 1)

                def prob(t):
                    act.wait_ge(*dve.at("sub", t))
                    act.activation(X.prob[:, :, :], X.prob[:, :, :], ACT.Exp).then_inc(a.done("prob"), 1)

                def PT(half):
                    def run(t):
                        act.wait_ge(*p.at(f"PT{half}", t))
                        act.wait_ge(*p.at("O1", t - 1))
                        act.copy(X.PT[:, 4 * half:4 * half + 4, :], banks[f"{s}.PT{half}"][:, :])\
                           .then_inc(a.done(f"PT{half}"), 1)
                    return run

                def PV(b):
                    def run(t):
                        act.wait_ge(*p.at(f"O{b}", t))
                        act.wait_ge(*p.at("W", t - 1))
                        act.activation(X.OT[:, :, b * S:(b + 1) * S],
                                       banks[f"{s}.O{b}"][:, :].rearrange("p (h i) -> p h i", h=HP),
                                       ACT.Identity, bias=nv_col[:, :]).then_inc(a.done(f"O{b}"), 1)
                    return run

                def rstd2(t):
                    act.wait_ge(*dve.at("mv2", t))
                    act.wait_ge(*dve.at("cn", t - 1))
                    rstd_of(X, t, X.mv2, X.rstd2_l, X.rstd2, "rstd2_l", "rstd2")

                return {"rstd": rstd, "xnT": xnT, "ksq": ksq_, "kr": kr_, "q0": q(0), "q1": q(1), "qr": qr_,
                        "expm": expm, "prob": prob, "PT0": PT(0), "PT1": PT(1), "O0": PV(0), "O1": PV(1),
                        "rstd2": rstd2}

            def scan():
                p, a, dve, pool = B.pe, B.act, B.dve, B.pool

                def rms(t):
                    act.wait_ge(*A.dve.at("c", t))
                    act.wait_ge(*p.at("z", t - 1))
                    act.activation(ynT[:, :, :], A.c[:, :], ACT.Square, accum_out=ss[:, :])\
                       .then_inc(a.done("ss"), 1)
                    act.wait_ge(*a.at("ss", t))
                    act.activation(r_l[:, :], ss[:, :], ACT.Ln, scale=1.0 / D, bias=eps6[:, :])\
                       .then_inc(a.done("r_l"), 1)
                    act.wait_ge(*a.at("r_l", t))
                    act.wait_ge(*dve.at("xn", t - 1))
                    act.activation(r_ms[:, :], r_l[:, :], ACT.Exp, scale=-0.5).then_inc(a.done("r"), 1)

                def xnT(t):
                    act.wait_ge(*p.at("xt", t))
                    act.wait_ge(*p.at("z", t - 1))
                    act.copy(ynT[:, :, :], banks["b.xt"][:, 0:D]).then_inc(a.done("xnT"), 1)

                def exp_x(t):
                    act.wait_ge(*p.at("x", t))
                    act.wait_ge(*dve.at("xi", t - 1))
                    act.activation(xe[:, :], banks["b.x"][:, :], ACT.Exp, scale=-1.0).then_inc(a.done("xe"), 1)

                def exp_z(t):
                    act.wait_ge(*p.at("z", t))
                    act.wait_ge(*dve.at("zi", t - 1))
                    act.activation(ze[:, :], banks["b.z"][:, :], ACT.Exp, scale=-1.0).then_inc(a.done("ze"), 1)

                def sig_x(t):
                    act.wait_ge(*dve.at("xg", t))
                    act.activation(xe[:, :], xe[:, :], ACT.Ln).then_inc(a.done("xl"), 1)
                    act.wait_ge(*a.at("xl", t))
                    act.activation(xs[:, :], xe[:, :], ACT.Exp, scale=-1.0).then_inc(a.done("xs"), 1)

                def sig_z(t):
                    act.wait_ge(*dve.at("zg", t))
                    act.activation(ze[:, :], ze[:, :], ACT.Ln).then_inc(a.done("zl"), 1)
                    act.wait_ge(*a.at("zl", t))
                    act.activation(zs[:, :], ze[:, :], ACT.Exp, scale=-1.0).then_inc(a.done("zs"), 1)

                def xiT_(t):
                    act.wait_ge(*p.at("xiT", t))
                    act.wait_ge(*p.at("bc", t - 1))
                    act.copy(xiT[:, :, :], banks["b.xiT"][:, :]).then_inc(a.done("xiT"), 1)

                def exp_a(t):
                    act.wait_ge(*p.at("a", t))
                    act.wait_ge(*p.at("E3", t - 1))
                    act.activation(ae[:, :], banks["b.a"][:, :], ACT.Exp, scale=-1.0).then_inc(a.done("ae"), 1)

                def log_a(t):
                    act.wait_ge(*dve.at("ag", t))
                    act.activation(nl[:, :], ae[:, :], ACT.Ln).then_inc(a.done("nl"), 1)

                def BT_(t):
                    act.wait_ge(*p.at("gt", t))
                    act.wait_ge(*p.at("G", t - 1))
                    act.copy(BTt[:, :], banks["b.gt"][:, 0:P]).then_inc(a.done("BT"), 1)

                def E0u_(t):
                    act.wait_ge(*p.at("E0", t))
                    act.wait_ge(*pool.at("u0", t - 1))
                    act.activation(E0u[:, :], banks["b.E0"][:, :], ACT.Exp).then_inc(a.done("E0u"), 1)

                def E(l):
                    def run(t):
                        act.wait_ge(*p.at(f"E{l}", t))
                        act.wait_ge(*dve.at(f"t{l}", t - 1))
                        if l:
                            act.wait_ge(*pool.at(f"u{l}", t - 1))
                        act.activation(Ef[l][:, :], banks[f"b.E{l}"][:, :], ACT.Exp, scale=-1.0)\
                           .then_inc(a.done(f"E{l}"), 1)
                    return run

                def yT_(t):
                    act.wait_ge(*p.at("yT", t))
                    act.wait_ge(*p.at("out", t - 1))
                    act.copy(yT[:, :, :], banks["b.yT"][:, :]).then_inc(a.done("yT"), 1)

                return {"rms": rms, "xnT": xnT, "xe": exp_x, "ze": exp_z, "xs": sig_x, "zs": sig_z, "xiT": xiT_,
                        "ae": exp_a, "nl": log_a, "BT": BT_, "E0u": E0u_, "yT": yT_}\
                    | {f"E{l}": E(l) for l in range(NLV)}

            def experts():
                p, a, dve = C.pe, C.act, C.dve

                def cT_(t):
                    act.wait_ge(*p.at("ct", t))
                    act.wait_ge(*p.at("ex3", t - 1))
                    act.copy(cT[:, :, :], banks["c.ct"][:, 0:D]).then_inc(a.done("cT"), 1)

                def le_(t):
                    act.wait_ge(*dve.at("ld", t))
                    act.activation(le[:, :], ld[:, :], ACT.Exp).then_inc(a.done("le"), 1)

                def oT(t):
                    act.wait_ge(*p.at("oT", t))
                    act.wait_ge(*p.at("eb", t - 1))
                    act.copy(ohT[:, :], banks["c.oT"][0:NE, 0:P]).then_inc(a.done("oT"), 1)

                return {"cT": cT_, "le": le_, "oT": oT}

            act.preload_act_table_set("natural_log_exp_and_others")

            def setup_a():
                act.wait_ge(ld_a, n_ld[ld_a.name])
                act.wait_ge(prep_a, 1)

            def setup_bc():
                act.wait_ge(ld_b, n_ld[ld_b.name])
                act.activation(lam_e[:, :], a_base[:, :], ACT.Exp, scale=-1.0).then_inc(prep_lam, 1)
                act.wait_ge(prep_lam_g, 1)
                act.activation(lam[:, :], lam_g[:, :], ACT.Ln).then_inc(prep_lam, 1)
                act.wait_ge(prep_lam, 2)
                for l in range(NLV):
                    act.activation(lam_b[:, l, :], lam[:, :], ACT.Exp, scale=const("neg_count_b")[:, l:l + 1])\
                       .then_inc(prep_lam, 1)
                    act.activation(lam_c[:, l, :], lam[:, :], ACT.Exp, scale=const("neg_count_c")[:, l:l + 1])\
                       .then_inc(prep_lam, 1)
                act.wait_ge(prep_nk, 2)
                act.activation(nk_l[:, :], nk_ss[:, :], ACT.Ln, scale=L2_SCALE).then_inc(prep_nk_act, 1)
                act.wait_ge(prep_nk_act, 1)
                act.activation(nk_r[:, :], nk_l[:, :], ACT.Exp, scale=-0.5).then_inc(prep_nk_act, 1)
                for layer in range(2):
                    act.wait_ge(*mlp_dve.at(f"mv{layer}", 0))
                    act.activation(C.rstd_l[:, :], C.mv[:, 1:2], ACT.Ln, bias=eps5[:, :])\
                       .then_inc(mlp_act.done(f"rl{layer}"), 1)
                    act.wait_ge(*mlp_act.at(f"rl{layer}", 0))
                    act.activation(C.rstd[:, :], C.rstd_l[:, :], ACT.Exp, scale=-0.5)\
                       .then_inc(mlp_act.done(f"r{layer}"), 1)
                    v = mh[1] if layer == 0 else mh[4]
                    act.wait_ge(*mlp_dve.at(f"v{layer}", 0))
                    act.activation(mh[3], v, ACT.Exp, scale=-1.0).then_inc(mlp_act.done(f"e{layer}"), 1)
                    act.wait_ge(*mlp_dve.at(f"e{layer}", 0))
                    act.activation(mh[3], mh[3], ACT.Ln).then_inc(mlp_act.done(f"l{layer}"), 1)
                    act.wait_ge(*mlp_act.at(f"l{layer}", 0))
                    act.activation(mh[3], mh[3], ACT.Exp, scale=-1.0).then_inc(mlp_act.done(f"s{layer}"), 1)

            iterations(act, "act", {"a": attention(A), "b": scan(), "c": attention(C) | experts()},
                       before={0: setup_a, 1: setup_bc})

        @block.vector
        def _(dve):
            def stats(X, t, src, st, mv, mark_st, mark_mv):
                dve.bn_stats(st[:, :], src).then_inc(X.dve.done(mark_st), 1)
                dve.wait_ge(*X.dve.at(mark_st, t))
                dve.memset(wait_carrier[:, :], 0.0)
                dve.bn_aggr(mv[:, :], st[:, :]).then_inc(X.dve.done(mark_mv), 1)

            def attention(X):
                s, p, act, d, pool = X.name, X.pe, X.act, X.dve, X.pool

                def st(t):
                    if s == "a":
                        dve.wait_ge(*x_loaded.at(t))
                        dve.wait_ge(*d.at("xn", t - 1))
                    else:
                        dve.wait_ge(*B.dve.at("x1", t))
                        dve.wait_ge(*d.at("ac0", t - 1))
                        dve.tensor_copy(X.xin[:, :], x1[:, :]).then_inc(d.done("x1c"), 1)
                        dve.wait_ge(*d.at("x1c", t))
                    stats(X, t, X.xin[:, :], X.st, X.mv, "st", "mv")

                def xn(t):
                    dve.wait_ge(*act.at("rstd", t))
                    dve.wait_ge(*p.at("xt", t - 1))
                    dve.tensor_scalar(X.xn[:, :], X.xin[:, :], X.mv[:, 0:1], X.rstd[:, :],
                                      ALU.subtract, ALU.mult).then_inc(d.done("xn"), 1)

                def K(t):
                    if s == "a":
                        dve.wait_ge(*p.at("kv", t))
                    else:
                        dve.wait_ge(*act.at("kr", t))
                        dve.wait_ge(*d.at("kc", t))
                        dve.tensor_tensor(kn[:, :], kraw[:, :], kr[:, :], ALU.mult).then_inc(d.done("kn"), 1)
                        dve.wait_ge(*d.at("kn", t))
                    dve.wait_ge(*p.at("S1", t - 1))
                    for half in range(2):
                        part = slice(half * DH, (half + 1) * DH)
                        dst = X.K[part, :, half * S:(half + 1) * S]
                        if s == "a":
                            dve.tensor_scalar(dst, banks["a.kv"][part, 0:P].rearrange("p (b j) -> p b j", b=BT),
                                              nk_col[part, :], None, ALU.subtract).then_inc(d.done(f"K{half}"), 1)
                        else:
                            dve.tensor_scalar(dst, kn[part, :].rearrange("p (b j) -> p b j", b=BT),
                                              kq[part, :], nk_n[part, :], ALU.mult, ALU.subtract)\
                               .then_inc(d.done(f"K{half}"), 1)

                def V(t):
                    dve.wait_ge(*p.at("kv", t))
                    dve.wait_ge(*p.at("O1", t - 1))
                    for half in range(2):
                        part = slice(half * S, (half + 1) * S)
                        dve.tensor_tensor(X.V[part, :, half * DH:(half + 1) * DH],
                                          banks[f"{s}.kv"][part, P:2 * P].rearrange("p (b n) -> p b n", b=BT),
                                          nv_row[part, :].unsqueeze(1).broadcast_to([S, BT, DH]),
                                          ALU.subtract).then_inc(d.done(f"V{half}"), 1)

                def kc(t):
                    dve.wait_ge(*act.at("ksq", t))
                    dve.wait_ge(*d.at("kn", t - 1))
                    dve.tensor_copy(kraw[:, :], banks["c.kv"][:, 0:P]).then_inc(d.done("kc"), 1)

                def ks(t):
                    dve.wait_ge(*p.at("ks", t))
                    dve.wait_ge(*d.at("K1", t - 1))
                    dve.tensor_scalar(kss[:, :], banks["c.ks"][:, 0:P], 1.0e-24, None, ALU.max)\
                       .then_inc(d.done("ks"), 1)

                def qs(t):
                    dve.wait_ge(*p.at("qs", t))
                    dve.wait_ge(*d.at("S0", t - 1))
                    dve.tensor_scalar(qss[:, :], banks["c.qs"][:, 0:H], 1.0e-24, None, ALU.max)\
                       .then_inc(d.done("qs"), 1)

                def scores(half):
                    def run(t):
                        heads = slice(8 * half, 8 * half + 8)
                        dve.wait_ge(*p.at(f"S{half}", t))
                        dve.wait_ge(*p.at("PT1", t - 1))
                        src = banks[f"{s}.S{half}"][:, :].rearrange("p (h j) -> p h j", h=8)
                        if s == "a":
                            dve.wait_ge(*pool.at("biasm", t))
                            dve.tensor_tensor(X.prob[:, heads, :], src, X.biasm[:, heads, :], ALU.add)\
                               .then_inc(d.done(f"S{half}"), 1)
                        else:
                            dve.wait_ge(*act.at("qr", t))
                            dve.tensor_tensor(X.prob[:, heads, :], src,
                                              qr[:, heads].unsqueeze(2).broadcast_to([P, 8, S]), ALU.mult)\
                               .then_inc(d.done(f"S{half}"), 1)
                    return run

                def mx(t):
                    if s == "a":
                        dve.wait_ge(*d.at("S1", t))
                    else:
                        dve.wait_ge(*pool.at("addb", t))
                    dve.tensor_reduce(X.mx[:, :], X.prob[:, :, :], AX_X, ALU.max).then_inc(d.done("mx"), 1)
                    dve.wait_ge(*d.at("mx", t))
                    dve.tensor_scalar(X.mx0[:, :], X.mx[:, :], 0.0, None, ALU.max).then_inc(d.done("mx0"), 1)

                def sub(t):
                    dve.wait_ge(*d.at("mx0", t))
                    dve.tensor_tensor(X.prob[:, :, :], X.prob[:, :, :],
                                      X.mx0[:, :].unsqueeze(2).broadcast_to([P, H, S]), ALU.subtract)\
                       .then_inc(d.done("sub"), 1)

                def den(t):
                    dve.wait_ge(*act.at("prob", t))
                    dve.tensor_reduce(X.sum[:, :], X.prob[:, :, :], AX_X, ALU.add).then_inc(d.done("sum"), 1)
                    dve.wait_ge(*d.at("sum", t))
                    dve.tensor_tensor(X.den[:, :], X.sum[:, :], X.expm[:, :], ALU.add).then_inc(d.done("den"), 1)
                    dve.wait_ge(*d.at("den", t))
                    dve.wait_ge(*pool.at("norm", t - 1))
                    dve.reciprocal(X.rden[:, :], X.den[:, :]).then_inc(d.done("rden"), 1)

                def st2(t):
                    dve.wait_ge(*p.at("W", t))
                    dve.wait_ge(*d.at("cn", t - 1))
                    stats(X, t, banks[f"{s}.W"][:, 0:D], X.st2, X.mv2, "st2", "mv2")

                def c(t):
                    dve.wait_ge(*act.at("rstd2", t))
                    if s == "a":
                        dve.wait_ge(*B.act.at("ss", t - 1))
                        dve.wait_ge(*B.pool.at("resid", t - 1))
                        dve.wait_ge(*B.dve.at("xn", t - 1))
                    else:
                        dve.wait_ge(*p.at("ct", t - 1))
                        dve.wait_ge(*d.at("out", t - 1))
                    dve.tensor_scalar(X.cn[:, :], banks[f"{s}.W"][:, 0:D], X.mv2[:, 0:1], X.rstd2[:, :],
                                      ALU.subtract, ALU.mult).then_inc(d.done("cn"), 1)
                    dve.wait_ge(*d.at("cn", t))
                    dve.tensor_tensor(X.c[:, :], X.cn[:, :], X.g_out[:, :], ALU.mult).then_inc(d.done("c"), 1)

                return {"st": st, "xn": xn, "K": K, "V": V, "kc": kc, "ks": ks, "qs": qs, "S0": scores(0),
                        "S1": scores(1), "mx": mx, "sub": sub, "den": den, "st2": st2, "c": c}

            def scan():
                p, act, d, pool = B.pe, B.act, B.dve, B.pool

                def xn(t):
                    dve.wait_ge(*act.at("r", t))
                    dve.wait_ge(*p.at("xt", t - 1))
                    dve.tensor_scalar(yn[:, :], A.c[:, :], r_ms[:, :], None, ALU.mult).then_inc(d.done("xn"), 1)

                def xg(t):
                    dve.wait_ge(*act.at("xe", t))
                    dve.tensor_scalar(xe[:, :], xe[:, :], GUARD, 1.0, ALU.min, ALU.add).then_inc(d.done("xg"), 1)

                def zg(t):
                    dve.wait_ge(*act.at("ze", t))
                    dve.tensor_scalar(ze[:, :], ze[:, :], GUARD, 1.0, ALU.min, ALU.add).then_inc(d.done("zg"), 1)

                def xi_(t):
                    dve.wait_ge(*act.at("xs", t))
                    dve.wait_ge(*p.at("xiT", t - 1))
                    dve.wait_ge(*pool.at("u3", t - 1))
                    dve.tensor_tensor(xi[:, :], banks["b.x"][:, :], xs[:, :], ALU.mult).then_inc(d.done("xi"), 1)

                def zi_(t):
                    dve.wait_ge(*act.at("zs", t))
                    dve.wait_ge(*pool.at("y", t - 1))
                    dve.tensor_tensor(zi[:, :], banks["b.z"][:, :], zs[:, :], ALU.mult).then_inc(d.done("zi"), 1)

                def ag(t):
                    dve.wait_ge(*act.at("ae", t))
                    dve.tensor_scalar(ae[:, :], ae[:, :], float(np.exp(DECAY_FLOOR)), 1.0, ALU.min, ALU.add)\
                       .then_inc(d.done("ag"), 1)

                def BC(t):
                    dve.wait_ge(*p.at("bc", t))
                    dve.wait_ge(*p.at("gt", t - 1))
                    for n, (dst, table, mark) in enumerate(((Bt, lam_b, "Bt"), (Ct, lam_c, "Ct"))):
                        src = banks["b.bc"][:, n * NST:(n + 1) * NST].unsqueeze(1).broadcast_to([P, NLV, NST])
                        dve.tensor_tensor(dst[:, :, 0:NST], src, table[:, :, :], ALU.mult)\
                           .then_inc(d.done(mark), 1)

                def CD_(t):
                    dve.wait_ge(*act.at("BT", t))
                    dve.wait_ge(*p.at("G", t - 1))
                    dve.tensor_tensor(CD[:, :, :],
                                      banks["b.gt"][:, P:2 * P].unsqueeze(1).broadcast_to([P, NLV, P]),
                                      const("level_rows").unsqueeze(2).broadcast_to([P, NLV, P]), ALU.mult)\
                       .then_inc(d.done("CD"), 1)

                def Gm_(t):
                    dve.wait_ge(*p.at("G", t))
                    dve.wait_ge(*p.at("m3", t - 1))
                    dve.tensor_tensor(Gm[:, :, :], banks["b.G"][:, :].rearrange("p (l n) -> p l n", l=NLV),
                                      const("scan_mask").rearrange("p (l n) -> p l n", l=NLV), ALU.mult)\
                       .then_inc(d.done("Gm"), 1)

                def mix(l):
                    def run(t):
                        dve.wait_ge(*p.at(f"m{l}", t))
                        dve.wait_ge(*act.at(f"E{l}", t))
                        dve.tensor_tensor(tm[l][:, :], banks[f"b.m{l}"][:, :], Ef[l][:, :], ALU.mult)\
                           .then_inc(d.done(f"t{l}"), 1)
                    return run

                def x1_(t):
                    dve.wait_ge(*p.at("out", t))
                    dve.wait_ge(*pool.at("resid", t))
                    dve.wait_ge(*C.dve.at("x1c", t - 1))
                    dve.tensor_tensor(x1[:, :], banks["b.out"][:, 0:D], resid[:, :], ALU.add)\
                       .then_inc(d.done("x1"), 1)

                return {"xn": xn, "xg": xg, "zg": zg, "xi": xi_, "zi": zi_, "ag": ag, "BC": BC, "CD": CD_,
                        "Gm": Gm_, "x1": x1_} | {f"t{l}": mix(l) for l in range(NLV)}

            def experts():
                p, act, d = C.pe, C.act, C.dve

                def lg(t):
                    dve.wait_ge(*p.at("lg", t))
                    dve.wait_ge(*d.at("oh", t - 1))
                    dve.tensor_tensor(lb[:, :], banks["c.lg"][:, 0:NE], gate_b[:, :], ALU.add)\
                       .then_inc(d.done("lb"), 1)
                    dve.wait_ge(*d.at("lb", t))
                    dve.tensor_reduce(lm[:, :], lb[:, :], AX_X, ALU.max).then_inc(d.done("lm"), 1)
                    dve.wait_ge(*d.at("lm", t))
                    dve.tensor_scalar(ld[:, :], lb[:, :], lm[:, :], None, ALU.subtract).then_inc(d.done("ld"), 1)

                def oh_(t):
                    dve.wait_ge(*act.at("le", t))
                    dve.wait_ge(*d.at("ac7", t - 1))
                    dve.scalar_tensor_tensor(eq[:, :], le[:, :], 1.0, const("rank"), ALU.is_ge, ALU.mult)\
                       .then_inc(d.done("eq"), 1)
                    dve.wait_ge(*d.at("eq", t))
                    dve.tensor_reduce(em[:, :], eq[:, :], AX_X, ALU.max).then_inc(d.done("em"), 1)
                    dve.wait_ge(*d.at("em", t))
                    dve.wait_ge(*p.at("oT", t - 1))
                    dve.tensor_scalar(oh[:, :], eq[:, :], em[:, :], None, ALU.is_equal).then_inc(d.done("oh"), 1)

                def ac(e):
                    def run(t):
                        dve.wait_ge(*p.at(f"ex{e // 2}", t))
                        if e == 0:
                            dve.wait_ge(*d.at("oh", t))
                            dve.wait_ge(*out_stored.at(t - 1))
                        else:
                            dve.wait_ge(*d.at(f"ac{e - 1}", t))
                        src = C.xin if e == 0 else (acc2 if e % 2 == 0 else acc)
                        dst = acc if e % 2 == 0 else acc2
                        dve.scalar_tensor_tensor(dst[:, :], banks[f"c.ex{e // 2}"][:, (e % 2) * D:(e % 2 + 1) * D],
                                                 oh[:, e:e + 1], src[:, :], ALU.mult, ALU.add)\
                           .then_inc(d.done(f"ac{e}"), 1)
                    return run

                def out_(t):
                    dve.wait_ge(*p.at("eb", t))
                    dve.wait_ge(*d.at(f"ac{NE - 1}", t))
                    dve.tensor_tensor(yout[:, :], banks["c.eb"][:, 0:D], acc2[:, :], ALU.add)\
                       .then_inc(d.done("out"), 1)

                return {"lg": lg, "oh": oh_, "out": out_} | {f"ac{e}": ac(e) for e in range(NE)}

            def setup_weights(X, prep, scale):
                for k in range(KD):
                    dve.tensor_scalar(X.wq[:, k, :], X.wq[:, k, :], X.g[:, k:k + 1], scale, ALU.mult, ALU.mult)
                    for half in range(2):
                        dve.tensor_scalar(X.wkk[:, k, half, :], X.wkv[:, k, 0:DH], X.g[:, k:k + 1], None, ALU.mult)
                    dve.tensor_scalar(X.wv[:, k, :], X.wkv[:, k, DH:], X.g[:, k:k + 1], None, ALU.mult)

            def setup_a():
                dve.memset(eps5[:, :], 1.0e-5)
                dve.memset(eps6[:, :], 1.0e-6)
                dve.memset(A.K[:, :, :], 0.0)
                dve.memset(A.V[:, :, :], 0.0)
                dve.memset(C.K[:, :, :], 0.0)
                dve.memset(C.V[:, :, :], 0.0)
                dve.memset(Bt[:, :, :], 0.0)
                dve.memset(Ct[:, :, :], 0.0)
                dve.memset(ones_f[:, :], 1.0)
                dve.wait_ge(ld_const, 16)
                dve.wait_ge(ld_a, n_ld[ld_a.name])
                setup_weights(A, prep_a, float(DH) ** -0.5)
                dve.tensor_scalar(A.mask[:, :, :], A.mask_u8[:, :, :], -NEG, NEG, ALU.mult, ALU.add)\
                   .then_inc(prep_a, 1)
                dve.wait_ge(prep_a, 1)

            def setup_b():
                dve.wait_ge(ld_b, n_ld[ld_b.name])
                for k in range(KD):
                    dve.tensor_scalar(w_in[:, k, :], w_in[:, k, :], norm_w[:, k:k + 1], None, ALU.mult)
                dve.wait_ge(prep_lam, 1)
                dve.tensor_scalar(lam_g[:, :], lam_e[:, :], float(np.exp(LAMBDA_FLOOR)), 1.0, ALU.min, ALU.add)\
                   .then_inc(prep_lam_g, 1)
                dve.tensor_copy(ones_r[:, :], ones_f[:, :])
                dve.tensor_copy(a_bias_hi[:, :], a_bias[:, :]).then_inc(prep_lam_g, 1)
                dve.wait_ge(prep_lam_g, 2)
                dve.tensor_tensor(a_bias_lo[:, :], a_bias[:, :], a_bias_hi[:, :].bitcast(F32), ALU.subtract)\
                   .then_inc(prep_b, 1)
                dve.wait_ge(prep_lam, 2 + 2 * NLV)

            def setup_c():
                dve.wait_ge(ld_c, n_ld[ld_c.name])
                dve.tensor_tensor(nk_sq[:, :], nk_col[:, :], nk_col[:, :], ALU.mult).then_inc(prep_nk, 1)
                setup_weights(C, prep_c, 1.0)
                dve.tensor_scalar(C.mask[:, :, :], C.mask_u8[:, :, :], -NEG, NEG, ALU.mult, ALU.add)
                dve.wait_ge(prep_nk_pe, 1)
                dve.tensor_scalar(nk_ss[:, :], mlp_bank[0][:, 0:1], 1.0e-24, None, ALU.max).then_inc(prep_nk, 1)
                dve.tensor_scalar(kq[:, :], q_scale[:, :], k_scale[:, :], 8.0 * L2_SCALE, ALU.mult, ALU.mult)\
                   .then_inc(prep_nk, 1)
                dve.wait_ge(prep_nk, 3)
                dve.wait_ge(prep_nk_act, 2)
                dve.tensor_scalar(nk_n[:, :], nk_col[:, :], nk_r[:, :], kq[:, :], ALU.mult, ALU.mult)\
                   .then_inc(prep_c, 1)
                dve.wait_ge(prep_c, 1)

            def setup_mlp():
                d, bank = mlp_dve, mlp_bank
                dve.wait_ge(ld_mlp, n_ld[ld_mlp.name])
                dve.scalar_tensor_tensor(mh[0], m_w0, const("distance"), m_b0, ALU.mult, ALU.add)\
                   .then_inc(d.done("h0"), 1)
                for layer, (nrm, res, gain) in enumerate(((mh[1], mh[2], m_g0), (mh[4], mh[5], m_g1))):
                    dve.wait_ge(*d.at(f"h{layer}", 0))
                    dve.bn_stats(C.st[:, :], mh[0]).then_inc(d.done(f"st{layer}"), 1)
                    dve.wait_ge(*d.at(f"st{layer}", 0))
                    dve.bn_aggr(C.mv[:, :], C.st[:, :]).then_inc(d.done(f"mv{layer}"), 1)
                    dve.wait_ge(*mlp_act.at(f"r{layer}", 0))
                    dve.tensor_scalar(nrm, mh[0], C.mv[:, 0:1], C.rstd[:, :], ALU.subtract, ALU.mult)\
                       .then_inc(d.done(f"n{layer}"), 1)
                    dve.wait_ge(*d.at(f"n{layer}", 0))
                    dve.tensor_tensor(nrm, nrm, gain, ALU.mult).then_inc(d.done(f"v{layer}"), 1)
                    dve.wait_ge(*mlp_act.at(f"e{layer}", 0))
                    dve.tensor_scalar(mh[3], mh[3], GUARD, 1.0, ALU.min, ALU.add).then_inc(d.done(f"e{layer}"), 1)
                    dve.wait_ge(*mlp_act.at(f"s{layer}", 0))
                    dve.tensor_tensor(res, nrm, mh[3], ALU.mult).then_inc(d.done(f"s{layer}"), 1)
                    dve.wait_ge(*mlp_pe.at(f"T{layer}", 0))
                    dve.tensor_copy(mhT, bank[1][:, 0:D].rearrange("p (k n) -> p k n", k=KD))\
                       .then_inc(d.done(f"T{layer}"), 1)
                    if layer == 0:
                        dve.wait_ge(*mlp_pe.at("h1", 0))
                        dve.tensor_tensor(mh[0], bank[2][:, 0:D], m_b1, ALU.add).then_inc(d.done("h1"), 1)
                dve.wait_ge(*mlp_pe.at("pos", 0))
                dve.tensor_tensor(m_pos, bank[2][:, 0:H], m_b2, ALU.add).then_inc(d.done("pos"), 1)
                dve.wait_ge(*mlp_pe.at("posT", 0))
                dve.tensor_copy(m_posT, bank[1][0:H, 0:P]).then_inc(d.done("posT"), 1)

            def setup_bc():
                setup_b()
                setup_c()
                setup_mlp()

            iterations(dve, "dve", {"a": attention(A), "b": scan(), "c": attention(C) | experts()},
                       before={0: setup_a, 1: setup_bc})

        @block.gpsimd
        def _(pool):
            def attention(X):
                s, p, act, dve, g = X.name, X.pe, X.act, X.dve, X.pool

                def biasm(t):
                    if s == "a":
                        pool.wait_ge(*dve.at("S1", t - 1))
                    else:
                        pool.wait_ge(*g.at("addb", t - 1))
                    pool.tensor_tensor(X.biasm[:, :, :], X.bias[:, :, :],
                                       X.mask[:, t, :].unsqueeze(1).broadcast_to([P, H, S]), ALU.add)\
                        .then_inc(g.done("biasm"), 1)

                def qsq_(t):
                    pool.wait_ge(*act.at("q1", t))
                    pool.wait_ge(*p.at("O1", t - 1))
                    pool.tensor_tensor(qsq[:, :, :], X.qT[:, :, :], X.qT[:, :, :], ALU.mult)\
                        .then_inc(g.done("qsq"), 1)

                def addb(t):
                    pool.wait_ge(*g.at("biasm", t))
                    pool.wait_ge(*dve.at("S1", t))
                    pool.tensor_tensor(X.prob[:, :, :], X.prob[:, :, :], X.biasm[:, :, :], ALU.add)\
                        .then_inc(g.done("addb"), 1)

                def norm(t):
                    pool.wait_ge(*dve.at("rden", t))
                    pool.tensor_tensor(X.prob[:, :, :], X.prob[:, :, :],
                                       X.rden[:, :].unsqueeze(2).broadcast_to([P, H, S]), ALU.mult)\
                        .then_inc(g.done("norm"), 1)

                return {"biasm": biasm, "qsq": qsq_, "addb": addb, "norm": norm}

            def scan():
                p, act, dve, g = B.pe, B.act, B.dve, B.pool

                def resid_(t):
                    pool.wait_ge(*A.dve.at("c", t))
                    pool.wait_ge(*xres_loaded.at(t))
                    pool.wait_ge(*dve.at("x1", t - 1))
                    pool.tensor_tensor(resid[:, :], xres[:, :], A.c[:, :], ALU.add).then_inc(g.done("resid"), 1)

                def dx(t):
                    pool.wait_ge(*dve.at("xi", t))
                    pool.wait_ge(*p.at("yT", t - 1))
                    pool.tensor_tensor(y[:, :], xi[:, :], d_row[:, :], ALU.mult).then_inc(g.done("dx"), 1)

                def u_(l):
                    def run(t):
                        pool.wait_ge(*act.at("E0u" if l == 0 else f"E{l}", t))
                        pool.wait_ge(*p.at(f"m{l}", t - 1))
                        pool.wait_ge(*g.at(f"y{l}", t - 1))
                        pool.tensor_tensor(u[l][:, :], xi[:, :], (E0u if l == 0 else Ef[l])[:, :], ALU.mult)\
                            .then_inc(g.done(f"u{l}"), 1)
                    return run

                def mix(l):
                    def run(t):
                        pool.wait_ge(*g.at("dx" if l == 0 else f"y{l - 1}", t))
                        pool.wait_ge(*dve.at(f"t{l}", t))
                        pool.tensor_tensor(y[:, :], y[:, :], tm[l][:, :], ALU.add).then_inc(g.done(f"y{l}"), 1)
                    return run

                def gate(t):
                    pool.wait_ge(*g.at(f"y{NLV - 1}", t))
                    pool.wait_ge(*dve.at("zi", t))
                    pool.tensor_tensor(y[:, :], y[:, :], zi[:, :], ALU.mult).then_inc(g.done("y"), 1)

                return {"resid": resid_, "dx": dx, "y": gate} | {f"u{l}": u_(l) for l in range(NLV)}\
                    | {f"y{l}": mix(l) for l in range(NLV)}

            def fold_bias(X):
                done = sem("bias_folded_" + X.name)
                pool.tensor_tensor(X.bias[:, :, :], X.bias[:, :, :],
                                   X.null_bias[:, :].unsqueeze(2).broadcast_to([P, H, S]), ALU.subtract)\
                    .then_inc(done, 1)
                pool.wait_ge(done, 1)
                pool.tensor_tensor(X.bias[:, :, :], X.bias[:, :, :],
                                   const("causal").unsqueeze(1).broadcast_to([P, H, S]), ALU.add)\
                    .then_inc(done, 1)
                pool.wait_ge(done, 2)

            def setup_a():
                pool.wait_ge(ld_const, 16)
                pool.wait_ge(ld_a, n_ld[ld_a.name])
                fold_bias(A)
                pool.wait_ge(prep_a, 1)

            def setup_c():
                pool.wait_ge(ld_c, n_ld[ld_c.name])
                pool.wait_ge(mlp_dma, 16 + 16 * BT)
                fold_bias(C)
                pool.wait_ge(prep_c, 1)

            iterations(pool, "pool", {"a": attention(A), "b": scan(), "c": attention(C)},
                       before={0: setup_a, 1: lambda: pool.wait_ge(ld_b, n_ld[ld_b.name]), 2: setup_c})


_INS = ["cond_64", "fside_16xSxS_0", "mask_BxS_bk0", "mask_BxS_bf1",
        "L0_cond_g_in", "L0_cond_null_attn_bias", "L0_cond_Wq", "L0_cond_Wkv", "L0_cond_Wo", "L0_cond_g_out",
        "L0_attn_norm_w", "L0_attn_in_proj_w", "L0_attn_A_proj_w", "L0_attn_A_proj_b", "L0_attn_A_base",
        "L0_attn_B_proj_w", "L0_attn_C_proj_w", "L0_attn_D", "L0_attn_out_proj_w",
        "L0_cond2_g_norm", "L0_cond2_Wq", "L0_cond2_Wkv", "L0_cond2_q_scale", "L0_cond2_k_scale",
        "L0_cond2_null_attn_bias", "L0_cond2_w0", "L0_cond2_b0", "L0_cond2_g0", "L0_cond2_w1", "L0_cond2_b1",
        "L0_cond2_g1", "L0_cond2_w2", "L0_cond2_b2", "L0_cond2_Wout", "L0_cond2_g_out",
        "L0_ffn_gate_w", "L0_ffn_gate_b", "L0_ffn_expert_w", "L0_ffn_expert_b"]


def kernel(**inputs):
    import numpy as _np
    import concourse.bacc as _bacc
    from concourse import mybir as _mybir
    from concourse.bass_utils import run_bass_kernel_spmd as _run

    nc = _bacc.Bacc("TRN2", target_bir_lowering=False, num_devices=1)
    arrays, aps = {}, {}
    for name in ["x"] + _INS:
        a = _np.ascontiguousarray(inputs[name])
        arrays[f"in_{name}"] = a
        aps[name] = nc.dram_tensor(f"in_{name}", a.shape, _mybir.dt.from_np(a.dtype), kind="ExternalInput").ap()
    at, table = constants()
    arrays["in_constants"] = table
    table_ap = nc.dram_tensor("in_constants", table.shape, _mybir.dt.float32, kind="ExternalInput").ap()
    shape = inputs["x"].shape
    out = nc.dram_tensor("out_0", shape, _mybir.dt.float32, kind="ExternalOutput").ap()
    build(nc, aps["x"], out, aps, table_ap, at)
    r = _run(nc, [arrays], core_ids=[0])
    return r.results[0]["out_0"]
```

```python
from contextlib import ExitStack

import numpy as np

import concourse.bass as bass
from concourse import mybir

P = 128
S = 64
BT = P // S
D = 256
KD = D // P
H = 16
DH = 64
HP = H // 2
HI = H * S
E2 = 512
KE = E2 // P
NST = 16
NLV = 4
LVW = 32
NE = 8
NPOS = 2 * S - 1
NEG = -1.0e30
DECAY_FLOOR = 20.0
LAMBDA_FLOOR = 12.0
GUARD = float(2.0 ** 57)
L2_SCALE = float(2.0 ** 20)

ALU = mybir.AluOpType
ACT = mybir.ActivationFunctionType
F32 = mybir.dt.float32
F32R = mybir.dt.float32r
U8 = mybir.dt.uint8
AX_X = mybir.AxisListType.X


def constants():
    tok = np.arange(P)
    seq, pos = tok // S, tok % S
    same = seq[:, None] == seq[None, :]
    parts = {"ident": np.eye(P)}
    parts["causal"] = np.where(np.arange(S)[None, :] > pos[:, None], NEG, 0.0)
    half = (tok[:, None] // DH) == (tok[None, :] // DH)
    parts["halves"] = half * 1.0
    parts["pair"] = half[:, [0, DH]] * 1.0
    sums, count_b, count_c, masks = [], [], [], []
    r, t = pos[:, None], pos[None, :]
    ref = (t // 8) * 8 + 3
    sums.append(same * (1.0 * ((r > ref) & (r <= t)) - 1.0 * ((r > t) & (r <= ref))))
    count_c.append(pos - ((pos // 8) * 8 + 3))
    count_b.append(-count_c[0])
    masks.append(same & (r // 8 == t // 8) & (r <= t))
    for m in (8, 16, 32):
        left = (t // m) % 2 == 0
        start = (t // (2 * m)) * 2 * m + m
        sums.append(same * np.where(left, (r > t) & (r < start), (r >= start) & (r <= t)))
        start = (pos // (2 * m)) * 2 * m + m
        is_left = (pos // m) % 2 == 0
        count_b.append(np.where(is_left, start - 1 - pos, 0))
        count_c.append(np.where(is_left, 0, pos - start + 1))
        masks.append(same & (r // (2 * m) == t // (2 * m)) & ((r // m) % 2 == 0) & ((t // m) % 2 == 1))
    parts["neg_count_b"] = -np.stack(count_b, 1)
    parts["neg_count_c"] = -np.stack(count_c, 1)
    parts["scan_mask"] = np.concatenate(masks, 1)
    parts["level_rows"] = (tok[:, None] // LVW == np.arange(NLV)[None, :]) * 1.0
    parts["rank"] = np.broadcast_to(NE - np.arange(NE), (P, NE))
    parts["distance"] = (S - 1 - tok)[:, None]
    parts["sums"] = np.concatenate(sums, 1)
    at, n = {}, 0
    for name, a in parts.items():
        at[name] = (n, a.shape[1])
        n += a.shape[1]
    return at, np.concatenate([np.asarray(a, np.float32) for a in parts.values()], 1)

ORDER = {
    "pe": """
        a.q0@1 b.xt@2 c.ct@4 b.out@3 c.lg@4 b.x@2 b.z@2 c.oT@4 c.ex0@4 a.q1@1 a.S0@1 b.xiT@2
        c.xt@3 a.S1@1 c.kv@3 c.ex1@4 c.ks@3 c.q0@3 c.q1@3 b.a@2 c.ex2@4 c.qs@3 c.S0@3 c.S1@3
        b.bc@2 a.PT0@1 a.PT1@1 c.ex3@4 a.xt@0 b.gt@2 b.E0@2 a.O0@1 a.O1@1 b.E1@2 b.E2@2 b.E3@2
        b.G@2 a.kv@0 a.W@1 b.m0@2 b.m1@2 c.PT0@3 c.PT1@3 b.m2@2 c.O0@3 c.O1@3 b.m3@2 c.eb@4
        c.W@3 b.yT@2""",
    "act": """
        b.rms@2 c.rstd2@4 b.yT@3 c.cT@4 b.xnT@2 a.q0@1 c.le@4 b.xe@2 b.ze@2 c.oT@4 b.xs@2
        c.rstd@3 a.q1@1 c.xnT@3 b.zs@2 b.xiT@2 c.ksq@3 a.rstd@0 c.kr@3 c.q0@3 c.q1@3 a.expm@1
        a.prob@1 b.ae@2 c.qr@3 b.nl@2 a.PT0@1 a.PT1@1 b.BT@2 a.xnT@0 b.E0@2 a.O0@1 b.E0u@2
        a.O1@1 b.E1@2 c.expm@3 b.E2@2 b.E3@2 c.prob@3 c.PT0@3 c.PT1@3 c.O0@3 c.O1@3 a.rstd2@1""",
    "dve": """
        a.c@2 c.st2@4 b.xn@2 c.c@4 c.cl@4 b.yl@2 c.lg@4 b.x1@3 c.oh@4 b.xg@2 a.st@0 b.zg@2
        c.ac0@4 c.st@3 b.xi@2 c.mk@3 c.xn@3 a.S0@1 c.ac1@4 a.S1@1 c.kc@3 c.V@3 c.ks@3 b.zi@2
        c.ac2@4 c.ac3@4 b.xl@2 a.mx@1 a.sub@1 c.K@3 a.den@1 a.mk@0 c.ac4@4 c.qs@3 b.ag@2 c.S0@3
        c.S1@3 a.xn@0 b.nh@2 b.BC@2 c.ac5@4 c.ac6@4 b.CD@2 c.mx@3 c.sub@3 b.Gm@2 c.den@3 c.ac7@4
        a.K@0 a.V@0 b.t0@2 b.t1@2 b.t2@2 b.t3@2 a.st2@1 c.out@4""",
    "pool": """
        b.y@3 b.resid@2 a.addm@1 c.qsq@3 a.norm@1 c.addb@3 c.addm@3 b.dx@2 b.u0@2 b.u1@2 b.u2@2
        c.norm@3 b.u3@2 b.y0@2 b.y1@2 b.y2@2 b.y3@2""",
    "sp": """
        c.mask@4 b.xres@3 a.mask@1 a.x@1 c.store@5""",
}
RESULTS = {
    "act": {"rstd": "rstd_l rstd", "rms": "ss r_l r", "xs": "xl xs", "zs": "zl zs", "kr": "kr_l kr",
            "qr": "qr_l qr", "rstd2": "rstd2_l rstd2"},
    "dve": {"a.st": "st mv", "c.st": "x1c st mv", "K": "K0 K1", "c.K": "kn K0 K1", "V": "V0 V1",
            "mx": "mx mx0", "den": "sum den rden", "st2": "st2 mv2", "a.c": "cn c", "c.c": "cn",
            "BC": "Bt Ct", "nh": "nh nl",
            "lg": "lb lm ld", "oh": "eq em oh"},
}
TURNS = {
    0: """
        c.ks@3>dve.ks b.bc@2>dve.Ct a.xt@0>act.xnT a.kv@0>dve.V1 c.PT0@3>act.PT0 c.W@3>dve.cn""",
    1: """
        b.x@2>dve.xi c.xt@3>act.xnT c.kv@3>dve.V1 b.a@2>act.ae a.PT0@1>act.PT0 a.O1@1>act.O1
        b.yT@2>act.yT""",
    2: """
        b.z@2>dve.zi a.PT1@1>act.PT1 a.O0@1>act.O0 b.E2@2>act.E2 a.W@1>dve.cn""",
    3: """
        a.q1@1>act.q1 a.S1@1>dve.S1 c.q0@3>act.q0 c.S0@3>dve.S0 c.ex3@4>dve.ac7 b.m1@2>dve.t1
        b.m2@2>dve.t2""",
    4: """
        a.q0@1>act.q0 c.lg@4>dve.lb a.S0@1>dve.S0 c.ex1@4>dve.ac3 c.S1@3>dve.S1 b.E3@2>act.E3
        c.PT1@3>act.PT1 c.O1@3>act.O1""",
    5: """
        b.xt@2>dve.yl c.ex0@4>dve.ac1 c.q1@3>act.q1 c.ex2@4>dve.ac5 b.E0@2>act.E0u b.G@2>dve.Gm
        b.m3@2>dve.t3""",
    6: """
        b.out@3>dve.x1 c.qs@3>dve.qs c.O0@3>act.O0 c.eb@4>dve.out""",
    7: """
        c.ct@4>dve.cl c.oT@4>act.oT b.xiT@2>dve.xl b.gt@2>dve.CD b.E1@2>act.E1 b.m0@2>dve.t0""",
}
MLP_BANKS = (5, 6, 7)

MLP_DVE = ["h0", "st0", "mv0", "n0", "v0", "e0", "s0", "T0", "h1", "st1", "mv1", "n1", "v1", "e1", "s1", "T1",
           "pos", "posT"]
MLP_ACT = ["rl0", "r0", "e0", "l0", "s0", "rl1", "r1", "e1", "l1", "s1"]
MLP_PE = ["T0", "h1", "T1", "pos", "posT"]


def steps_of(engine):
    entries = [entry.replace("@", ".").split(".") for entry in ORDER[engine].split()]
    return [(s, step, int(lag)) for s, step, lag in entries]


def results_of(engine, stream):
    table, out = RESULTS.get(engine, {}), []
    for s, step, lag in steps_of(engine):
        if s == stream:
            names = table.get(f"{s}.{step}", table.get(step, step))
            out += [(name, lag) for name in names.split()]
    return out


ENGINES = ("pe", "act", "dve", "pool")
MAX_LAG = max(lag for e in ORDER for _, _, lag in steps_of(e))
LOOP_FROM = MAX_LAG + 1


class Progress:

    def __init__(self, sem, results, tiles=1):
        self.sem, self.tiles = sem, tiles
        self.lag, self.place = dict(results), {name: n for n, (name, _) in enumerate(results)}

    def at(self, name, t):
        i = t + self.lag[name]
        done = [(self.lag[n], self.place[n] <= self.place[name]) for n in self.place]
        if not isinstance(t, int):
            return self.sem, i * len(done) + sum(upto - lag for lag, upto in done)
        if t < 0:
            return self.sem, 0
        return self.sem, sum(min(max(i - lag + upto, 0), self.tiles) for lag, upto in done)

    def done(self, name):
        assert name in self.place, name
        return self.sem


class Transfers:

    def __init__(self, sem, name):
        self.sem, self.name = sem, name

    def at(self, t):
        return self.sem, max(16 * (t + 1), 0) if isinstance(t, int) else 16 * (t + 1)


class Stream:

    def __init__(self, s, sem, tiles):
        self.name = s
        self.pe, self.act, self.dve, self.pool = (
            Progress(sem(f"{s}_{e}_done"), results_of(e, s), tiles) for e in ENGINES)


class Banks:

    def __init__(self, tensors, streams, tiles):
        self.streams, self.tiles, self.bank, self.turns = streams, tiles, {}, {}
        for n, text in TURNS.items():
            turns = []
            for turn in text.split():
                key, lag, end = turn.replace("@", ">").split(">")
                turns.append((key, int(lag), *end.split(".")))
            for key, *_ in turns:
                self.bank[key], self.turns[key] = tensors[n], turns

    def __getitem__(self, key):
        return self.bank[key]

    def free(self, key, t):
        turns = self.turns[key]
        n = [k for k, *_ in turns].index(key)
        for back in range(1, 1 + len(turns) * (2 + MAX_LAG)):
            before, lag, engine, step = turns[(n - back) % len(turns)]
            tile = t + turns[n][1] + (n - back) // len(turns) - lag
            if not isinstance(tile, int) or 0 <= tile < self.tiles:
                break
        stream = self.streams[before[0]]
        return {"act": stream.act, "dve": stream.dve}[engine].at(step, tile)


def build(nc, x, out, ins, consts_dram, consts_at):
    NT = x.shape[0] * x.shape[1] // P
    ctx = ExitStack()
    with ctx:
        def sb(name, shape, dt=F32):
            return ctx.enter_context(nc.sbuf_tensor(name, shape, dt))

        def sem(name):
            return ctx.enter_context(nc.semaphore(name))

        A, B, C = (Stream(s, sem, NT) for s in "abc")
        psum = [ctx.enter_context(nc.psum_tensor(f"bank{n}", [P, 512], F32)) for n in range(8)]
        banks = Banks(psum, {"a": A, "b": B, "c": C}, NT)
        mlp_bank = [psum[n] for n in MLP_BANKS]

        n_consts = consts_at["sums"][0]
        consts = sb("consts", [P, n_consts])
        sums = sb("sums", [P, NLV * P], F32R)

        def const(name, rows=P):
            n, w = consts_at[name]
            return consts[0:rows, n:n + w]

        ident = const("ident")
        for X, s in ((A, "a"), (C, "c")):
            X.wq = sb(f"{s}_wq", [P, KD, H * DH])
            X.wkk = sb(f"{s}_wkk", [P, KD, 2, DH])
            X.wv = sb(f"{s}_wv", [P, KD, DH])
            X.wo = sb(f"{s}_wo", [P, HP, D])
            X.g = sb(f"{s}_g", [P, KD])
            X.null_bias = sb(f"{s}_null_bias", [P, H])
            X.bias = sb(f"{s}_bias", [P, H, S])
            X.mask_u8 = sb(f"{s}_mask_u8", [P, S], U8)
            X.mask = sb(f"{s}_mask", [P, S])
            X.xin = sb(f"{s}_xin", [P, D])
            X.st = sb(f"{s}_st", [P, 6])
            X.mv = sb(f"{s}_mv", [P, 2])
            X.rstd_l = sb(f"{s}_rstd_l", [P, 1])
            X.rstd = sb(f"{s}_rstd", [P, 1])
            X.xn = sb(f"{s}_xn", [P, D])
            X.xnT = sb(f"{s}_xnT", [P, KD, P])
            X.K = sb(f"{s}_K", [P, BT, P])
            X.V = sb(f"{s}_V", [P, BT, P])
            X.qT = sb(f"{s}_qT", [P, HP, P])
            X.prob = sb(f"{s}_prob", [P, H, S])
            X.mx = sb(f"{s}_mx", [P, H])
            X.mx0 = sb(f"{s}_mx0", [P, H])
            X.expm = sb(f"{s}_expm", [P, H])
            X.sum = sb(f"{s}_sum", [P, H])
            X.den = sb(f"{s}_den", [P, H])
            X.rden = sb(f"{s}_rden", [P, H])
            X.PT = X.qT
            X.OT = X.prob[:, :, :].rearrange("p (h two) s -> p h (two s)", two=2)
            X.st2 = sb(f"{s}_st2", [P, 6])
            X.mv2 = sb(f"{s}_mv2", [P, 2])
            X.rstd2_l = sb(f"{s}_rstd2_l", [P, 1])
            X.rstd2 = sb(f"{s}_rstd2", [P, 1])
            X.c = X.cn = sb(f"{s}_c", [P, D])
            X.wkv = X.PT[:, 0:KD, :]
        nk_col = sb("nk_col", [P, 1])
        nv_col = sb("nv_col", [P, 1])
        nv_row = sb("nv_row", [P, DH])
        eps5 = sb("eps5", [P, 1])
        wait_carrier = sb("wait_carrier", [P, 1])
        eps6 = sb("eps6", [P, 1])
        A.g_out = sb("a_g_out", [P, D])
        g_out_col = sb("g_out_col", [P, KD])
        def parts(name, shape):
            return sb(name + "_hi", shape, F32R), sb(name + "_lo", shape, F32R)

        w_in = parts("w_in", [P, KD, 2 * E2])
        w_a = parts("w_a", [P, KE, E2])
        w_bc = parts("w_bc", [P, KE, 2 * NST])
        w_out = sb("w_out", [P, KE, D])
        norm_w = sb("norm_w", [P, KD])
        a_bias_parts = sb("decay_bias", [33, E2], F32R)
        bias_ones = sb("bias_ones", [33, P], F32R)
        d_row = sb("d_row", [P, E2])
        a_base = sb("a_base", [P, NST])
        lam_e = sb("lam_e", [P, NST])
        lam_g = sb("lam_g", [P, NST])
        lam = sb("lam", [P, NST])
        lam_b = sb("lam_b", [P, NLV, NST])
        lam_c = sb("lam_c", [P, NLV, NST])
        xres = sb("xres", [P, D])
        resid = sb("resid", [P, D])
        ss = sb("ss", [P, 1])
        r_l = sb("r_l", [P, 1])
        r_ms = sb("r_ms", [P, 1])
        yn = sb("yn", [P, D])
        ynT = parts("ynT", [P, KD, P])
        xe = sb("xe", [P, E2])
        ze = sb("ze", [P, E2])
        xs, zs = xe, ze
        xi, zi = xe, ze
        xiT = parts("xiT", [P, KE, P])
        yT = sb("yT", [P, KE, P])
        nl = yT[:, :, :].rearrange("p k n -> p (k n)")
        nl_parts = parts("nl", [P, E2])
        ae = nl
        Bt = sb("Bt", [P, NLV, LVW])
        Ct = sb("Ct", [P, NLV, LVW])
        BTt = sb("BTt", [P, P])
        CD = sb("CD", [P, NLV, P])
        Gm = sb("Gm", [P, NLV, P])
        Ef = [sb(f"Ef{l}", [P, E2]) for l in range(NLV)]
        u = [sb(f"u{l}", [P, E2]) for l in range(NLV)]
        E0u = u[0]
        tm = u
        y = sb("y", [P, E2])
        a_bias = y[0:33, :]
        ones_f = yn[0:33, 0:P]
        x1 = sb("x1", [P, D])
        q_scale = sb("q_scale", [P, 1])
        k_scale = sb("k_scale", [P, 1])
        kq = sb("kq", [P, 1])
        nk_sq = sb("nk_sq", [P, 1])
        nk_ss = sb("nk_ss", [P, 1])
        nk_l = sb("nk_l", [P, 1])
        nk_r = sb("nk_r", [P, 1])
        nk_n = sb("nk_n", [P, 1])
        ksq = sb("ksq", [P, P])
        kss = sb("kss", [P, P])
        kraw = sb("kraw", [P, P])
        kr_l = kr = kn = kss
        qss = sb("qss", [P, H])
        qr_l = sb("qr_l", [P, H])
        qr = sb("qr", [P, H])
        gate_w = parts("gate_w", [P, KD, NE])
        gate_b = sb("gate_b", [P, NE])
        w_e = parts("w_e", [P, KD, NE, D])
        b_e = sb("b_e", [NE, D])
        cT = parts("cT", [P, KD, P])
        lb = sb("lb", [P, NE])
        lm = sb("lm", [P, 1])
        ld = sb("ld", [P, NE])
        le = sb("le", [P, NE])
        eq = sb("eq", [P, NE])
        em = sb("em", [P, 1])
        oh = sb("oh", [P, NE])
        ohT = sb("ohT", [NE, P])
        acc = sb("acc", [P, D])
        acc2 = C.cn
        yout = acc
        qsq = C.OT
        sums_staged = nl
        w_in_staged = [[xe[:, :], ze[:, :]], [u[1][:, :], u[2][:, :]]]
        w_a_staged = [u[3][:, :], C.prob[:, 0:8, :].rearrange("p h s -> p (h s)"),
                      C.prob[:, 8:16, :].rearrange("p h s -> p (h s)"),
                      C.qT[:, 4:8, :].rearrange("p h s -> p (h s)")]
        w_bc_staged = ksq[:, :].rearrange("p (k n) -> p k n", k=KE)
        gate_w_staged = kss[:, 0:KD * NE].rearrange("p (k n) -> p k n", k=KD)
        w_e_staged = w_in_staged[0] + w_in_staged[1] + w_a_staged
        w_e_staged = [[b.rearrange("p (e n) -> p e n", e=2) for b in w_e_staged[4 * k:4 * k + 4]] for k in range(KD)]
        m_w0, m_b0, m_g0 = Ef[0][:, 0:D], Ef[0][:, D:], Ef[1][:, 0:D]
        m_b1, m_g1 = Ef[1][:, D:], Ef[2][:, 0:D]
        m_w1 = u[0][:, :].rearrange("p (k n) -> p k n", k=KD)
        m_w2 = Ef[3][:, 0:KD * H].rearrange("p (k n) -> p k n", k=KD)
        m_b2 = Ef[3][:, 64:64 + H]
        mh = [CD[:, 0:2, :], CD[:, 2:4, :], Gm[:, 0:2, :], Gm[:, 2:4, :], y[:, 0:D], y[:, D:]]
        mh = [m.rearrange("p l n -> p (l n)") for m in mh[0:4]] + mh[4:]
        mhT = nl[:, 0:D].rearrange("p (k n) -> p k n", k=KD)
        m_pos = ksq[:, 0:H]
        m_posT = kraw[0:H, :]
        m_scr = nc.dram_tensor("position_rows", (H, S, NPOS), F32, kind="Internal").ap()

        ld_const, ld_a, ld_b, ld_mlp, ld_c = sem("ld_const"), sem("ld_a"), sem("ld_b"), sem("ld_mlp"), sem("ld_c")
        n_ld = {}

        def load(eng, s, dst, src):
            eng.dma_start(dst, src, allow_slow_non_contiguous=True).then_inc(s, 16)
            n_ld[s.name] = n_ld.get(s.name, 0) + 16

        prep_a, prep_b, prep_c = sem("prep_a"), sem("prep_b"), sem("prep_c")
        prep_lam = sem("prep_lam")
        prep_lam_g = sem("prep_lam_g")
        prep_pool_a, prep_pool_c = sem("prep_pool_a"), sem("prep_pool_c")
        ld_e, zeroed, split_b, split_c = sem("ld_e"), sem("zeroed"), sem("split_b"), sem("split_c")
        prep_nk, prep_nk_pe, prep_nk_act = sem("prep_nk"), sem("prep_nk_pe"), sem("prep_nk_act")
        mlp_dve = Progress(sem("mlp_dve"), [(name, 0) for name in MLP_DVE])
        mlp_act = Progress(sem("mlp_act"), [(name, 0) for name in MLP_ACT])
        mlp_pe = Progress(sem("mlp_pe"), [(name, 0) for name in MLP_PE])
        mlp_dma = sem("mlp_dma")
        x_loaded, xres_loaded, out_stored = (Transfers(sem(name), name)
                                             for name in ("x_loaded", "xres_loaded", "out_stored"))
        A.bias_folded, C.bias_folded = sem("bias_folded_a"), sem("bias_folded_c")
        A.mask_loaded = Transfers(sem("a_mask_loaded"), "a_mask_loaded")
        C.mask_loaded = Transfers(sem("c_mask_loaded"), "c_mask_loaded")

        xt_dram = x.rearrange("(t b) s d -> t (b s) d", b=BT)
        ot_dram = out.rearrange("(t b) s d -> t (b s) d", b=BT)

        def col(ap):
            return ap.rearrange("(k p) -> p k", p=P)

        def rows(ap, n=P):
            return ap.unsqueeze(0).broadcast_to([n, ap.shape[0]])

        null_k, null_v = ins["cond_64"][0], ins["cond_64"][1]

        block = ctx.enter_context(nc.Block())

        def iterations(eng, engine, steps, before=None):
            def run(i):
                for s, step, lag in steps_of(engine):
                    if not isinstance(i, int) or 0 <= i - lag < NT:
                        steps[s][step](i - lag)

            for i in range(LOOP_FROM):
                if before and i in before:
                    before[i]()
                run(i)
            with eng.Fori(LOOP_FROM, NT) as i:
                run(i)
            for i in range(NT, NT + MAX_LAG):
                run(i)

        @block.sync
        def _(sp):
            mask_a, mask_c = (ins[name].rearrange("(t b) j -> t b j", b=BT)
                              for name in ("mask_BxS_bk0", "mask_BxS_bf1"))

            def load_weights():
                load(sp, ld_const, consts[:, :], consts_dram[:, 0:n_consts])
                load(sp, ld_const, sums_staged[:, :], consts_dram[:, n_consts:])
                sp.dma_start(A.xin[:, :], xt_dram[0]).then_inc(x_loaded.sem, 16)
                for X, src in ((A, mask_a), (C, mask_c)):
                    sp.dma_start(X.mask_u8[:, :], src[0].unsqueeze(1).broadcast_to([BT, S, S]))\
                      .then_inc(X.mask_loaded.sem, 16)
                load(sp, ld_a, A.g[:, :], col(ins["L0_cond_g_in"]))
                load(sp, ld_a, A.wkv[:, :, :], ins["L0_cond_Wkv"].rearrange("(k p) n -> p k n", p=P))
                load(sp, ld_a, A.wq[:, :, :], ins["L0_cond_Wq"].rearrange("(k p) n -> p k n", p=P))
                load(sp, ld_a, nk_col[0:DH, :], null_k.unsqueeze(1))
                load(sp, ld_a, nk_col[DH:P, :], null_k.unsqueeze(1))
                load(sp, ld_a, nv_col[0:DH, :], null_v.unsqueeze(1))
                load(sp, ld_a, nv_col[DH:P, :], null_v.unsqueeze(1))
                load(sp, ld_a, nv_row[:, :], rows(null_v))
                load(sp, ld_a, A.null_bias[:, :], rows(ins["L0_cond_null_attn_bias"]))
                for b in range(BT):
                    part = slice(b * S, (b + 1) * S)
                    load(sp, ld_a, A.bias[part, :, :], ins["fside_16xSxS_0"].rearrange("h i j -> i h j"))
                load(sp, ld_a, A.wo[:, :, :], ins["L0_cond_Wo"].rearrange("(k p) n -> p k n", p=P))
                load(sp, ld_a, A.g_out[:, :], rows(ins["L0_cond_g_out"]))
                load(sp, ld_b, norm_w[:, :], col(ins["L0_attn_norm_w"]))
                for k in range(KD):
                    for n in range(2):
                        load(sp, ld_b, w_in_staged[k][n],
                             ins["L0_attn_in_proj_w"][k * P:(k + 1) * P, n * E2:(n + 1) * E2])
                for k in range(KE):
                    load(sp, ld_b, w_a_staged[k], ins["L0_attn_A_proj_w"][k * P:(k + 1) * P, :])
                load(sp, ld_b, w_bc_staged[:, :, 0:NST], ins["L0_attn_B_proj_w"].rearrange("(k p) n -> p k n", p=P))
                load(sp, ld_b, w_bc_staged[:, :, NST:], ins["L0_attn_C_proj_w"].rearrange("(k p) n -> p k n", p=P))
                load(sp, ld_b, w_out[:, :, :], ins["L0_attn_out_proj_w"].rearrange("(k p) n -> p k n", p=P))
                sp.wait_ge(zeroed, 1)
                for row in (0, 32):
                    load(sp, ld_b, a_bias[row:row + 1, :], ins["L0_attn_A_proj_b"].unsqueeze(0))
                load(sp, ld_b, d_row[:, :], rows(ins["L0_attn_D"]))
                load(sp, ld_b, a_base[:, :], rows(ins["L0_attn_A_base"]))
                load(sp, ld_mlp, m_w0, rows(ins["L0_cond2_w0"][0]))
                for dst, name in ((m_b0, "b0"), (m_g0, "g0"), (m_b1, "b1"), (m_g1, "g1"), (m_b2, "b2")):
                    load(sp, ld_mlp, dst, rows(ins["L0_cond2_" + name]))
                load(sp, ld_mlp, m_w1, ins["L0_cond2_w1"].rearrange("(k p) n -> p k n", p=P))
                load(sp, ld_mlp, m_w2, ins["L0_cond2_w2"].rearrange("(k p) n -> p k n", p=P))
                load(sp, ld_c, C.g[:, :], col(ins["L0_cond2_g_norm"]))
                load(sp, ld_c, C.wkv[:, :, :], ins["L0_cond2_Wkv"].rearrange("(k p) n -> p k n", p=P))
                load(sp, ld_c, C.wq[:, :, :], ins["L0_cond2_Wq"].rearrange("(k p) n -> p k n", p=P))
                for part in (slice(0, DH), slice(DH, P)):
                    load(sp, ld_c, q_scale[part, :], ins["L0_cond2_q_scale"].unsqueeze(1))
                    load(sp, ld_c, k_scale[part, :], ins["L0_cond2_k_scale"].unsqueeze(1))
                load(sp, ld_c, C.null_bias[:, :], rows(ins["L0_cond2_null_attn_bias"]))
                for b in range(BT):
                    part = slice(b * S, (b + 1) * S)
                load(sp, ld_c, C.wo[:, :, :], ins["L0_cond2_Wout"].rearrange("(k p) n -> p k n", p=P))
                load(sp, ld_c, g_out_col[:, :], col(ins["L0_cond2_g_out"]))
                load(sp, ld_c, gate_w_staged, ins["L0_ffn_gate_w"].rearrange("(k p) n -> p k n", p=P))
                load(sp, ld_c, gate_b[:, :], rows(ins["L0_ffn_gate_b"]))
                load(sp, ld_c, b_e[:, :], ins["L0_ffn_expert_b"])

            def load_experts():
                sp.wait_ge(split_b, 2)
                for k in range(KD):
                    for n in range(NE // 2):
                        load(sp, ld_e, w_e_staged[k][n],
                             ins["L0_ffn_expert_w"][2 * n:2 * n + 2, k * P:(k + 1) * P, :].rearrange("e p n -> p e n"))

            def position_bias():
                sp.wait_ge(*mlp_dve.at("posT", 0))
                sp.dma_start(m_scr, m_posT[:, 0:NPOS].unsqueeze(1).broadcast_to([H, S, NPOS])).then_inc(mlp_dma, 16)
                sp.wait_ge(mlp_dma, 16)
                flat = m_scr.rearrange("h i w -> h (i w)")[:, S - 1:S - 1 + S * (NPOS - 1)]
                skewed = flat.rearrange("h (i w) -> i h w", w=NPOS - 1)[:, :, 0:S]
                for b in range(BT):
                    sp.dma_start(C.bias[b * S:(b + 1) * S, :, :], skewed).then_inc(mlp_dma, 16)

            def load_x(t):
                if isinstance(t, int) and t == 0:
                    return
                sp.wait_ge(*A.dve.at("xn", t - 1))
                sp.dma_start(A.xin[:, :], xt_dram[t]).then_inc(x_loaded.sem, 16)

            def load_xres(t):
                sp.wait_ge(*B.pool.at("resid", t - 1))
                sp.dma_start(xres[:, :], xt_dram[t]).then_inc(xres_loaded.sem, 16)

            def store(t):
                sp.wait_ge(*C.dve.at("out", t))
                sp.dma_start(ot_dram[t], yout[:, :]).then_inc(out_stored.sem, 16)

            def load_mask(X, src):
                def run(t):
                    if isinstance(t, int) and t == 0:
                        return
                    sp.wait_ge(*X.dve.at("mk", t - 1))
                    sp.dma_start(X.mask_u8[:, :], src[t].unsqueeze(1).broadcast_to([BT, S, S]))\
                      .then_inc(X.mask_loaded.sem, 16)
                return run

            steps = {"a": {"x": load_x, "mask": load_mask(A, mask_a)}, "b": {"xres": load_xres},
                     "c": {"store": store, "mask": load_mask(C, mask_c)}}
            iterations(sp, "sp", steps, before={0: load_weights, 3: load_experts, 4: position_bias})
            sp.wait_ge(*out_stored.at(NT - 1))

        @block.tensor
        def _(pe):
            def product(out, lhs, rhs, k, first, last):
                pe.matmul(out, lhs[0][:, k, :], rhs[0], start=first, stop=False)
                pe.matmul(out, lhs[0][:, k, :], rhs[1], start=False, stop=False)
                return pe.matmul(out, lhs[1][:, k, :], rhs[0], start=False, stop=last)

            def attention(X):
                s, p, act, dve, pool = X.name, X.pe, X.act, X.dve, X.pool

                def bank(unit):
                    return banks[f"{s}.{unit}"]

                def xt(t):
                    pe.wait_ge(*banks.free(f"{s}.xt", t))
                    pe.wait_ge(*dve.at("xn", t))
                    for k in range(KD):
                        mm = pe.transpose(bank("xt")[:, k * P:(k + 1) * P], X.xn[:, k * P:(k + 1) * P], ident)
                    mm.then_inc(p.done("xt"), 1)

                def kv(t):
                    pe.wait_ge(*banks.free(f"{s}.kv", t))
                    pe.wait_ge(*act.at("xnT", t))
                    for k in range(KD):
                        pe.matmul(bank("kv")[:, 0:P], X.wkk[:, k, :, :], X.xnT[:, k, :],
                                  start=k == 0, stop=k == KD - 1)
                    for b in range(BT):
                        for k in range(KD):
                            for half in range(2):
                                mm = pe.matmul(bank("kv")[half * S:(half + 1) * S, P + b * DH:P + (b + 1) * DH],
                                               X.xnT[:, k, b * S:(b + 1) * S], X.wv[:, k, :],
                                               start=k == 0, stop=k == KD - 1)
                    mm.then_inc(p.done("kv"), 1)

                def ks(t):
                    pe.wait_ge(*banks.free(f"{s}.ks", t))
                    pe.wait_ge(*act.at("ksq", t))
                    pe.matmul(bank("ks")[:, 0:P], const("halves"), ksq[:, :], start=True, stop=True)\
                      .then_inc(p.done("ks"), 1)

                def q(half):
                    def run(t):
                        pe.wait_ge(*banks.free(f"{s}.q{half}", t))
                        for m in range(4):
                            hp = 4 * half + m
                            for k in range(KD):
                                mm = pe.matmul(bank(f"q{half}")[:, m * P:(m + 1) * P],
                                               X.wq[:, k, hp * P:(hp + 1) * P], X.xnT[:, k, :],
                                               start=k == 0, stop=k == KD - 1)
                        mm.then_inc(p.done(f"q{half}"), 1)
                    return run

                def qs(t):
                    pe.wait_ge(*banks.free(f"{s}.qs", t))
                    pe.wait_ge(*pool.at("qsq", t))
                    for hp in range(HP):
                        mm = pe.matmul(bank("qs")[:, 2 * hp:2 * hp + 2], qsq[:, hp, :], const("pair"),
                                       start=True, stop=True)
                    mm.then_inc(p.done("qs"), 1)

                def scores(half):
                    def run(t):
                        pe.wait_ge(*banks.free(f"{s}.S{half}", t))
                        if half == 0:
                            pe.wait_ge(*dve.at("K1", t))
                        pe.wait_ge(*act.at(f"q{half}", t))
                        for m in range(4):
                            for b in range(BT):
                                mm = pe.matmul(bank(f"S{half}")[b * S:(b + 1) * S, m * P:(m + 1) * P],
                                               X.qT[:, 4 * half + m, b * S:(b + 1) * S], X.K[:, b, :],
                                               start=True, stop=True)
                        mm.then_inc(p.done(f"S{half}"), 1)
                    return run

                def PT(half):
                    def run(t):
                        pe.wait_ge(*banks.free(f"{s}.PT{half}", t))
                        if half == 0:
                            pe.wait_ge(*pool.at("norm", t))
                        for m in range(4):
                            hp = 4 * half + m
                            mm = pe.transpose(bank(f"PT{half}")[:, m * P:(m + 1) * P],
                                              X.prob[:, 2 * hp:2 * hp + 2, :], ident)
                        mm.then_inc(p.done(f"PT{half}"), 1)
                    return run

                def PV(b):
                    def run(t):
                        pe.wait_ge(*banks.free(f"{s}.O{b}", t))
                        if b == 0:
                            pe.wait_ge(*dve.at("V1", t))
                            pe.wait_ge(*act.at("PT1", t))
                        pe.matmul(bank(f"O{b}")[:, :], X.V[:, b, :], X.PT[:, :, b * S:(b + 1) * S],
                                  start=True, stop=True).then_inc(p.done(f"O{b}"), 1)
                    return run

                def W(t):
                    pe.wait_ge(*banks.free(f"{s}.W", t))
                    pe.wait_ge(*act.at("O1", t))
                    for hp in range(HP):
                        mm = pe.matmul(bank("W")[:, 0:D], X.OT[:, hp, :], X.wo[:, hp, :],
                                       start=hp == 0, stop=hp == HP - 1)
                    mm.then_inc(p.done("W"), 1)

                return {"xt": xt, "kv": kv, "ks": ks, "q0": q(0), "q1": q(1), "qs": qs, "S0": scores(0),
                        "S1": scores(1), "PT0": PT(0), "PT1": PT(1), "O0": PV(0), "O1": PV(1), "W": W}

            def scan():
                p, act, dve, pool = B.pe, B.act, B.dve, B.pool

                def xt(t):
                    pe.wait_ge(*banks.free("b.xt", t))
                    pe.wait_ge(*dve.at("xn", t))
                    for k in range(KD):
                        mm = pe.transpose(banks["b.xt"][:, k * P:(k + 1) * P], yn[:, k * P:(k + 1) * P], ident)
                    mm.then_inc(p.done("xt"), 1)

                def proj(n, unit):
                    def run(t):
                        pe.wait_ge(*banks.free(f"b.{unit}", t))
                        if unit == "x":
                            pe.wait_ge(*dve.at("yl", t))
                        cols = slice(n * E2, (n + 1) * E2)
                        for k in range(KD):
                            mm = product(banks[f"b.{unit}"][:, :], ynT, [w[:, k, cols] for w in w_in], k,
                                         k == 0, k == KD - 1)
                        mm.then_inc(p.done(unit), 1)
                    return run

                def xiT_(t):
                    pe.wait_ge(*banks.free("b.xiT", t))
                    pe.wait_ge(*dve.at("xi", t))
                    for k in range(KE):
                        mm = pe.transpose(banks["b.xiT"][:, k * P:(k + 1) * P], xi[:, k * P:(k + 1) * P], ident)
                    mm.then_inc(p.done("xiT"), 1)

                def a(t):
                    pe.wait_ge(*banks.free("b.a", t))
                    pe.wait_ge(*dve.at("xl", t))
                    for k in range(KE):
                        product(banks["b.a"][:, :], xiT, [w[:, k, :] for w in w_a], k, k == 0, False)
                    pe.matmul(banks["b.a"][:, :], bias_ones[:, :], a_bias_parts[:, :], start=False, stop=True)\
                      .then_inc(p.done("a"), 1)

                def bc(t):
                    pe.wait_ge(*banks.free("b.bc", t))
                    for k in range(KE):
                        mm = product(banks["b.bc"][:, 0:2 * NST], xiT, [w[:, k, :] for w in w_bc], k,
                                     k == 0, k == KE - 1)
                    mm.then_inc(p.done("bc"), 1)

                def gt(t):
                    pe.wait_ge(*banks.free("b.gt", t))
                    pe.wait_ge(*dve.at("Ct", t))
                    pe.transpose(banks["b.gt"][:, 0:P], Bt[:, :, :], ident)
                    pe.transpose(banks["b.gt"][:, P:2 * P], Ct[:, :, :], ident).then_inc(p.done("gt"), 1)

                def G(t):
                    pe.wait_ge(*banks.free("b.G", t))
                    pe.wait_ge(*dve.at("CD", t))
                    pe.matmul(banks["b.G"][:, :], BTt[:, :], CD[:, :, :], start=True, stop=True)\
                      .then_inc(p.done("G"), 1)

                def E(l):
                    def run(t):
                        pe.wait_ge(*banks.free(f"b.E{l}", t))
                        if l == 0:
                            pe.wait_ge(*dve.at("nl", t))
                        for n, part in enumerate(nl_parts):
                            mm = pe.matmul(banks[f"b.E{l}"][:, :], sums[:, l * P:(l + 1) * P], part[:, :],
                                           start=n == 0, stop=n == 1)
                        mm.then_inc(p.done(f"E{l}"), 1)
                    return run

                def mix(l):
                    def run(t):
                        pe.wait_ge(*banks.free(f"b.m{l}", t))
                        if l == 0:
                            pe.wait_ge(*dve.at("Gm", t))
                        pe.wait_ge(*pool.at(f"u{l}", t))
                        pe.matmul(banks[f"b.m{l}"][:, :], Gm[:, l, :], u[l][:, :],
                                  start=True, stop=True).then_inc(p.done(f"m{l}"), 1)
                    return run

                def yT_(t):
                    pe.wait_ge(*banks.free("b.yT", t))
                    pe.wait_ge(*pool.at("y", t))
                    for k in range(KE):
                        mm = pe.transpose(banks["b.yT"][:, k * P:(k + 1) * P], y[:, k * P:(k + 1) * P], ident)
                    mm.then_inc(p.done("yT"), 1)

                def out_(t):
                    pe.wait_ge(*banks.free("b.out", t))
                    pe.wait_ge(*act.at("yT", t))
                    for k in range(KE):
                        mm = pe.matmul(banks["b.out"][:, 0:D], yT[:, k, :], w_out[:, k, :],
                                       start=k == 0, stop=k == KE - 1)
                    mm.then_inc(p.done("out"), 1)

                return {"xt": xt, "x": proj(0, "x"), "z": proj(1, "z"), "xiT": xiT_, "a": a, "bc": bc, "gt": gt,
                        "G": G, "yT": yT_, "out": out_} | {f"E{l}": E(l) for l in range(NLV)}\
                    | {f"m{l}": mix(l) for l in range(NLV)}

            def experts():
                p, act, dve = C.pe, C.act, C.dve

                def ct(t):
                    pe.wait_ge(*banks.free("c.ct", t))
                    pe.wait_ge(*dve.at("cn", t))
                    for k in range(KD):
                        mm = pe.transpose(banks["c.ct"][:, k * P:(k + 1) * P], C.c[:, k * P:(k + 1) * P], ident)
                    mm.then_inc(p.done("ct"), 1)

                def lg(t):
                    pe.wait_ge(*banks.free("c.lg", t))
                    pe.wait_ge(*dve.at("cl", t))
                    for k in range(KD):
                        mm = product(banks["c.lg"][:, 0:NE], cT, [w[:, k, :] for w in gate_w], k,
                                     k == 0, k == KD - 1)
                    mm.then_inc(p.done("lg"), 1)

                def oT(t):
                    pe.wait_ge(*banks.free("c.oT", t))
                    pe.wait_ge(*dve.at("oh", t))
                    pe.transpose(banks["c.oT"][0:NE, 0:P], oh[:, :], ident).then_inc(p.done("oT"), 1)

                def ex(n):
                    def run(t):
                        pe.wait_ge(*banks.free(f"c.ex{n}", t))
                        for k in range(KD):
                            mm = product(banks[f"c.ex{n}"][:, :], cT, [w[:, k, 2 * n:2 * n + 2, :] for w in w_e],
                                         k, k == 0, k == KD - 1)
                        mm.then_inc(p.done(f"ex{n}"), 1)
                    return run

                def eb(t):
                    pe.wait_ge(*banks.free("c.eb", t))
                    pe.wait_ge(*act.at("oT", t))
                    pe.matmul(banks["c.eb"][:, 0:D], ohT[:, :], b_e[:, :], start=True, stop=True)\
                      .then_inc(p.done("eb"), 1)

                return {"ct": ct, "lg": lg, "oT": oT, "eb": eb} | {f"ex{n}": ex(n) for n in range(NE // 2)}

            pe.wait_ge(ld_const, n_ld[ld_const.name])
            pe.wait_ge(prep_a, 1)

            def setup_bc():
                bank = mlp_bank
                pe.wait_ge(prep_nk, 1)
                pe.matmul(bank[0][:, 0:1], const("halves"), nk_sq[:, :], start=True, stop=True)\
                  .then_inc(prep_nk_pe, 1)
                for layer in range(2):
                    pe.wait_ge(*mlp_dve.at(f"s{layer}", 0))
                    src = mh[2] if layer == 0 else mh[5]
                    for k in range(KD):
                        mm = pe.transpose(bank[1][:, k * P:(k + 1) * P], src[:, k * P:(k + 1) * P], ident)
                    mm.then_inc(mlp_pe.done(f"T{layer}"), 1)
                    pe.wait_ge(*mlp_dve.at(f"T{layer}", 0))
                    w, n = (m_w1, D) if layer == 0 else (m_w2, H)
                    for k in range(KD):
                        mm = pe.matmul(bank[2][:, 0:n], mhT[:, k, :], w[:, k, :],
                                       start=k == 0, stop=k == KD - 1)
                    mm.then_inc(mlp_pe.done("h1" if layer == 0 else "pos"), 1)
                pe.wait_ge(*mlp_dve.at("pos", 0))
                pe.transpose(bank[1][0:H, 0:P], m_pos, ident).then_inc(mlp_pe.done("posT"), 1)
                pe.wait_ge(*mlp_dve.at("posT", 0))
                pe.wait_ge(prep_b, 1)
                pe.wait_ge(prep_c, 1)
                pe.wait_ge(split_c, 2)

            iterations(pe, "pe", {"a": attention(A), "b": scan(), "c": attention(C) | experts()},
                       before={2: setup_bc})

        @block.scalar
        def _(act):
            def rstd_of(X, t, src, mid, dst, mark_l, mark):
                act.activation(mid[:, :], src[:, 1:2], ACT.Ln, bias=eps5[:, :]).then_inc(X.act.done(mark_l), 1)
                act.wait_ge(*X.act.at(mark_l, t))
                act.activation(dst[:, :], mid[:, :], ACT.Exp, scale=-0.5).then_inc(X.act.done(mark), 1)

            def attention(X):
                s, p, a, dve, pool = X.name, X.pe, X.act, X.dve, X.pool

                def rstd(t):
                    act.wait_ge(*dve.at("mv", t))
                    act.wait_ge(*dve.at("xn", t - 1))
                    rstd_of(X, t, X.mv, X.rstd_l, X.rstd, "rstd_l", "rstd")

                def xnT(t):
                    act.wait_ge(*p.at("xt", t))
                    act.wait_ge(*p.at("q1", t - 1))
                    act.copy(X.xnT[:, :, :], banks[f"{s}.xt"][:, 0:D]).then_inc(a.done("xnT"), 1)

                def ksq_(t):
                    act.wait_ge(*p.at("kv", t))
                    act.wait_ge(*p.at("ks", t - 1))
                    act.activation(ksq[:, :], banks["c.kv"][:, 0:P], ACT.Square).then_inc(a.done("ksq"), 1)

                def kr_(t):
                    act.wait_ge(*dve.at("ks", t))
                    act.activation(kr_l[:, :], kss[:, :], ACT.Ln, scale=L2_SCALE).then_inc(a.done("kr_l"), 1)
                    act.wait_ge(*a.at("kr_l", t))
                    act.activation(kr[:, :], kr_l[:, :], ACT.Exp, scale=-0.5).then_inc(a.done("kr"), 1)

                def q(half):
                    def run(t):
                        act.wait_ge(*p.at(f"q{half}", t))
                        act.wait_ge(*p.at("O1", t - 1))
                        act.copy(X.qT[:, 4 * half:4 * half + 4, :], banks[f"{s}.q{half}"][:, :])\
                           .then_inc(a.done(f"q{half}"), 1)
                    return run

                def qr_(t):
                    act.wait_ge(*dve.at("qs", t))
                    act.activation(qr_l[:, :], qss[:, :], ACT.Ln, scale=L2_SCALE).then_inc(a.done("qr_l"), 1)
                    act.wait_ge(*a.at("qr_l", t))
                    act.wait_ge(*dve.at("S1", t - 1))
                    act.activation(qr[:, :], qr_l[:, :], ACT.Exp, scale=-0.5).then_inc(a.done("qr"), 1)

                def expm(t):
                    act.wait_ge(*dve.at("mx0", t))
                    act.wait_ge(*dve.at("den", t - 1))
                    act.activation(X.expm[:, :], X.mx0[:, :], ACT.Exp, scale=-1.0).then_inc(a.done("expm"), 1)

                def prob(t):
                    act.wait_ge(*dve.at("sub", t))
                    act.activation(X.prob[:, :, :], X.prob[:, :, :], ACT.Exp).then_inc(a.done("prob"), 1)

                def PT(half):
                    def run(t):
                        act.wait_ge(*p.at(f"PT{half}", t))
                        act.copy(X.PT[:, 4 * half:4 * half + 4, :], banks[f"{s}.PT{half}"][:, :])\
                           .then_inc(a.done(f"PT{half}"), 1)
                    return run

                def PV(b):
                    def run(t):
                        act.wait_ge(*p.at(f"O{b}", t))
                        act.activation(X.OT[:, :, b * S:(b + 1) * S],
                                       banks[f"{s}.O{b}"][:, :].rearrange("p (h i) -> p h i", h=HP),
                                       ACT.Identity, bias=nv_col[:, :]).then_inc(a.done(f"O{b}"), 1)
                    return run

                def rstd2(t):
                    act.wait_ge(*dve.at("mv2", t))
                    act.wait_ge(*dve.at("cn", t - 1))
                    rstd_of(X, t, X.mv2, X.rstd2_l, X.rstd2, "rstd2_l", "rstd2")

                return {"rstd": rstd, "xnT": xnT, "ksq": ksq_, "kr": kr_, "q0": q(0), "q1": q(1), "qr": qr_,
                        "expm": expm, "prob": prob, "PT0": PT(0), "PT1": PT(1), "O0": PV(0), "O1": PV(1),
                        "rstd2": rstd2}

            def scan():
                p, a, dve, pool = B.pe, B.act, B.dve, B.pool

                def rms(t):
                    act.wait_ge(*A.dve.at("c", t))
                    act.wait_ge(*p.at("xt", t - 1))
                    act.activation(yn[:, :], A.c[:, :], ACT.Square, accum_out=ss[:, :])\
                       .then_inc(a.done("ss"), 1)
                    act.wait_ge(*a.at("ss", t))
                    act.activation(r_l[:, :], ss[:, :], ACT.Ln, scale=1.0 / D, bias=eps6[:, :])\
                       .then_inc(a.done("r_l"), 1)
                    act.wait_ge(*a.at("r_l", t))
                    act.wait_ge(*dve.at("xn", t - 1))
                    act.activation(r_ms[:, :], r_l[:, :], ACT.Exp, scale=-0.5).then_inc(a.done("r"), 1)

                def xnT(t):
                    act.wait_ge(*p.at("xt", t))
                    act.wait_ge(*p.at("z", t - 1))
                    act.copy(ynT[0][:, :, :], banks["b.xt"][:, 0:D]).then_inc(a.done("xnT"), 1)

                def exp_x(t):
                    act.wait_ge(*p.at("x", t))
                    act.wait_ge(*p.at("xiT", t - 1))
                    act.wait_ge(*pool.at("u3", t - 1))
                    act.activation(xe[:, :], banks["b.x"][:, :], ACT.Exp, scale=-1.0).then_inc(a.done("xe"), 1)

                def exp_z(t):
                    act.wait_ge(*p.at("z", t))
                    act.wait_ge(*pool.at("y", t - 1))
                    act.activation(ze[:, :], banks["b.z"][:, :], ACT.Exp, scale=-1.0).then_inc(a.done("ze"), 1)

                def sig_x(t):
                    act.wait_ge(*dve.at("xg", t))
                    act.activation(xe[:, :], xe[:, :], ACT.Ln).then_inc(a.done("xl"), 1)
                    act.wait_ge(*a.at("xl", t))
                    act.activation(xs[:, :], xe[:, :], ACT.Exp, scale=-1.0).then_inc(a.done("xs"), 1)

                def sig_z(t):
                    act.wait_ge(*dve.at("zg", t))
                    act.activation(ze[:, :], ze[:, :], ACT.Ln).then_inc(a.done("zl"), 1)
                    act.wait_ge(*a.at("zl", t))
                    act.activation(zs[:, :], ze[:, :], ACT.Exp, scale=-1.0).then_inc(a.done("zs"), 1)

                def xiT_(t):
                    act.wait_ge(*p.at("xiT", t))
                    act.wait_ge(*p.at("bc", t - 1))
                    act.copy(xiT[0][:, :, :], banks["b.xiT"][:, :]).then_inc(a.done("xiT"), 1)

                def exp_a(t):
                    act.wait_ge(*p.at("a", t))
                    act.wait_ge(*p.at("out", t - 1))
                    act.activation(ae[:, :], banks["b.a"][:, :], ACT.Exp, scale=-1.0).then_inc(a.done("ae"), 1)

                def log_a(t):
                    act.wait_ge(*dve.at("ag", t))
                    act.activation(nl[:, :], ae[:, :], ACT.Ln).then_inc(a.done("nl"), 1)

                def BT_(t):
                    act.wait_ge(*p.at("gt", t))
                    act.wait_ge(*p.at("G", t - 1))
                    act.copy(BTt[:, :], banks["b.gt"][:, 0:P]).then_inc(a.done("BT"), 1)

                def E0u_(t):
                    act.wait_ge(*p.at("E0", t))
                    act.wait_ge(*pool.at("y0", t - 1))
                    act.activation(E0u[:, :], banks["b.E0"][:, :], ACT.Exp).then_inc(a.done("E0u"), 1)

                def E(l):
                    def run(t):
                        act.wait_ge(*p.at(f"E{l}", t))
                        act.wait_ge(*dve.at(f"t{l}", t - 1))
                        if l:
                            act.wait_ge(*pool.at(f"u{l}", t - 1))
                        act.activation(Ef[l][:, :], banks[f"b.E{l}"][:, :], ACT.Exp, scale=-1.0)\
                           .then_inc(a.done(f"E{l}"), 1)
                    return run

                def yT_(t):
                    act.wait_ge(*p.at("yT", t))
                    act.wait_ge(*p.at("out", t - 1))
                    act.copy(yT[:, :, :], banks["b.yT"][:, :]).then_inc(a.done("yT"), 1)

                return {"rms": rms, "xnT": xnT, "xe": exp_x, "ze": exp_z, "xs": sig_x, "zs": sig_z, "xiT": xiT_,
                        "ae": exp_a, "nl": log_a, "BT": BT_, "E0u": E0u_, "yT": yT_}\
                    | {f"E{l}": E(l) for l in range(NLV)}

            def experts():
                p, a, dve = C.pe, C.act, C.dve

                def cT_(t):
                    act.wait_ge(*p.at("ct", t))
                    act.wait_ge(*p.at("ex3", t - 1))
                    act.copy(cT[0][:, :, :], banks["c.ct"][:, 0:D]).then_inc(a.done("cT"), 1)

                def le_(t):
                    act.wait_ge(*dve.at("ld", t))
                    act.activation(le[:, :], ld[:, :], ACT.Exp).then_inc(a.done("le"), 1)

                def oT(t):
                    act.wait_ge(*p.at("oT", t))
                    act.wait_ge(*p.at("eb", t - 1))
                    act.copy(ohT[:, :], banks["c.oT"][0:NE, 0:P]).then_inc(a.done("oT"), 1)

                return {"cT": cT_, "le": le_, "oT": oT}

            act.preload_act_table_set("natural_log_exp_and_others")

            def setup_a():
                act.wait_ge(ld_a, n_ld[ld_a.name])
                act.wait_ge(prep_a, 1)

            def setup_bc():
                act.wait_ge(ld_b, n_ld[ld_b.name])
                act.activation(lam_e[:, :], a_base[:, :], ACT.Exp, scale=-1.0).then_inc(prep_lam, 1)
                act.wait_ge(prep_lam_g, 1)
                act.activation(lam[:, :], lam_g[:, :], ACT.Ln).then_inc(prep_lam, 1)
                act.wait_ge(prep_lam, 2)
                for l in range(NLV):
                    act.activation(lam_b[:, l, :], lam[:, :], ACT.Exp, scale=const("neg_count_b")[:, l:l + 1])\
                       .then_inc(prep_lam, 1)
                    act.activation(lam_c[:, l, :], lam[:, :], ACT.Exp, scale=const("neg_count_c")[:, l:l + 1])\
                       .then_inc(prep_lam, 1)
                act.wait_ge(prep_nk, 2)
                act.activation(nk_l[:, :], nk_ss[:, :], ACT.Ln, scale=L2_SCALE).then_inc(prep_nk_act, 1)
                act.wait_ge(prep_nk_act, 1)
                act.activation(nk_r[:, :], nk_l[:, :], ACT.Exp, scale=-0.5).then_inc(prep_nk_act, 1)
                for layer in range(2):
                    act.wait_ge(*mlp_dve.at(f"mv{layer}", 0))
                    act.activation(C.rstd_l[:, :], C.mv[:, 1:2], ACT.Ln, bias=eps5[:, :])\
                       .then_inc(mlp_act.done(f"rl{layer}"), 1)
                    act.wait_ge(*mlp_act.at(f"rl{layer}", 0))
                    act.activation(C.rstd[:, :], C.rstd_l[:, :], ACT.Exp, scale=-0.5)\
                       .then_inc(mlp_act.done(f"r{layer}"), 1)
                    v = mh[1] if layer == 0 else mh[4]
                    act.wait_ge(*mlp_dve.at(f"v{layer}", 0))
                    act.activation(mh[3], v, ACT.Exp, scale=-1.0).then_inc(mlp_act.done(f"e{layer}"), 1)
                    act.wait_ge(*mlp_dve.at(f"e{layer}", 0))
                    act.activation(mh[3], mh[3], ACT.Ln).then_inc(mlp_act.done(f"l{layer}"), 1)
                    act.wait_ge(*mlp_act.at(f"l{layer}", 0))
                    act.activation(mh[3], mh[3], ACT.Exp, scale=-1.0).then_inc(mlp_act.done(f"s{layer}"), 1)

            iterations(act, "act", {"a": attention(A), "b": scan(), "c": attention(C) | experts()},
                       before={0: setup_a, 2: setup_bc})

        @block.vector
        def _(dve):
            def stats(X, t, src, st, mv, mark_st, mark_mv):
                dve.bn_stats(st[:, :], src).then_inc(X.dve.done(mark_st), 1)
                dve.wait_ge(*X.dve.at(mark_st, t))
                dve.memset(wait_carrier[:, :], 0.0)
                dve.bn_aggr(mv[:, :], st[:, :]).then_inc(X.dve.done(mark_mv), 1)

            def attention(X):
                s, p, act, d, pool = X.name, X.pe, X.act, X.dve, X.pool

                def st(t):
                    if s == "a":
                        dve.wait_ge(*x_loaded.at(t))
                        dve.wait_ge(*d.at("xn", t - 1))
                    else:
                        dve.wait_ge(*B.dve.at("x1", t))
                        dve.wait_ge(*d.at("ac0", t - 1))
                        dve.tensor_copy(X.xin[:, :], x1[:, :]).then_inc(d.done("x1c"), 1)
                        dve.wait_ge(*d.at("x1c", t))
                    stats(X, t, X.xin[:, :], X.st, X.mv, "st", "mv")

                def xn(t):
                    dve.wait_ge(*act.at("rstd", t))
                    dve.wait_ge(*p.at("xt", t - 1))
                    dve.tensor_scalar(X.xn[:, :], X.xin[:, :], X.mv[:, 0:1], X.rstd[:, :],
                                      ALU.subtract, ALU.mult).then_inc(d.done("xn"), 1)

                def K(t):
                    if s == "a":
                        dve.wait_ge(*p.at("kv", t))
                    else:
                        dve.wait_ge(*act.at("kr", t))
                        dve.wait_ge(*d.at("kc", t))
                        dve.tensor_tensor(kn[:, :], kraw[:, :], kr[:, :], ALU.mult).then_inc(d.done("kn"), 1)
                        dve.wait_ge(*d.at("kn", t))
                    dve.wait_ge(*p.at("S1", t - 1))
                    for half in range(2):
                        part = slice(half * DH, (half + 1) * DH)
                        dst = X.K[part, :, half * S:(half + 1) * S]
                        if s == "a":
                            dve.tensor_scalar(dst, banks["a.kv"][part, 0:P].rearrange("p (b j) -> p b j", b=BT),
                                              nk_col[part, :], None, ALU.subtract).then_inc(d.done(f"K{half}"), 1)
                        else:
                            dve.tensor_scalar(dst, kn[part, :].rearrange("p (b j) -> p b j", b=BT),
                                              kq[part, :], nk_n[part, :], ALU.mult, ALU.subtract)\
                               .then_inc(d.done(f"K{half}"), 1)

                def V(t):
                    dve.wait_ge(*p.at("kv", t))
                    dve.wait_ge(*p.at("O1", t - 1))
                    for half in range(2):
                        part = slice(half * S, (half + 1) * S)
                        dve.tensor_tensor(X.V[part, :, half * DH:(half + 1) * DH],
                                          banks[f"{s}.kv"][part, P:2 * P].rearrange("p (b n) -> p b n", b=BT),
                                          nv_row[part, :].unsqueeze(1).broadcast_to([S, BT, DH]),
                                          ALU.subtract).then_inc(d.done(f"V{half}"), 1)

                def kc(t):
                    dve.wait_ge(*act.at("ksq", t))
                    dve.wait_ge(*d.at("kn", t - 1))
                    dve.tensor_copy(kraw[:, :], banks["c.kv"][:, 0:P]).then_inc(d.done("kc"), 1)

                def ks(t):
                    dve.wait_ge(*p.at("ks", t))
                    dve.wait_ge(*d.at("K1", t - 1))
                    dve.tensor_scalar(kss[:, :], banks["c.ks"][:, 0:P], 1.0e-24, None, ALU.max)\
                       .then_inc(d.done("ks"), 1)

                def qs(t):
                    dve.wait_ge(*p.at("qs", t))
                    dve.wait_ge(*d.at("S0", t - 1))
                    dve.tensor_scalar(qss[:, :], banks["c.qs"][:, 0:H], 1.0e-24, None, ALU.max)\
                       .then_inc(d.done("qs"), 1)

                def scores(half):
                    def run(t):
                        heads = slice(8 * half, 8 * half + 8)
                        dve.wait_ge(*p.at(f"S{half}", t))
                        dve.wait_ge(*p.at("W", t - 1))
                        src = banks[f"{s}.S{half}"][:, :].rearrange("p (h j) -> p h j", h=8)
                        if s == "a":
                            dve.tensor_tensor(X.prob[:, heads, :], src, X.bias[:, heads, :], ALU.add)\
                               .then_inc(d.done(f"S{half}"), 1)
                        else:
                            dve.wait_ge(*act.at("qr", t))
                            dve.tensor_tensor(X.prob[:, heads, :], src,
                                              qr[:, heads].unsqueeze(2).broadcast_to([P, 8, S]), ALU.mult)\
                               .then_inc(d.done(f"S{half}"), 1)
                    return run

                def mx(t):
                    dve.wait_ge(*pool.at("addm", t))
                    dve.tensor_reduce(X.mx[:, :], X.prob[:, :, :], AX_X, ALU.max).then_inc(d.done("mx"), 1)
                    dve.wait_ge(*d.at("mx", t))
                    dve.tensor_scalar(X.mx0[:, :], X.mx[:, :], 0.0, None, ALU.max).then_inc(d.done("mx0"), 1)

                def mk(t):
                    dve.wait_ge(*X.mask_loaded.at(t))
                    dve.wait_ge(*pool.at("addm", t - 1))
                    dve.tensor_scalar(X.mask[:, :], X.mask_u8[:, :], -NEG, NEG, ALU.mult, ALU.add)\
                       .then_inc(d.done("mk"), 1)

                def sub(t):
                    dve.wait_ge(*d.at("mx0", t))
                    dve.tensor_tensor(X.prob[:, :, :], X.prob[:, :, :],
                                      X.mx0[:, :].unsqueeze(2).broadcast_to([P, H, S]), ALU.subtract)\
                       .then_inc(d.done("sub"), 1)

                def den(t):
                    dve.wait_ge(*act.at("prob", t))
                    dve.tensor_reduce(X.sum[:, :], X.prob[:, :, :], AX_X, ALU.add).then_inc(d.done("sum"), 1)
                    dve.wait_ge(*d.at("sum", t))
                    dve.tensor_tensor(X.den[:, :], X.sum[:, :], X.expm[:, :], ALU.add).then_inc(d.done("den"), 1)
                    dve.wait_ge(*d.at("den", t))
                    dve.wait_ge(*pool.at("norm", t - 1))
                    dve.reciprocal(X.rden[:, :], X.den[:, :]).then_inc(d.done("rden"), 1)

                def st2(t):
                    dve.wait_ge(*p.at("W", t))
                    dve.wait_ge(*d.at("cn", t - 1))
                    stats(X, t, banks[f"{s}.W"][:, 0:D], X.st2, X.mv2, "st2", "mv2")

                def c(t):
                    dve.wait_ge(*act.at("rstd2", t))
                    if s == "a":
                        dve.wait_ge(*B.act.at("ss", t - 1))
                        dve.wait_ge(*B.pool.at("resid", t - 1))
                        dve.wait_ge(*B.dve.at("xn", t - 1))
                    else:
                        dve.wait_ge(*p.at("ct", t - 1))
                        dve.wait_ge(*d.at("out", t - 1))
                    dve.tensor_scalar(X.cn[:, :], banks[f"{s}.W"][:, 0:D], X.mv2[:, 0:1], X.rstd2[:, :],
                                      ALU.subtract, ALU.mult).then_inc(d.done("cn"), 1)
                    if s == "a":
                        dve.wait_ge(*d.at("cn", t))
                        dve.tensor_tensor(X.c[:, :], X.cn[:, :], X.g_out[:, :], ALU.mult).then_inc(d.done("c"), 1)

                return {"st": st, "xn": xn, "K": K, "V": V, "kc": kc, "ks": ks, "qs": qs, "S0": scores(0),
                        "S1": scores(1), "mk": mk, "mx": mx, "sub": sub, "den": den, "st2": st2, "c": c}

            def scan():
                p, act, d, pool = B.pe, B.act, B.dve, B.pool

                def xn(t):
                    dve.wait_ge(*act.at("r", t))
                    dve.wait_ge(*p.at("xt", t - 1))
                    dve.tensor_scalar(yn[:, :], A.c[:, :], r_ms[:, :], None, ALU.mult).then_inc(d.done("xn"), 1)

                def xg(t):
                    dve.wait_ge(*act.at("xe", t))
                    dve.tensor_scalar(xe[:, :], xe[:, :], GUARD, 1.0, ALU.min, ALU.add).then_inc(d.done("xg"), 1)

                def zg(t):
                    dve.wait_ge(*act.at("ze", t))
                    dve.tensor_scalar(ze[:, :], ze[:, :], GUARD, 1.0, ALU.min, ALU.add).then_inc(d.done("zg"), 1)

                def xi_(t):
                    dve.wait_ge(*act.at("xs", t))
                    dve.tensor_tensor(xi[:, :], banks["b.x"][:, :], xs[:, :], ALU.mult).then_inc(d.done("xi"), 1)

                def zi_(t):
                    dve.wait_ge(*act.at("zs", t))
                    dve.tensor_tensor(zi[:, :], banks["b.z"][:, :], zs[:, :], ALU.mult).then_inc(d.done("zi"), 1)

                def ag(t):
                    dve.wait_ge(*act.at("ae", t))
                    dve.tensor_scalar(ae[:, :], ae[:, :], float(np.exp(DECAY_FLOOR)), 1.0, ALU.min, ALU.add)\
                       .then_inc(d.done("ag"), 1)

                def low(step, unit, part):
                    def run(t):
                        dve.wait_ge(*act.at({"yl": "xnT", "xl": "xiT"}[step], t))
                        dve.wait_ge(*p.at({"yl": "z", "xl": "bc"}[step], t - 1))
                        n = part[0].shape[1] * P
                        dve.tensor_tensor(part[1][:, :, :], banks[unit][:, 0:n].rearrange("p (k n) -> p k n", n=P),
                                          part[0][:, :, :].bitcast(F32), ALU.subtract).then_inc(d.done(step), 1)
                    return run

                def nh(t):
                    dve.wait_ge(*act.at("nl", t))
                    dve.wait_ge(*p.at("E3", t - 1))
                    dve.tensor_copy(nl_parts[0][:, :], nl[:, :]).then_inc(d.done("nh"), 1)
                    dve.wait_ge(*d.at("nh", t))
                    dve.tensor_tensor(nl_parts[1][:, :], nl[:, :], nl_parts[0][:, :].bitcast(F32), ALU.subtract)\
                       .then_inc(d.done("nl"), 1)

                def BC(t):
                    dve.wait_ge(*p.at("bc", t))
                    dve.wait_ge(*p.at("gt", t - 1))
                    for n, (dst, table, mark) in enumerate(((Bt, lam_b, "Bt"), (Ct, lam_c, "Ct"))):
                        src = banks["b.bc"][:, n * NST:(n + 1) * NST].unsqueeze(1).broadcast_to([P, NLV, NST])
                        dve.tensor_tensor(dst[:, :, 0:NST], src, table[:, :, :], ALU.mult)\
                           .then_inc(d.done(mark), 1)

                def CD_(t):
                    dve.wait_ge(*act.at("BT", t))
                    dve.wait_ge(*p.at("G", t - 1))
                    dve.tensor_tensor(CD[:, :, :],
                                      banks["b.gt"][:, P:2 * P].unsqueeze(1).broadcast_to([P, NLV, P]),
                                      const("level_rows").unsqueeze(2).broadcast_to([P, NLV, P]), ALU.mult)\
                       .then_inc(d.done("CD"), 1)

                def Gm_(t):
                    dve.wait_ge(*p.at("G", t))
                    dve.wait_ge(*p.at("m3", t - 1))
                    dve.tensor_tensor(Gm[:, :, :], banks["b.G"][:, :].rearrange("p (l n) -> p l n", l=NLV),
                                      const("scan_mask").rearrange("p (l n) -> p l n", l=NLV), ALU.mult)\
                       .then_inc(d.done("Gm"), 1)

                def mix(l):
                    def run(t):
                        dve.wait_ge(*p.at(f"m{l}", t))
                        dve.wait_ge(*act.at(f"E{l}", t))
                        dve.tensor_tensor(tm[l][:, :], banks[f"b.m{l}"][:, :], Ef[l][:, :], ALU.mult)\
                           .then_inc(d.done(f"t{l}"), 1)
                    return run

                def x1_(t):
                    dve.wait_ge(*p.at("out", t))
                    dve.wait_ge(*pool.at("resid", t))
                    dve.wait_ge(*C.dve.at("x1c", t - 1))
                    dve.tensor_tensor(x1[:, :], banks["b.out"][:, 0:D], resid[:, :], ALU.add)\
                       .then_inc(d.done("x1"), 1)

                return {"xn": xn, "xg": xg, "zg": zg, "xi": xi_, "zi": zi_, "ag": ag, "BC": BC,
                        "nh": nh, "yl": low("yl", "b.xt", ynT), "xl": low("xl", "b.xiT", xiT), "CD": CD_,
                        "Gm": Gm_, "x1": x1_} | {f"t{l}": mix(l) for l in range(NLV)}

            def experts():
                p, act, d = C.pe, C.act, C.dve

                def cl(t):
                    dve.wait_ge(*act.at("cT", t))
                    dve.wait_ge(*p.at("ex3", t - 1))
                    dve.tensor_tensor(cT[1][:, :, :], banks["c.ct"][:, 0:D].rearrange("p (k n) -> p k n", n=P),
                                      cT[0][:, :, :].bitcast(F32), ALU.subtract).then_inc(d.done("cl"), 1)

                def lg(t):
                    dve.wait_ge(*p.at("lg", t))
                    dve.wait_ge(*d.at("oh", t - 1))
                    dve.tensor_tensor(lb[:, :], banks["c.lg"][:, 0:NE], gate_b[:, :], ALU.add)\
                       .then_inc(d.done("lb"), 1)
                    dve.wait_ge(*d.at("lb", t))
                    dve.tensor_reduce(lm[:, :], lb[:, :], AX_X, ALU.max).then_inc(d.done("lm"), 1)
                    dve.wait_ge(*d.at("lm", t))
                    dve.tensor_scalar(ld[:, :], lb[:, :], lm[:, :], None, ALU.subtract).then_inc(d.done("ld"), 1)

                def oh_(t):
                    dve.wait_ge(*act.at("le", t))
                    dve.wait_ge(*d.at("ac7", t - 1))
                    dve.scalar_tensor_tensor(eq[:, :], le[:, :], 1.0, const("rank"), ALU.is_ge, ALU.mult)\
                       .then_inc(d.done("eq"), 1)
                    dve.wait_ge(*d.at("eq", t))
                    dve.tensor_reduce(em[:, :], eq[:, :], AX_X, ALU.max).then_inc(d.done("em"), 1)
                    dve.wait_ge(*d.at("em", t))
                    dve.wait_ge(*p.at("oT", t - 1))
                    dve.tensor_scalar(oh[:, :], eq[:, :], em[:, :], None, ALU.is_equal).then_inc(d.done("oh"), 1)

                def ac(e):
                    def run(t):
                        dve.wait_ge(*p.at(f"ex{e // 2}", t))
                        if e == 0:
                            dve.wait_ge(*d.at("oh", t))
                            dve.wait_ge(*out_stored.at(t - 1))
                        else:
                            dve.wait_ge(*d.at(f"ac{e - 1}", t))
                        src = C.xin if e == 0 else (acc2 if e % 2 == 0 else acc)
                        dst = acc if e % 2 == 0 else acc2
                        dve.scalar_tensor_tensor(dst[:, :], banks[f"c.ex{e // 2}"][:, (e % 2) * D:(e % 2 + 1) * D],
                                                 oh[:, e:e + 1], src[:, :], ALU.mult, ALU.add)\
                           .then_inc(d.done(f"ac{e}"), 1)
                    return run

                def out_(t):
                    dve.wait_ge(*p.at("eb", t))
                    dve.wait_ge(*d.at(f"ac{NE - 1}", t))
                    dve.tensor_tensor(yout[:, :], banks["c.eb"][:, 0:D], acc2[:, :], ALU.add)\
                       .then_inc(d.done("out"), 1)

                return {"cl": cl, "lg": lg, "oh": oh_, "out": out_} | {f"ac{e}": ac(e) for e in range(NE)}

            def setup_weights(X, prep, scale):
                for k in range(KD):
                    dve.tensor_scalar(X.wq[:, k, :], X.wq[:, k, :], X.g[:, k:k + 1], scale, ALU.mult, ALU.mult)
                    for half in range(2):
                        dve.tensor_scalar(X.wkk[:, k, half, :], X.wkv[:, k, 0:DH], X.g[:, k:k + 1], None, ALU.mult)
                    dve.tensor_scalar(X.wv[:, k, :], X.wkv[:, k, DH:], X.g[:, k:k + 1], None, ALU.mult)

            def split(chunks, done):
                for hi, lo, chunk, gain in chunks:
                    mm = dve.tensor_scalar(hi, chunk, gain, None, ALU.mult) if gain is not None\
                        else dve.tensor_copy(hi, chunk)
                mm.then_inc(done, 1)
                dve.wait_ge(done, 1)
                for hi, lo, chunk, gain in chunks:
                    if gain is None:
                        mm = dve.tensor_tensor(lo, chunk, hi.bitcast(F32), ALU.subtract)
                    else:
                        mm = dve.scalar_tensor_tensor(lo, chunk, gain, hi.bitcast(F32), ALU.mult, ALU.subtract)
                mm.then_inc(done, 1)
                dve.wait_ge(done, 2)

            def setup_a():
                dve.memset(eps5[:, :], 1.0e-5)
                dve.memset(eps6[:, :], 1.0e-6)
                dve.memset(A.K[:, :, :], 0.0)
                dve.memset(A.V[:, :, :], 0.0)
                dve.memset(C.K[:, :, :], 0.0)
                dve.memset(C.V[:, :, :], 0.0)
                dve.memset(Bt[:, :, :], 0.0)
                dve.memset(Ct[:, :, :], 0.0)
                dve.memset(ones_f, 1.0)
                dve.memset(a_bias, 0.0).then_inc(zeroed, 1)
                dve.wait_ge(ld_const, n_ld[ld_const.name])
                dve.wait_ge(ld_a, n_ld[ld_a.name])
                setup_weights(A, prep_a, float(DH) ** -0.5)
                dve.tensor_copy(sums[:, :], sums_staged[:, :]).then_inc(prep_a, 1)
                dve.wait_ge(prep_a, 1)
                dve.wait_ge(A.bias_folded, 2)

            def setup_b():
                dve.wait_ge(ld_b, n_ld[ld_b.name])
                split([(w_in[0][:, k, n * E2:(n + 1) * E2], w_in[1][:, k, n * E2:(n + 1) * E2],
                        w_in_staged[k][n], norm_w[:, k:k + 1]) for k in range(KD) for n in range(2)]
                      + [(w_a[0][:, k, :], w_a[1][:, k, :], w_a_staged[k], None) for k in range(KE)]
                      + [(w_bc[0][:, :, :], w_bc[1][:, :, :], w_bc_staged, None)], split_b)
                dve.wait_ge(prep_lam, 1)
                dve.tensor_scalar(lam_g[:, :], lam_e[:, :], float(np.exp(LAMBDA_FLOOR)), 1.0, ALU.min, ALU.add)\
                   .then_inc(prep_lam_g, 1)
                dve.tensor_copy(bias_ones[:, :], ones_f)
                dve.tensor_copy(a_bias_parts[:, :], a_bias).then_inc(prep_lam_g, 1)
                dve.wait_ge(prep_lam_g, 2)
                dve.tensor_tensor(a_bias_parts[32:33, :], a_bias[32:33, :], a_bias_parts[32:33, :].bitcast(F32),
                                  ALU.subtract)\
                   .then_inc(prep_b, 1)
                dve.wait_ge(prep_lam, 2 + 2 * NLV)

            def setup_c():
                dve.wait_ge(ld_c, n_ld[ld_c.name])
                dve.tensor_tensor(nk_sq[:, :], nk_col[:, :], nk_col[:, :], ALU.mult).then_inc(prep_nk, 1)
                setup_weights(C, prep_c, 1.0)
                dve.wait_ge(prep_nk_pe, 1)
                dve.tensor_scalar(nk_ss[:, :], mlp_bank[0][:, 0:1], 1.0e-24, None, ALU.max).then_inc(prep_nk, 1)
                dve.tensor_scalar(kq[:, :], q_scale[:, :], k_scale[:, :], 8.0 * L2_SCALE, ALU.mult, ALU.mult)\
                   .then_inc(prep_nk, 1)
                dve.wait_ge(prep_nk, 3)
                dve.wait_ge(prep_nk_act, 2)
                dve.tensor_scalar(nk_n[:, :], nk_col[:, :], nk_r[:, :], kq[:, :], ALU.mult, ALU.mult)\
                   .then_inc(prep_c, 1)
                dve.wait_ge(prep_c, 1)

            def setup_experts():
                dve.wait_ge(ld_e, n_ld[ld_e.name])
                split([(w_e[0][:, k, 2 * n:2 * n + 2, :], w_e[1][:, k, 2 * n:2 * n + 2, :], w_e_staged[k][n],
                        g_out_col[:, k:k + 1]) for k in range(KD) for n in range(NE // 2)]
                      + [(gate_w[0][:, k, :], gate_w[1][:, k, :], gate_w_staged[:, k, :], g_out_col[:, k:k + 1])
                         for k in range(KD)], split_c)

            def setup_mlp():
                d, bank = mlp_dve, mlp_bank
                dve.wait_ge(ld_mlp, n_ld[ld_mlp.name])
                dve.scalar_tensor_tensor(mh[0], m_w0, const("distance"), m_b0, ALU.mult, ALU.add)\
                   .then_inc(d.done("h0"), 1)
                for layer, (nrm, res, gain) in enumerate(((mh[1], mh[2], m_g0), (mh[4], mh[5], m_g1))):
                    dve.wait_ge(*d.at(f"h{layer}", 0))
                    dve.bn_stats(C.st[:, :], mh[0]).then_inc(d.done(f"st{layer}"), 1)
                    dve.wait_ge(*d.at(f"st{layer}", 0))
                    dve.bn_aggr(C.mv[:, :], C.st[:, :]).then_inc(d.done(f"mv{layer}"), 1)
                    dve.wait_ge(*mlp_act.at(f"r{layer}", 0))
                    dve.tensor_scalar(nrm, mh[0], C.mv[:, 0:1], C.rstd[:, :], ALU.subtract, ALU.mult)\
                       .then_inc(d.done(f"n{layer}"), 1)
                    dve.wait_ge(*d.at(f"n{layer}", 0))
                    dve.tensor_tensor(nrm, nrm, gain, ALU.mult).then_inc(d.done(f"v{layer}"), 1)
                    dve.wait_ge(*mlp_act.at(f"e{layer}", 0))
                    dve.tensor_scalar(mh[3], mh[3], GUARD, 1.0, ALU.min, ALU.add).then_inc(d.done(f"e{layer}"), 1)
                    dve.wait_ge(*mlp_act.at(f"s{layer}", 0))
                    dve.tensor_tensor(res, nrm, mh[3], ALU.mult).then_inc(d.done(f"s{layer}"), 1)
                    dve.wait_ge(*mlp_pe.at(f"T{layer}", 0))
                    dve.tensor_copy(mhT, bank[1][:, 0:D].rearrange("p (k n) -> p k n", k=KD))\
                       .then_inc(d.done(f"T{layer}"), 1)
                    if layer == 0:
                        dve.wait_ge(*mlp_pe.at("h1", 0))
                        dve.tensor_tensor(mh[0], bank[2][:, 0:D], m_b1, ALU.add).then_inc(d.done("h1"), 1)
                dve.wait_ge(*mlp_pe.at("pos", 0))
                dve.tensor_tensor(m_pos, bank[2][:, 0:H], m_b2, ALU.add).then_inc(d.done("pos"), 1)
                dve.wait_ge(*mlp_pe.at("posT", 0))
                dve.tensor_copy(m_posT, bank[1][0:H, 0:P]).then_inc(d.done("posT"), 1)

            def setup_bc():
                setup_b()
                setup_c()
                setup_mlp()
                setup_experts()

            iterations(dve, "dve", {"a": attention(A), "b": scan(), "c": attention(C) | experts()},
                       before={0: setup_a, 2: setup_bc})

        @block.gpsimd
        def _(pool):
            def attention(X):
                s, p, act, dve, g = X.name, X.pe, X.act, X.dve, X.pool

                def qsq_(t):
                    pool.wait_ge(*act.at("q1", t))
                    pool.wait_ge(*p.at("W", t - 1))
                    pool.tensor_tensor(qsq[:, :, :], X.qT[:, :, :], X.qT[:, :, :], ALU.mult)\
                        .then_inc(g.done("qsq"), 1)

                def addb(t):
                    pool.wait_ge(*dve.at("S1", t))
                    pool.tensor_tensor(X.prob[:, :, :], X.prob[:, :, :], X.bias[:, :, :], ALU.add)\
                        .then_inc(g.done("addb"), 1)

                def addm(t):
                    pool.wait_ge(*dve.at("mk", t))
                    if s == "a":
                        pool.wait_ge(*dve.at("S1", t))
                    else:
                        pool.wait_ge(*g.at("addb", t))
                    pool.tensor_tensor(X.prob[:, :, :], X.prob[:, :, :],
                                       X.mask[:, :].unsqueeze(1).broadcast_to([P, H, S]), ALU.add)\
                        .then_inc(g.done("addm"), 1)

                def norm(t):
                    pool.wait_ge(*dve.at("rden", t))
                    pool.tensor_tensor(X.prob[:, :, :], X.prob[:, :, :],
                                       X.rden[:, :].unsqueeze(2).broadcast_to([P, H, S]), ALU.mult)\
                        .then_inc(g.done("norm"), 1)

                return {"qsq": qsq_, "addb": addb, "addm": addm, "norm": norm}

            def scan():
                p, act, dve, g = B.pe, B.act, B.dve, B.pool

                def resid_(t):
                    pool.wait_ge(*A.dve.at("c", t))
                    pool.wait_ge(*xres_loaded.at(t))
                    pool.wait_ge(*dve.at("x1", t - 1))
                    pool.tensor_tensor(resid[:, :], xres[:, :], A.c[:, :], ALU.add).then_inc(g.done("resid"), 1)

                def dx(t):
                    pool.wait_ge(*dve.at("xi", t))
                    pool.wait_ge(*p.at("yT", t - 1))
                    pool.tensor_tensor(y[:, :], xi[:, :], d_row[:, :], ALU.mult).then_inc(g.done("dx"), 1)

                def u_(l):
                    def run(t):
                        pool.wait_ge(*act.at("E0u" if l == 0 else f"E{l}", t))
                        if l:
                            pool.wait_ge(*g.at(f"y{l}", t - 1))
                        pool.tensor_tensor(u[l][:, :], xi[:, :], (E0u if l == 0 else Ef[l])[:, :], ALU.mult)\
                            .then_inc(g.done(f"u{l}"), 1)
                    return run

                def mix(l):
                    def run(t):
                        pool.wait_ge(*g.at("dx" if l == 0 else f"y{l - 1}", t))
                        pool.wait_ge(*dve.at(f"t{l}", t))
                        pool.tensor_tensor(y[:, :], y[:, :], tm[l][:, :], ALU.add).then_inc(g.done(f"y{l}"), 1)
                    return run

                def gate(t):
                    pool.wait_ge(*g.at(f"y{NLV - 1}", t))
                    pool.wait_ge(*dve.at("zi", t))
                    pool.tensor_tensor(y[:, :], y[:, :], zi[:, :], ALU.mult).then_inc(g.done("y"), 1)

                return {"resid": resid_, "dx": dx, "y": gate} | {f"u{l}": u_(l) for l in range(NLV)}\
                    | {f"y{l}": mix(l) for l in range(NLV)}

            def fold_bias(X):
                done = X.bias_folded
                pool.tensor_tensor(X.bias[:, :, :], X.bias[:, :, :],
                                   X.null_bias[:, :].unsqueeze(2).broadcast_to([P, H, S]), ALU.subtract)\
                    .then_inc(done, 1)
                pool.wait_ge(done, 1)
                pool.tensor_tensor(X.bias[:, :, :], X.bias[:, :, :],
                                   const("causal").unsqueeze(1).broadcast_to([P, H, S]), ALU.add)\
                    .then_inc(done, 1)
                pool.wait_ge(done, 2)

            def setup_a():
                pool.wait_ge(ld_const, n_ld[ld_const.name])
                pool.wait_ge(ld_a, n_ld[ld_a.name])
                fold_bias(A)
                pool.wait_ge(prep_a, 1)

            def setup_c():
                pool.wait_ge(ld_c, n_ld[ld_c.name])
                pool.wait_ge(mlp_dma, 16 + 16 * BT)
                fold_bias(C)
                pool.wait_ge(prep_c, 1)

            iterations(pool, "pool", {"a": attention(A), "b": scan(), "c": attention(C)},
                       before={0: setup_a, 2: lambda: pool.wait_ge(ld_b, n_ld[ld_b.name]), 3: setup_c})


_INS = ["cond_64", "fside_16xSxS_0", "mask_BxS_bk0", "mask_BxS_bf1",
        "L0_cond_g_in", "L0_cond_null_attn_bias", "L0_cond_Wq", "L0_cond_Wkv", "L0_cond_Wo", "L0_cond_g_out",
        "L0_attn_norm_w", "L0_attn_in_proj_w", "L0_attn_A_proj_w", "L0_attn_A_proj_b", "L0_attn_A_base",
        "L0_attn_B_proj_w", "L0_attn_C_proj_w", "L0_attn_D", "L0_attn_out_proj_w",
        "L0_cond2_g_norm", "L0_cond2_Wq", "L0_cond2_Wkv", "L0_cond2_q_scale", "L0_cond2_k_scale",
        "L0_cond2_null_attn_bias", "L0_cond2_w0", "L0_cond2_b0", "L0_cond2_g0", "L0_cond2_w1", "L0_cond2_b1",
        "L0_cond2_g1", "L0_cond2_w2", "L0_cond2_b2", "L0_cond2_Wout", "L0_cond2_g_out",
        "L0_ffn_gate_w", "L0_ffn_gate_b", "L0_ffn_expert_w", "L0_ffn_expert_b"]


def kernel(**inputs):
    import numpy as _np
    import concourse.bacc as _bacc
    from concourse import mybir as _mybir
    from concourse.bass_utils import run_bass_kernel_spmd as _run

    nc = _bacc.Bacc("TRN2", target_bir_lowering=False, num_devices=1)
    arrays, aps = {}, {}
    for name in ["x"] + _INS:
        a = _np.ascontiguousarray(inputs[name])
        arrays[f"in_{name}"] = a
        aps[name] = nc.dram_tensor(f"in_{name}", a.shape, _mybir.dt.from_np(a.dtype), kind="ExternalInput").ap()
    at, table = constants()
    arrays["in_constants"] = table
    table_ap = nc.dram_tensor("in_constants", table.shape, _mybir.dt.float32, kind="ExternalInput").ap()
    shape = inputs["x"].shape
    out = nc.dram_tensor("out_0", shape, _mybir.dt.float32, kind="ExternalOutput").ap()
    build(nc, aps["x"], out, aps, table_ap, at)
    r = _run(nc, [arrays], core_ids=[0])
    return r.results[0]["out_0"]
```
